# Optimizing a Trainium2 kernel written in Bass

```python
import numpy as np
import jax
import jax.numpy as jnp

def _softmax(x, axis=-1):
    return jax.nn.softmax(x, axis=axis)

def _gelu(x):
    return jax.nn.gelu(x, approximate=True)

def _silu(x):
    return jax.nn.silu(x)

def _sigmoid(x):
    return jax.nn.sigmoid(x)

def _layernorm(x, axis=-1, eps=1e-05):
    m = jnp.mean(x, axis=axis, keepdims=True)
    v = jnp.var(x, axis=axis, keepdims=True)
    return (x - m) / jnp.sqrt(v + eps)

def _scatter_add(tgt, idx, src, axis=0):
    return tgt.at[idx].add(src)

def _segment_sum(src, seg, n):
    return jax.ops.segment_sum(src, seg, n)
kernel_name = 'mk_perceiver_d2_seqx_r8_4f14db'

def setup_inputs(seed: int=0):
    np.random.seed(seed)
    _w = jnp.asarray

    def _rec_inputs():
        import jax
        import jax.numpy as jnp
        _rk = jax.random.key(seed)
        x = -0.0005207 + 1.001 * jax.random.normal(jax.random.fold_in(_rk, 1), (1, 128, 512), jnp.float32)
        _lenS = 128 - jax.random.randint(jax.random.fold_in(_rk, 7), (1,), 0, max(1, 128 // 4) + 1, jnp.int32)
        _lenS2 = 2048 - jax.random.randint(jax.random.fold_in(_rk, 8), (1,), 0, max(1, 2048 // 4) + 1, jnp.int32)
        _ctx_4096P = jax.random.normal(jax.random.fold_in(_rk, 11), (1, 16, 512), jnp.float32)
        _ctx_4096c = jax.random.dirichlet(jax.random.fold_in(_rk, 511), 0.3 * jnp.ones((16,), jnp.float32), (1, 2048))
        _ctx_4096t = jnp.einsum('bsk,bkd->bsd', _ctx_4096c, _ctx_4096P)
        _ctx_4096t = _ctx_4096t * jax.lax.rsqrt(jnp.mean(jnp.square(_ctx_4096t)) + 1e-12) * 0.953939
        ctx_4096 = -0.00010331 + 0.999899 * (_ctx_4096t + 0.3 * jax.random.normal(jax.random.fold_in(_rk, 611), (1, 2048, 512), jnp.float32))
        return (x, ctx_4096)
    x, ctx_4096 = _rec_inputs()

    def _L0_xattn_setup():
        import jax, jax.numpy as jnp
        import numpy as np
        import math
        HIDDEN = 512
        N_HEADS = 32
        HEAD_DIM = 128
        N_KV_HEADS = 4
        N_GROUPS = N_HEADS // N_KV_HEADS
        key = jax.random.key(seed)
        ks = jax.random.split(key, 6)
        B, NL, S = (8, 64, 512)
        latents = jax.random.normal(ks[0], (B, NL, HIDDEN), dtype=jnp.float32)
        context = jax.random.normal(ks[1], (B, S, HIDDEN), dtype=jnp.float32)
        scale = 1.0 / math.sqrt(HIDDEN)
        Wq = jax.random.normal(ks[2], (HIDDEN, N_HEADS * HEAD_DIM), dtype=jnp.float32) * scale
        Wk = jax.random.normal(ks[3], (HIDDEN, N_KV_HEADS * HEAD_DIM), dtype=jnp.float32) * scale
        Wv = jax.random.normal(ks[4], (HIDDEN, N_KV_HEADS * HEAD_DIM), dtype=jnp.float32) * scale
        Wo = jax.random.normal(ks[5], (N_HEADS * HEAD_DIM, HIDDEN), dtype=jnp.float32) * scale
        return {'latents': latents, 'context': context, 'Wq': Wq, 'Wk': Wk, 'Wv': Wv, 'Wo': Wo}
    _L0_xattn_all = _L0_xattn_setup()
    _L0_xattn_in = {k: v for k, v in _L0_xattn_all.items() if k in ('Wq', 'Wk', 'Wv', 'Wo')}
    del _L0_xattn_all

    def _L0_attn_setup():
        import math
        import jax, jax.numpy as jnp
        import numpy as np
        H = 32
        NOPE = 64
        ROPE = 64
        VD = 128
        QHD = NOPE + ROPE
        KVR = 32
        EPS = 1e-06

        def _yarn_cos_sin(seq_len, dim=ROPE, base=10000.0, factor=128.0, beta_fast=32.0, beta_slow=1.0, orig_max=1024, mscale=1.0, mscale_all_dim=1.0):

            def corr_dim(r):
                return dim * math.log(orig_max / (r * 2 * math.pi)) / (2 * math.log(base))
            low = max(math.floor(corr_dim(beta_fast)), 0)
            high = min(math.ceil(corr_dim(beta_slow)), dim - 1)
            hi = high + 0.001 if low == high else float(high)
            ramp = np.clip((np.arange(dim // 2, dtype=np.float32) - low) / (hi - low), 0.0, 1.0)
            inv_freq_mask = 1.0 - ramp
            freq_extra = 1.0 / base ** (np.arange(0, dim, 2, dtype=np.float32) / dim)
            freq_inter = freq_extra / factor
            inv_freq = freq_inter * (1.0 - inv_freq_mask) + freq_extra * inv_freq_mask
            t = np.arange(seq_len, dtype=np.float32)
            freqs = np.outer(t, inv_freq)
            emb = np.concatenate([freqs, freqs], axis=-1)

            def gm(s, m):
                return 1.0 if s <= 1 else 0.1 * m * math.log(s) + 1.0
            ms = gm(factor, mscale) / gm(factor, mscale_all_dim)
            return (jnp.asarray(np.cos(emb) * ms), jnp.asarray(np.sin(emb) * ms))

        def _rmsnorm(x, w, eps=EPS):
            var = jnp.mean(jnp.square(x), axis=-1, keepdims=True)
            return x * jax.lax.rsqrt(var + eps) * w

        def _deinterleave(x):
            d = x.shape[-1]
            x = x.reshape(*x.shape[:-1], d // 2, 2)
            return jnp.concatenate([x[..., 0], x[..., 1]], axis=-1)

        def _rotate_half(x):
            d = x.shape[-1] // 2
            return jnp.concatenate([-x[..., d:], x[..., :d]], axis=-1)

        def _apply_rope(x, cos, sin):
            return x * cos + _rotate_half(x) * sin
        key = jax.random.key(seed)
        ks = jax.random.split(key, 6)
        B, S, D = (1, 256, 512)
        std = 0.02
        return {'x': jax.random.normal(ks[0], (B, S, D), dtype=jnp.float32), 'wq_a': jax.random.normal(ks[1], (128, D), dtype=jnp.float32) * std, 'q_a_ln_w': jnp.ones((128,), dtype=jnp.float32), 'wq_b': jax.random.normal(ks[2], (H * QHD, 128), dtype=jnp.float32) * std, 'wkv_a': jax.random.normal(ks[3], (KVR + ROPE, D), dtype=jnp.float32) * std, 'kv_a_ln_w': jnp.ones((KVR,), dtype=jnp.float32), 'wkv_b': jax.random.normal(ks[4], (H * (NOPE + VD), KVR), dtype=jnp.float32) * std, 'wo': jax.random.normal(ks[5], (D, H * VD), dtype=jnp.float32) * std}
    _L0_attn_all = _L0_attn_setup()
    _L0_attn_in = {k: v for k, v in _L0_attn_all.items() if k in ('wq_a', 'q_a_ln_w', 'wq_b', 'wkv_a', 'kv_a_ln_w', 'wkv_b', 'wo')}
    del _L0_attn_all

    def _L0_ffn_setup():
        import jax, jax.numpy as jnp
        import numpy as np
        B, S, D = (4, 256, 512)
        NUM_EXPERTS, TOP_K = (3, 2)

        def _expert_outputs(h, w1, b1, w2, b2):
            pre = jnp.einsum('bsd,edf->ebsf', h, w1) + b1[:, None, None, :]
            act = jnp.stack([jnp.tanh(pre[0]), jax.nn.gelu(pre[1], approximate=False), jax.nn.silu(pre[2])])
            return jnp.einsum('ebsf,efd->ebsd', act, w2) + b2[:, None, None, :]
        key = jax.random.key(seed)
        ks = jax.random.split(key, 8)
        scale_in = 1.0 / np.sqrt(D)
        scale_gate = 1.0 / np.sqrt(D + 1)
        return {'h': jax.random.normal(ks[0], (B, S, D), dtype=jnp.float32), 'gate_w': jax.random.uniform(ks[1], (D + 1, NUM_EXPERTS), minval=-scale_gate, maxval=scale_gate, dtype=jnp.float32), 'gate_b': jnp.zeros((NUM_EXPERTS,), dtype=jnp.float32), 'w1': jax.random.uniform(ks[2], (NUM_EXPERTS, D, D), minval=-scale_in, maxval=scale_in, dtype=jnp.float32), 'b1': jnp.zeros((NUM_EXPERTS, D), dtype=jnp.float32), 'w2': jax.random.uniform(ks[3], (NUM_EXPERTS, D, D), minval=-scale_in, maxval=scale_in, dtype=jnp.float32), 'b2': jnp.zeros((NUM_EXPERTS, D), dtype=jnp.float32)}
    _L0_ffn_all = _L0_ffn_setup()
    _L0_ffn_in = {k: v for k, v in _L0_ffn_all.items() if k in ('gate_w', 'gate_b', 'w1', 'b1', 'w2', 'b2')}
    del _L0_ffn_all

    def _L1_xattn_setup():
        import jax, jax.numpy as jnp
        import numpy as np
        HID = 512
        NHEAD = 32
        NKV = 8
        HDIM = 128
        G = NHEAD // NKV
        key = jax.random.key(seed)
        ks = jax.random.split(key, 6)
        s = 0.02
        B, L = (2, 256)
        return {'query': jax.random.normal(ks[0], (B, L, HID), jnp.float32), 'kv': jax.random.normal(ks[1], (B, L, HID), jnp.float32), 'Wq': jax.random.normal(ks[2], (HID, NHEAD * HDIM), jnp.float32) * s, 'bq': jnp.zeros((NHEAD * HDIM,), jnp.float32), 'Wkv': jax.random.normal(ks[3], (HID, 2 * NKV * HDIM), jnp.float32) * s, 'bkv': jnp.zeros((2 * NKV * HDIM,), jnp.float32), 'Wo': jax.random.normal(ks[4], (NHEAD * HDIM, HID), jnp.float32) * s, 'bo': jnp.zeros((HID,), jnp.float32)}
    _L1_xattn_all = _L1_xattn_setup()
    _L1_xattn_in = {k: v for k, v in _L1_xattn_all.items() if k in ('Wq', 'bq', 'Wkv', 'bkv', 'Wo', 'bo')}
    del _L1_xattn_all

    def _L1_attn_setup():
        import jax, jax.numpy as jnp
        import numpy as np
        B, S, HID = (2, 256, 512)
        H, P, N, G, K = (128, 64, 128, 8, 4)
        INTER = H * P
        CONV_DIM = INTER + 2 * G * N
        CHUNK = 128
        EPS = 1e-05
        DT_MIN, DT_MAX = (0.0, 100.0)

        def _segsum(a):
            c = a.shape[-1]
            s = jnp.cumsum(a, axis=-1)
            diff = s[..., :, None] - s[..., None, :]
            mask = jnp.tril(jnp.ones((c, c), dtype=bool))
            return jnp.where(mask, diff, -jnp.inf)
        key = jax.random.key(seed)
        ks = jax.random.split(key, 4)
        proj = INTER + CONV_DIM + H
        return {'x': jax.random.normal(ks[0], (B, S, HID), jnp.float32), 'in_proj_w': jax.random.normal(ks[1], (proj, HID), jnp.float32) * 0.02, 'conv_w': jax.random.normal(ks[2], (CONV_DIM, 1, K), jnp.float32) * 0.2, 'conv_b': jnp.zeros((CONV_DIM,), jnp.float32), 'dt_bias': jnp.ones((H,), jnp.float32), 'A_log': jnp.log(jnp.arange(1, H + 1, dtype=jnp.float32)), 'D': jnp.ones((H,), jnp.float32), 'norm_w': jnp.ones((INTER,), jnp.float32), 'out_proj_w': jax.random.normal(ks[3], (HID, INTER), jnp.float32) * 0.02}
    _L1_attn_all = _L1_attn_setup()
    _L1_attn_in = {k: v for k, v in _L1_attn_all.items() if k in ('in_proj_w', 'conv_w', 'conv_b', 'dt_bias', 'A_log', 'D', 'norm_w', 'out_proj_w')}
    del _L1_attn_all

    def _L1_ffn_setup():
        import jax, jax.numpy as jnp
        import numpy as np

        @jax.custom_vjp
        def ste_sign(w):
            return jnp.sign(w)

        def _ste_fwd(w):
            return (jnp.sign(w), w)

        def _ste_bwd(w, g):
            mask = ((w > -1) & (w < 1)).astype(g.dtype)
            return (g * mask,)
        ste_sign.defvjp(_ste_fwd, _ste_bwd)
        key = jax.random.key(seed)
        k = jax.random.split(key, 6)
        B, S, H, O, E = (4, 256, 512, 512, 8)
        return {'x': jax.random.normal(k[0], (B, S, H), dtype=jnp.float32), 'weight': jax.random.normal(k[1], (O, H), dtype=jnp.float32) * 0.02, 'bias': jax.random.normal(k[2], (O,), dtype=jnp.float32) * 0.02, 'gate_w': jax.random.normal(k[3], (E, H), dtype=jnp.float32) * 0.02, 'in_channel_scale': jax.random.normal(k[4], (E, H), dtype=jnp.float32), 'out_channel_scale': jax.random.normal(k[5], (E, O), dtype=jnp.float32)}
    _L1_ffn_all = _L1_ffn_setup()
    _L1_ffn_in = {k: v for k, v in _L1_ffn_all.items() if k in ('weight', 'bias', 'gate_w', 'in_channel_scale', 'out_channel_scale')}
    del _L1_ffn_all
    return {'x': x, 'ctx_4096': ctx_4096, 'L0_xattn_Wq': _L0_xattn_in['Wq'], 'L0_xattn_Wk': _L0_xattn_in['Wk'], 'L0_xattn_Wv': _L0_xattn_in['Wv'], 'L0_xattn_Wo': _L0_xattn_in['Wo'], 'L0_attn_wq_a': _L0_attn_in['wq_a'], 'L0_attn_q_a_ln_w': _L0_attn_in['q_a_ln_w'], 'L0_attn_wq_b': _L0_attn_in['wq_b'], 'L0_attn_wkv_a': _L0_attn_in['wkv_a'], 'L0_attn_kv_a_ln_w': _L0_attn_in['kv_a_ln_w'], 'L0_attn_wkv_b': _L0_attn_in['wkv_b'], 'L0_attn_wo': _L0_attn_in['wo'], 'L0_ffn_gate_w': _L0_ffn_in['gate_w'], 'L0_ffn_gate_b': _L0_ffn_in['gate_b'], 'L0_ffn_w1': _L0_ffn_in['w1'], 'L0_ffn_b1': _L0_ffn_in['b1'], 'L0_ffn_w2': _L0_ffn_in['w2'], 'L0_ffn_b2': _L0_ffn_in['b2'], 'L1_xattn_Wq': _L1_xattn_in['Wq'], 'L1_xattn_bq': _L1_xattn_in['bq'], 'L1_xattn_Wkv': _L1_xattn_in['Wkv'], 'L1_xattn_bkv': _L1_xattn_in['bkv'], 'L1_xattn_Wo': _L1_xattn_in['Wo'], 'L1_xattn_bo': _L1_xattn_in['bo'], 'L1_attn_in_proj_w': _L1_attn_in['in_proj_w'], 'L1_attn_conv_w': _L1_attn_in['conv_w'], 'L1_attn_conv_b': _L1_attn_in['conv_b'], 'L1_attn_dt_bias': _L1_attn_in['dt_bias'], 'L1_attn_A_log': _L1_attn_in['A_log'], 'L1_attn_D': _L1_attn_in['D'], 'L1_attn_norm_w': _L1_attn_in['norm_w'], 'L1_attn_out_proj_w': _L1_attn_in['out_proj_w'], 'L1_ffn_weight': _L1_ffn_in['weight'], 'L1_ffn_bias': _L1_ffn_in['bias'], 'L1_ffn_gate_w': _L1_ffn_in['gate_w'], 'L1_ffn_in_channel_scale': _L1_ffn_in['in_channel_scale'], 'L1_ffn_out_channel_scale': _L1_ffn_in['out_channel_scale']}

def reference(x, ctx_4096, L0_xattn_Wq, L0_xattn_Wk, L0_xattn_Wv, L0_xattn_Wo, L0_attn_wq_a, L0_attn_q_a_ln_w, L0_attn_wq_b, L0_attn_wkv_a, L0_attn_kv_a_ln_w, L0_attn_wkv_b, L0_attn_wo, L0_ffn_gate_w, L0_ffn_gate_b, L0_ffn_w1, L0_ffn_b1, L0_ffn_w2, L0_ffn_b2, L1_xattn_Wq, L1_xattn_bq, L1_xattn_Wkv, L1_xattn_bkv, L1_xattn_Wo, L1_xattn_bo, L1_attn_in_proj_w, L1_attn_conv_w, L1_attn_conv_b, L1_attn_dt_bias, L1_attn_A_log, L1_attn_D, L1_attn_norm_w, L1_attn_out_proj_w, L1_ffn_weight, L1_ffn_bias, L1_ffn_gate_w, L1_ffn_in_channel_scale, L1_ffn_out_channel_scale):
    import jax
    import jax.numpy as jnp

    def _L0_xattn_ref(latents, context, Wq, Wk, Wv, Wo):
        import jax, jax.numpy as jnp
        import numpy as np
        import math
        HIDDEN = 512
        N_HEADS = 32
        HEAD_DIM = 128
        N_KV_HEADS = 4
        N_GROUPS = N_HEADS // N_KV_HEADS
        b, q_len, _ = latents.shape
        kv_len = q_len + context.shape[1]
        hidden_states = jnp.concatenate([context, latents], axis=1)
        q = (latents @ Wq).reshape(b, q_len, N_KV_HEADS, N_GROUPS, HEAD_DIM)
        k = (hidden_states @ Wk).reshape(b, kv_len, N_KV_HEADS, HEAD_DIM)
        v = (hidden_states @ Wv).reshape(b, kv_len, N_KV_HEADS, HEAD_DIM)
        scale = 1.0 / math.sqrt(HEAD_DIM)
        scores = jnp.einsum('bqhgd,bkhd->bhgqk', q, k) * scale
        attn = jax.nn.softmax(scores.astype(jnp.float32), axis=-1).astype(q.dtype)
        out = jnp.einsum('bhgqk,bkhd->bqhgd', attn, v)
        out = out.reshape(b, q_len, N_HEADS * HEAD_DIM)
        return out @ Wo

    def _L0_attn_ref(x, wq_a, q_a_ln_w, wq_b, wkv_a, kv_a_ln_w, wkv_b, wo):
        import math
        import jax, jax.numpy as jnp
        import numpy as np
        H = 32
        NOPE = 64
        ROPE = 64
        VD = 128
        QHD = NOPE + ROPE
        KVR = 32
        EPS = 1e-06

        def _yarn_cos_sin(seq_len, dim=ROPE, base=10000.0, factor=128.0, beta_fast=32.0, beta_slow=1.0, orig_max=1024, mscale=1.0, mscale_all_dim=1.0):

            def corr_dim(r):
                return dim * math.log(orig_max / (r * 2 * math.pi)) / (2 * math.log(base))
            low = max(math.floor(corr_dim(beta_fast)), 0)
            high = min(math.ceil(corr_dim(beta_slow)), dim - 1)
            hi = high + 0.001 if low == high else float(high)
            ramp = np.clip((np.arange(dim // 2, dtype=np.float32) - low) / (hi - low), 0.0, 1.0)
            inv_freq_mask = 1.0 - ramp
            freq_extra = 1.0 / base ** (np.arange(0, dim, 2, dtype=np.float32) / dim)
            freq_inter = freq_extra / factor
            inv_freq = freq_inter * (1.0 - inv_freq_mask) + freq_extra * inv_freq_mask
            t = np.arange(seq_len, dtype=np.float32)
            freqs = np.outer(t, inv_freq)
            emb = np.concatenate([freqs, freqs], axis=-1)

            def gm(s, m):
                return 1.0 if s <= 1 else 0.1 * m * math.log(s) + 1.0
            ms = gm(factor, mscale) / gm(factor, mscale_all_dim)
            return (jnp.asarray(np.cos(emb) * ms), jnp.asarray(np.sin(emb) * ms))

        def _rmsnorm(x, w, eps=EPS):
            var = jnp.mean(jnp.square(x), axis=-1, keepdims=True)
            return x * jax.lax.rsqrt(var + eps) * w

        def _deinterleave(x):
            d = x.shape[-1]
            x = x.reshape(*x.shape[:-1], d // 2, 2)
            return jnp.concatenate([x[..., 0], x[..., 1]], axis=-1)

        def _rotate_half(x):
            d = x.shape[-1] // 2
            return jnp.concatenate([-x[..., d:], x[..., :d]], axis=-1)

        def _apply_rope(x, cos, sin):
            return x * cos + _rotate_half(x) * sin
        B, S, D = x.shape
        m = 0.1 * 1.0 * math.log(128.0) + 1.0
        softmax_scale = QHD ** (-0.5) * m * m
        q = _rmsnorm(x @ wq_a.T, q_a_ln_w) @ wq_b.T
        q = q.reshape(B, S, H, QHD)
        q_nope, q_pe = (q[..., :NOPE], q[..., NOPE:])
        ckv_kpe = x @ wkv_a.T
        ckv, k_pe = (ckv_kpe[..., :KVR], ckv_kpe[..., KVR:])
        kv = _rmsnorm(ckv, kv_a_ln_w) @ wkv_b.T
        kv = kv.reshape(B, S, H, NOPE + VD)
        k_nope, v = (kv[..., :NOPE], kv[..., NOPE:])
        cos, sin = _yarn_cos_sin(S)
        q_pe = _apply_rope(_deinterleave(q_pe), cos[None, :, None, :], sin[None, :, None, :])
        k_pe = _apply_rope(_deinterleave(k_pe), cos[None, :, :], sin[None, :, :])
        q_full = jnp.concatenate([q_nope, q_pe], axis=-1)
        k_full = jnp.concatenate([k_nope, jnp.broadcast_to(k_pe[:, :, None, :], (B, S, H, ROPE))], axis=-1)
        scores = jnp.einsum('bqhd,bkhd->bhqk', q_full, k_full) * softmax_scale
        causal = jnp.tril(jnp.ones((S, S), dtype=bool))
        scores = jnp.where(causal[None, None], scores, jnp.finfo(scores.dtype).min)
        attn = jax.nn.softmax(scores, axis=-1)
        out = jnp.einsum('bhqk,bkhd->bqhd', attn, v).reshape(B, S, H * VD)
        return out @ wo.T

    def _L0_ffn_ref(h, gate_w, gate_b, w1, b1, w2, b2):
        import jax, jax.numpy as jnp
        import numpy as np
        B, S, D = (4, 256, 512)
        NUM_EXPERTS, TOP_K = (3, 2)

        def _expert_outputs(h, w1, b1, w2, b2):
            pre = jnp.einsum('bsd,edf->ebsf', h, w1) + b1[:, None, None, :]
            act = jnp.stack([jnp.tanh(pre[0]), jax.nn.gelu(pre[1], approximate=False), jax.nn.silu(pre[2])])
            return jnp.einsum('ebsf,efd->ebsd', act, w2) + b2[:, None, None, :]
        b, s, d = h.shape
        vision_len = int(s * 0.3)
        text_strength = jnp.mean(jnp.abs(h[:, vision_len:, :]), axis=(1, 2), keepdims=True)
        vision_strength = jnp.mean(jnp.abs(h[:, :vision_len, :]), axis=(1, 2), keepdims=True)
        modality_ratio = text_strength / (vision_strength + 1e-08)
        modality_ratio = jnp.broadcast_to(modality_ratio, (b, s, 1))
        router_input = jnp.concatenate([h, modality_ratio], axis=-1)
        gate_logits = router_input @ gate_w + gate_b
        gate_scores = jax.nn.softmax(gate_logits, axis=-1)
        top_val, top_idx = jax.lax.top_k(gate_scores, TOP_K)
        top_val = top_val / (jnp.sum(top_val, axis=-1, keepdims=True) + 1e-08)
        expert_out = _expert_outputs(h, w1, b1, w2, b2)
        moe_out = jnp.zeros_like(h)
        batch_idx = jnp.arange(b)
        for i in range(TOP_K):
            j = top_idx[:, 0, i]
            out_i = expert_out[j, batch_idx]
            moe_out = moe_out + top_val[..., i:i + 1] * out_i
        return moe_out

    def _L1_xattn_ref(query, kv, Wq, bq, Wkv, bkv, Wo, bo):
        import jax, jax.numpy as jnp
        import numpy as np
        HID = 512
        NHEAD = 32
        NKV = 8
        HDIM = 128
        G = NHEAD // NKV
        B, L, _ = query.shape
        Lk = kv.shape[1]
        scale = jnp.asarray(1.0 / np.sqrt(HDIM), query.dtype)
        q = (query @ Wq + bq).reshape(B, L, NKV, G, HDIM)
        k_, v_ = jnp.split(kv @ Wkv + bkv, 2, axis=-1)
        k = k_.reshape(B, Lk, NKV, HDIM)
        v = v_.reshape(B, Lk, NKV, HDIM)
        scores = jnp.einsum('blkgd,bmkd->bkglm', q, k) * scale
        attn = jax.nn.softmax(scores, axis=-1)
        o = jnp.einsum('bkglm,bmkd->blkgd', attn, v).reshape(B, L, NHEAD * HDIM)
        return o @ Wo + bo

    def _L1_attn_ref(x, in_proj_w, conv_w, conv_b, dt_bias, A_log, D, norm_w, out_proj_w):
        import jax, jax.numpy as jnp
        import numpy as np
        B, S, HID = (2, 256, 512)
        H, P, N, G, K = (128, 64, 128, 8, 4)
        INTER = H * P
        CONV_DIM = INTER + 2 * G * N
        CHUNK = 128
        EPS = 1e-05
        DT_MIN, DT_MAX = (0.0, 100.0)

        def _segsum(a):
            c = a.shape[-1]
            s = jnp.cumsum(a, axis=-1)
            diff = s[..., :, None] - s[..., None, :]
            mask = jnp.tril(jnp.ones((c, c), dtype=bool))
            return jnp.where(mask, diff, -jnp.inf)
        b, s, _ = x.shape
        proj = jnp.einsum('bsd,ed->bse', x, in_proj_w)
        gate = proj[..., :INTER]
        hBC = proj[..., INTER:INTER + CONV_DIM]
        dt = proj[..., INTER + CONV_DIM:]
        xc = jnp.transpose(hBC, (0, 2, 1))
        xc = jax.lax.conv_general_dilated(xc, conv_w, (1,), [(K - 1, 0)], dimension_numbers=('NCH', 'OIH', 'NCH'), feature_group_count=CONV_DIM)
        xc = xc + conv_b[None, :, None]
        hBC = jax.nn.silu(jnp.transpose(xc, (0, 2, 1)))
        hs = hBC[..., :INTER].reshape(b, s, H, P)
        Bm = hBC[..., INTER:INTER + G * N].reshape(b, s, G, N)
        Cm = hBC[..., INTER + G * N:].reshape(b, s, G, N)
        A = -jnp.exp(A_log)
        dt = jnp.clip(jax.nn.softplus(dt + dt_bias), DT_MIN, DT_MAX)
        rep = H // G
        Bh = jnp.repeat(Bm, rep, axis=2)
        Ch = jnp.repeat(Cm, rep, axis=2)
        nc = s // CHUNK
        xch = (hs * dt[..., None]).reshape(b, nc, CHUNK, H, P)
        Bc = Bh.reshape(b, nc, CHUNK, H, N)
        Cc = Ch.reshape(b, nc, CHUNK, H, N)
        A_dt = (dt * A).reshape(b, nc, CHUNK, H).transpose(0, 3, 1, 2)
        A_cum = jnp.cumsum(A_dt, axis=-1)
        L = jnp.exp(_segsum(A_dt))
        Y_diag = jnp.einsum('bzlhn,bzshn,bhzls,bzshp->bzlhp', Cc, Bc, L, xch)
        decay_states = jnp.exp(A_cum[..., -1:] - A_cum)
        states = jnp.einsum('bzlhn,bhzl,bzlhp->bzhpn', Bc, decay_states, xch)
        states_p = jnp.concatenate([jnp.zeros_like(states[:, :1]), states], axis=1)
        A_last = jnp.pad(A_cum[..., -1], ((0, 0), (0, 0), (1, 0)))
        decay_chunk = jnp.exp(_segsum(A_last))
        new_states = jnp.einsum('bhzc,bchpn->bzhpn', decay_chunk, states_p)
        prev = new_states[:, :-1]
        Y_off = jnp.einsum('bzlhn,bzhpn,bhzl->bzlhp', Cc, prev, jnp.exp(A_cum))
        Y = (Y_diag + Y_off).reshape(b, s, H, P) + hs * D[None, None, :, None]
        y = Y.reshape(b, s, INTER)
        g = y * jax.nn.silu(gate)
        gg = g.reshape(b, s, G, INTER // G)
        var = jnp.mean(gg * gg, axis=-1, keepdims=True)
        gg = gg * jax.lax.rsqrt(var + EPS)
        out = gg.reshape(b, s, INTER) * norm_w
        return jnp.einsum('bsi,oi->bso', out, out_proj_w)

    def _L1_ffn_ref(x, weight, bias, gate_w, in_channel_scale, out_channel_scale):
        import jax, jax.numpy as jnp
        import numpy as np

        @jax.custom_vjp
        def ste_sign(w):
            return jnp.sign(w)

        def _ste_fwd(w):
            return (jnp.sign(w), w)

        def _ste_bwd(w, g):
            mask = ((w > -1) & (w < 1)).astype(g.dtype)
            return (g * mask,)
        ste_sign.defvjp(_ste_fwd, _ste_bwd)
        B, S, H = x.shape
        xf = x.reshape(-1, H)
        router_logits = xf @ gate_w.T
        routing = jax.nn.softmax(router_logits.astype(jnp.float32), axis=1).astype(x.dtype)
        in_scale = routing @ in_channel_scale
        out_scale = routing @ out_channel_scale
        wb = ste_sign(weight)
        out = xf * in_scale @ wb.T * out_scale + bias
        return out.reshape(B, S, -1)
    x = x + _L0_xattn_ref(_layernorm(x, axis=-1), ctx_4096, L0_xattn_Wq, L0_xattn_Wk, L0_xattn_Wv, L0_xattn_Wo)
    x = x + _L0_attn_ref(_layernorm(x, axis=-1), L0_attn_wq_a, L0_attn_q_a_ln_w, L0_attn_wq_b, L0_attn_wkv_a, L0_attn_kv_a_ln_w, L0_attn_wkv_b, L0_attn_wo)
    x = x + _L0_ffn_ref(_layernorm(x, axis=-1), L0_ffn_gate_w, L0_ffn_gate_b, L0_ffn_w1, L0_ffn_b1, L0_ffn_w2, L0_ffn_b2)
    x = x + _L1_xattn_ref(_layernorm(x, axis=-1), ctx_4096, L1_xattn_Wq, L1_xattn_bq, L1_xattn_Wkv, L1_xattn_bkv, L1_xattn_Wo, L1_xattn_bo)
    x = x + _L1_attn_ref(_layernorm(x, axis=-1), L1_attn_in_proj_w, L1_attn_conv_w, L1_attn_conv_b, L1_attn_dt_bias, L1_attn_A_log, L1_attn_D, L1_attn_norm_w, L1_attn_out_proj_w)
    x = x + _L1_ffn_ref(_layernorm(x, axis=-1), L1_ffn_weight, L1_ffn_bias, L1_ffn_gate_w, L1_ffn_in_channel_scale, L1_ffn_out_channel_scale)
    return x

_drawn_inputs = setup_inputs


def setup_inputs(seed=0):
    import zlib

    import numpy as np

    out = dict(_drawn_inputs(seed))
    spreads = {'L0_attn_q_a_ln_w': (1.0, 0.6),
     'L0_attn_kv_a_ln_w': (1.0, 0.6),
     'L0_ffn_gate_b': (0.0, 0.574),
     'L0_ffn_b1': (0.0, 0.336),
     'L0_ffn_b2': (0.0, 0.1),
     'L1_xattn_bq': (0.0, 0.8),
     'L1_xattn_bkv': (0.0, 0.1),
     'L1_xattn_bo': (0.0, 0.1),
     'L1_attn_conv_b': (0.0, 0.1),
     'L1_attn_dt_bias': (1.0, 0.6),
     'L1_attn_D': (1.0, 0.2),
     'L1_attn_norm_w': (1.0, 0.2)}
    factors = {'L0_attn_wq_a': 8.0,
     'L0_attn_wq_b': 8.0,
     'L1_xattn_Wq': 3.508,
     'L1_attn_A_log': 8.0,
     'L1_ffn_bias': 8.0}
    for name, (base, spread) in spreads.items():
        noise = np.random.default_rng([zlib.crc32(name.encode()), seed]).standard_normal(out[name].shape)
        drawn = base * np.exp(spread * noise) if base else spread * noise
        out[name] = jnp.asarray(drawn.astype(out[name].dtype))
    for name, factor in factors.items():
        out[name] = (out[name] * factor).astype(out[name].dtype)
    return out
```

```python
import math
from contextlib import ExitStack

import concourse.bass as bass
from concourse import mybir

ALU = mybir.AluOpType
ACT = mybir.ActivationFunctionType
AX = mybir.AxisListType
F32 = mybir.dt.float32
F32R = mybir.dt.float32r

P = 128
TOK = 128
D = 512
DC = D // P
CTX = 2048
NHEAD = 32
EPS = 1e-5
RMS_EPS = 1e-6
ATT_SCALE = 1.0 / float(P) ** 0.5
MASKED = -1.0e30
C_IDENT, C_ONES, C_UPTO, C_AFTER, C_CAUSAL, C_COS, C_SIN, C_MEANS = 0, 128, 256, 384, 512, 640, 672, 704
C_WIDTH = 706


class Tally:

    def __init__(self, before=()):
        self.before, self.count, self.turn, self.step = dict(before), {}, 0, None

    def add(self, name, by=1):
        self.count[name] = self.count.get(name, 0) + by

    def local(self, name):
        return self.count.get(name, 0)

    def at(self, name, back=0):
        value = self.before.get(name, 0) + self.count.get(name, 0) - back
        if self.step is None:
            return value
        return value + self.turn * self.step.get(name, 0)


def attention_plan(kv_groups, key_tiles):
    pairs = 4 * kv_groups
    banks = (key_tiles + 3) // 4
    t_uses = (key_tiles + 1) // 2

    class Order(list):
        def __init__(self):
            super().__init__()
            self.waiting = []

        def scores(self, p, half):
            self.flush()
            self += [("S", p, half), ("MAX", p, half)]
            self.waiting = [("EXP", p, half, c) for c in range(banks)]

        def weave(self, event):
            self.append(event)
            if self.waiting:
                self.append(self.waiting.pop(0))

        def flush(self):
            self += self.waiting
            self.waiting = []

    prologue = Order()
    prologue += [("WV",), ("WK",), ("QMM",)]
    prologue += [("K", 0, c) for c in range(banks)]
    prologue += [("QTR",)]
    prologue.scores(0, 0)
    for k in range(t_uses):
        prologue.weave(("V", k))
    prologue.scores(0, 1)
    prologue.flush()

    def turn(last):
        o = Order()
        for p in range(pairs):
            more = p < pairs - 1 or not last
            q2, kv2 = (p + 2) % 2 == 0, (p + 2) % (2 * kv_groups) == 0
            more2 = p + 2 < pairs or not last
            if kv2 and more2:
                o.append(("WK",))
            if p == pairs - 1 and not last:
                o.append(("WV",))
            if more:
                o.scores((p + 1) % pairs, 0)
            if p > 0:
                o += [("PV", p - 1, t_uses - 1), ("NORM", p - 1)]
                if p % 4 == 0:
                    o.append(("WO",))
            middle = t_uses // 2
            for k in range(t_uses):
                if k == middle:
                    if more:
                        o.scores((p + 1) % pairs, 1)
                    else:
                        o.flush()
                    if q2 and more2:
                        o.append(("QMM",))
                o.weave(("T", p, k))
                if k == middle + 1:
                    o.append(("RD", p))
                    if q2 and more2:
                        o.append(("QTR",))
                if k > 0:
                    o.append(("PV", p, k - 1))
            o.flush()
            if kv2 and more2:
                o += [("K", ((p + 2) % pairs) // (2 * kv_groups), c) for c in range(banks)]
        o += [("PV", pairs - 1, t_uses - 1), ("NORM", pairs - 1)]
        if not last:
            o += [("V", k) for k in range(t_uses)]
        o.append(("WO",))
        return list(o)

    return list(prologue), turn(False), turn(True)


SIGNALS = {
    "WK": {"wk_hi": 1, "wk_lo": 1},
    "WV": {"wv_hi": 1, "wv_lo": 1},
    "QMM": {"q_half": 1, "t_full": 1, "q_row": 1},
    "QTR": {"t_full": 1, "q_col": 1, "q_hi": 1, "q_lo": 1},
    "K": {"k_full": 1, "k_hi": 1, "k_lo": 1},
    "V": {"t_full": 1, "v_hi": 1, "v_lo": 1},
    "S": {"s_part": 1, "s_full": 1},
    "MAX": {"max_step": 1, "neg_max": 1},
    "EXP": {"exps": 1},
    "T": {"t_full": 1, "p_hi": 1, "p_lo": 1},
    "PV": {"pv": 1},
    "RD": {"rd_step": 2, "diag": 1},
    "NORM": {"t_full": 1, "r_row": 1, "heads_out": 1},
    "WO": {"wo_part": 3, "wo_full": 1, "x_sum": 1},
}
T_READ = {"QMM": "q_row", "QTR": "q_col", "V": "v_lo", "T": "p_lo", "NORM": "r_row"}


STEPS = {
    "pe_steps": [("m_latent", 1), ("m_aT_full", 1), ("m_qT_full", 8), ("m_s_full", 8), ("m_pT_full", 8),
                 ("m_out_full", 8), ("m_wo_used", 16), ("e_means", 1), ("e_logits", 1), ("e_chosen", 1),
                 ("s_dt_full", 1), ("s_cb_full", 2), ("f_logits", 1), ("f_rT_full", 1), ("f_scales", 2),
                 ("f_xT_full", 1), ("f_out_full", 1)],
    "act_steps": [("m_sq", 2), ("m_aT_ready", 1), ("m_qT_ready", 8), ("m_exps", 32), ("m_pT_ready", 8),
                  ("e_abs", 1), ("e_exp", 1), ("s_dt_abs", 1), ("s_dt_exp", 1), ("s_a_exp", 1), ("s_dt_ln", 1),
                  ("f_sign_ready", 1), ("f_exp", 1), ("f_rT_ready", 1), ("f_os_ready", 1), ("f_xT_ready", 1)],
    "dve_steps": [("m_a_clear", 1), ("m_var", 1), ("m_a_ready", 1), ("m_out_ready", 8), ("m_x_sum", 1),
                  ("e_weighed", 1), ("e_ratio", 1), ("e_neg_max", 1), ("e_choice", 1), ("e_x_sum", 1),
                  ("bq_scaled", 1), ("bo_added", 1), ("s_dt_u", 1), ("s_cb_ready", 2), ("s_var_ready", 1),
                  ("s_scaled", 16), ("s_x_sum", 1), ("f_neg_max", 1), ("f_inv", 1), ("f_routing", 1),
                  ("f_scaled", 1), ("f_biased", 1), ("f_y", 1), ("f_x_sum", 1)],
}
SHARED = {}
for _carrier, _signals in STEPS.items():
    _before = 0
    for _name, _times in _signals:
        SHARED[_name] = (_carrier, _before)
        _before += _times


def build(nc, a, out):
    where = [-(-nc.sbuf_base // 64) * 64]

    def place(name, shape, dt=F32, at=None):
        size = 4
        for n in shape[1:]:
            size *= n
        offset = where[0] if at is None else at
        t = nc.alloc_sbuf_tensor_at(name, shape, dt, offset=offset)
        assert offset + size <= nc.sbuf_usable_end, (name, offset + size)
        if at is None:
            where[0] = offset + -(-size // 32) * 32
        return t

    with ExitStack() as ctx:
        sems = {}

        def sem(name):
            name = SHARED.get(name, (name, 0))[0]
            if name not in sems:
                sems[name] = ctx.enter_context(nc.semaphore(name))
            return sems[name]

        def reach(name, times=1):
            return sem(name), SHARED.get(name, (name, 0))[1] + times

        banks = ctx.enter_context(nc.psum_tensor("banks", [P, 8, 512], F32))
        PV_BANK = 7

        const = place("const", [P, C_WIDTH])
        ident = const[:, C_IDENT:C_IDENT + P]
        ones = const[:, C_ONES:C_ONES + P]
        x = place("x", [TOK, D])
        xlnT = place("xlnT", [P, DC, TOK])
        ln = place("ln", [TOK, 24])
        rows = place("rows", [TOK, D])
        xln = rows
        shared = where[0]

        KMAX = CTX + TOK
        ctx_hi = place("ctx_hi", [P, DC, KMAX], F32R)
        ctx_lo = place("ctx_lo", [P, DC, KMAX], F32R)
        attn_base = where[0]
        v_hi = place("v_hi", [P, 17, 256], F32R)
        v_lo = place("v_lo", [P, 17, 256], F32R)
        k_hi = place("k_hi", [P, KMAX], F32R)
        k_lo = place("k_lo", [P, KMAX], F32R)
        prob = place("prob", [TOK, 4, KMAX])
        q_hi = place("q_hi", [P, 4, TOK], F32R)
        q_lo = place("q_lo", [P, 4, TOK], F32R)
        heads = place("heads", [P, 8, TOK])
        pt_hi = place("pt_hi", [P, 2, 512], F32R)
        pt_lo = place("pt_lo", [P, 2, 512], F32R)
        ring = place("ring", [P, 2, 1024])
        wk_hi = place("wk_hi", [P, DC, P], F32R)
        wk_lo = place("wk_lo", [P, DC, P], F32R)
        wv_hi = place("wv_hi", [P, DC, 256], F32R)
        wv_lo = place("wv_lo", [P, DC, 256], F32R)
        wk_raw = place("wk_raw", [P, DC, P])
        wv_raw = place("wv_raw", [P, DC, 256])
        inv_row = place("inv_row", [P, 256])
        diag = place("diag", [P, 2, P])
        att = place("att", [P, 2, 2, 5 + 3 + 1])
        inv = place("inv", [P, 4])
        bias_q = place("bias_q", [P, NHEAD])
        bias_k = place("bias_k", [P, 8])
        bias_v = place("bias_v", [P, 8])


        where[0] = attn_base
        m_wa = place("m_wa", [P, DC, 224])
        m_wqb = place("m_wqb", [P, 4096])
        m_wkvb = place("m_wkvb", [P, 6144])
        m_a = place("m_a", [TOK, 384])
        m_aT = place("m_aT", [P, 3, TOK])
        m_q = place("m_q", [TOK, NHEAD, P])
        m_v = place("m_v", [TOK, NHEAD, P])
        m_qT = place("m_qT", [P, NHEAD, TOK])
        m_kT = place("m_kT", [P, NHEAD, TOK])
        m_st = place("m_st", [TOK, 4, NHEAD])
        m_rot = place("m_rot", [TOK, 4, 4, 32])
        m_lnw = place("m_lnw", [P, 2])
        m_ring = place("m_ring", [P, 4, 1024])

        where[0] = attn_base
        e_w1 = place("e_w1", [P, 3, DC, D])
        e_w2 = place("e_w2", [P, 3, DC, D])
        e_act = place("e_act", [P, 3, DC, TOK])
        e_gw = place("e_gw", [P, DC, 4])
        e_row = place("e_row", [1, 8 + 3 * D + P])
        e_b1 = place("e_b1", [P, 12])
        e_s = place("e_s", [TOK, 64])

        where[0] = shared
        NSLOT = 5
        s_w = place("s_w", [P, NSLOT, DC, D])
        s_decay = place("s_decay", [TOK, 128, P])
        s_g = place("s_g", [TOK, 8192])
        s_mix = place("s_mix", [TOK, 2, 8, P])
        s_conv = place("s_conv", [P, 2, DC, TOK])
        s_tanh = place("s_tanh", [P, 2, DC, TOK])
        s_chan = place("s_chan", [P, 2, DC, TOK])
        s_hs = place("s_hs", [TOK, 2, 512])
        s_gate = place("s_gate", [TOK, 2, 512])
        s_bT = place("s_bT", [P, 8, TOK])
        s_cT = place("s_cT", [P, 8, TOK])
        s_cb = place("s_cb", [TOK, 8, TOK])
        s_seg = place("s_seg", [TOK, 2, 4, P])
        s_cw = place("s_cw", [P, 80, 4])
        s_cbias = place("s_cbias", [P, 80])
        s_dt = place("s_dt", [TOK, 8, 128])
        s_row = place("s_row", [1, 3 * 128])
        s_nw = place("s_nw", [P, 64])
        s_var = place("s_var", [TOK, 4, 16])
        s_y = place("s_y", [TOK, 2, 512])
        s_sq = place("s_sq", [TOK, 512])

        where[0] = shared
        f_w = place("f_w", [P, DC, D])
        f_sign = place("f_sign", [P, DC, D])
        f_gw = place("f_gw", [P, DC, 8])
        f_scale = place("f_scale", [8, 2, D])
        f_bias = place("f_bias", [TOK, D])
        f_xs = place("f_xs", [TOK, D])
        f_xT = place("f_xT", [P, DC, TOK])
        f_r = place("f_r", [TOK, 24])
        f_rT = place("f_rT", [8, TOK])
        f_os = place("f_os", [TOK, D])

        def ln_dve(dve, n):
            nc.vector.bn_stats(ln[:, 0:6], x[:]).then_inc(sem("ln_stats"), 1)
            dve.wait_ge(*reach("ln_stats", n + 1))
            nc.vector.bn_aggr(ln[:, 6:8], ln[:, 0:6]).then_inc(sem("ln_aggr"), 1)
            dve.wait_ge(*reach("ln_aggr", n + 1))
            nc.vector.tensor_scalar(ln[:, 8:9], ln[:, 7:8], EPS, None, ALU.add).then_inc(sem("ln_var"), 1)
            rsqrt_dve(dve, ln[:, 8:9], ln[:, 9:10], ln[:, 11:12])
            nc.vector.tensor_scalar(xln[:], x[:], ln[:, 6:7], ln[:, 9:10], ALU.subtract,
                                    ALU.mult).then_inc(sem("xln_ready"), 1)

        roots = [0, 0]
        own_steps = [0]

        def rsqrt_act(act, ready, count, v, y):
            roots[0] += 1
            act.wait_ge(*reach(ready, count))
            nc.scalar.activation(y, v, ACT.Ln).then_inc(sem("root_ln"), 1)
            act.wait_ge(*reach("root_ln", roots[0]))
            nc.scalar.activation(y, y, ACT.Exp, scale=-0.5).then_inc(sem("root_guess"), 1)

        def rsqrt_dve(dve, v, y, t):
            n = roots[1]
            roots[1] += 1
            dve.wait_ge(*reach("root_guess", n + 1))
            nc.vector.tensor_tensor(t, y, y, ALU.mult).then_inc(sem("root_step"), 1)
            dve.wait_ge(*reach("root_step", 4 * n + 1))
            nc.vector.tensor_tensor(t, t, v, ALU.mult).then_inc(sem("root_step"), 1)
            dve.wait_ge(*reach("root_step", 4 * n + 2))
            nc.vector.tensor_scalar(t, t, -0.5, 1.5, ALU.mult, ALU.add).then_inc(sem("root_step"), 1)
            dve.wait_ge(*reach("root_step", 4 * n + 3))
            nc.vector.tensor_tensor(y, y, t, ALU.mult).then_inc(sem("root_step"), 1)
            dve.wait_ge(*reach("root_step", 4 * n + 4))

        def ln_act_head(act, n):
            rsqrt_act(act, "ln_var", n + 1, ln[:, 8:9], ln[:, 9:10])

        def ln_act(act, n):
            ln_act_head(act, n)
            ln_act_tail(act, n)

        def ln_act_tail(act, n):
            act.wait_ge(*reach("xln_turned", n + 1))
            nc.scalar.activation(xlnT[:], banks[:, PV_BANK, :], ACT.Copy).then_inc(sem("xlnT_ready"), 1)

        def ln_pe(pe, n):
            pe.wait_ge(*reach("xln_ready", n + 1))
            for c in range(DC):
                mm = pe.transpose(banks[:, PV_BANK, c * P:(c + 1) * P], xln[:, c * P:(c + 1) * P], ident)
            mm.then_inc(sem("xln_turned"), 1)
            pe.wait_ge(*reach("xlnT_ready", n + 1))

        def three_passes(pe, dst, pairs, start=True, stop=True):
            for n, (w_hi, w_lo, m_hi, m_lo) in enumerate(pairs):
                pe.matmul(dst, w_hi, m_hi, start=start and n == 0, stop=False)
                pe.matmul(dst, w_hi, m_lo, start=False, stop=False)
                mm = pe.matmul(dst, w_lo, m_hi, start=False, stop=stop and n == len(pairs) - 1)
            return mm

        def ctx_sync(sp):
            for c in range(DC):
                sp.dma_start(prob[:, c, 0:CTX], a["ctxT"][c * P:(c + 1) * P, :]).then_inc(sem(f"ctx_in{c}"), 16)

        def ctx_act(act):
            for c in range(DC):
                act.wait_ge(sem(f"ctx_in{c}"), 16)
                nc.scalar.activation(ctx_hi[:, c, 0:CTX], prob[:, c, 0:CTX], ACT.Copy).then_inc(sem("ctx_hi"), 1)

        def ctx_dve(dve):
            for c in range(DC):
                dve.wait_ge(*reach("ctx_hi", c + 1))
                nc.vector.tensor_tensor(ctx_lo[:, c, 0:CTX], prob[:, c, 0:CTX],
                                        ctx_hi[:, c, 0:CTX].bitcast(F32), ALU.subtract).then_inc(sem("ctx_lo"), 1)

        class Cross:
            def __init__(self, layer, before=None):
                self.layer = layer
                self.kv_groups, self.tiles, self.turns = ((2, 17, 2), (1, 16, 4))[layer]
                self.keys = self.tiles * P
                self.cuts = ([448, 448, 448, 448, 384], [512] * 4)[layer]
                self.nb = len(self.cuts)
                self.off = [sum(self.cuts[:c]) for c in range(self.nb)]
                self.maxima = ([(0, 2), (2, 4), (4, 5)], [(0, 2), (2, 4)])[layer]
                self.t_uses = (self.tiles + 1) // 2
                self.heads = 8 * self.kv_groups
                self.plan = attention_plan(self.kv_groups, self.tiles)
                self.Wq, self.Wo = a[f"Wq{layer}"], a[f"Wo{layer}"]
                self.before, self.items_before = (before.totals(), 32) if before else ({}, 0)

            def sem(self, name):
                return sem("x_" + name)

            def pair_exps(self, t):
                return self.before.get("exps", 0) + self.nb * (2 * t.local("NORM") + 2)

            def totals(self):
                last = []
                self.walk(lambda e, t, i: last.append(t))
                return last[-1].count

            def walk(self, visit):
                prologue, body, last = self.plan
                tally = Tally(self.before)
                turns = [(0, prologue)] + [(i, body) for i in range(self.turns - 1)] + [(self.turns - 1, last)]
                for i, events in turns:
                    for e in events:
                        visit(e, tally, i)
                        for name, by in SIGNALS[e[0]].items():
                            tally.add(name, by)
                        tally.add(e[0])
                        if e[0] == "MAX":
                            tally.add("max_step", len(self.maxima) - 1)

            def sync(self, sp):
                L = self.layer
                Wk, Wv = a[f"Wk{L}"], a[f"Wv{L}"]
                item, used = [0], []

                def load_kv(e, t):
                    n = t.local(e)
                    raw, W, w = (wk_raw, Wk, P) if e == "WK" else (wv_raw, Wv, 256)
                    if n > 0:
                        sp.wait_ge(self.sem(e.lower() + "_hi"), t.at(e.lower() + "_hi"))
                        sp.wait_ge(self.sem(e.lower() + "_lo"), t.at(e.lower() + "_lo"))
                    sp.dma_start(raw[:], W[:, n * w:(n + 1) * w].rearrange("(c p) n -> p c n", p=P)
                                 ).then_inc(self.sem(e.lower() + "_in"), 16)

                def ring_load(src, user, value):
                    n = item[0]
                    item[0] += 1
                    if n >= 2:
                        sp.wait_ge(self.sem(used[n - 2][0]), used[n - 2][1])
                    used.append((user, value))
                    sp.dma_start(ring[:, n % 2, :], src).then_inc(self.sem(f"ring_in{n % 2}"), 16)

                def visit(e, t, i):
                    if e[0] in ("WK", "WV"):
                        load_kv(e[0], t)
                    elif e[0] == "QMM":
                        g = t.local("QMM")
                        for h in range(2):
                            ring_load(self.Wq[h * 256:(h + 1) * 256, g * 512:(g + 1) * 512]
                                      .rearrange("(c p) n -> p c n", p=P),
                                      *(("q_half", t.at("q_half") + 1), ("t_full", t.at("t_full") + 1))[h])
                    elif e[0] == "WO":
                        g = t.local("WO")
                        for h in range(4):
                            r = (g * 8 + 2 * h) * P
                            ring_load(self.Wo[r:r + 2 * P, :].rearrange("(c p) n -> p c n", p=P),
                                      *(("wo_part", t.at("wo_part") + h + 1), ("wo_full", t.at("wo_full") + 1))[h == 3])

                self.walk(visit)

            def pe(self, pe):
                uses = []
                item = [0]

                def t_slot(e, t):
                    u = len(uses)
                    if u >= 2:
                        pe.wait_ge(self.sem(uses[u - 2][0]), uses[u - 2][1])
                    uses.append((T_READ[e], t.at(T_READ[e]) + 1))
                    return 5 + u % 2

                def ring_item():
                    n = item[0]
                    item[0] += 1
                    pe.wait_ge(self.sem(f"ring_in{n % 2}"), 16 * ((self.items_before + n) // 2 + 1))
                    return ring[:, n % 2, :].rearrange("p (c n) -> p c n", c=2)

                def visit(e, t, i):
                    kind = e[0]
                    if kind == "QMM":
                        b = t_slot(kind, t)
                        for h in range(2):
                            w = ring_item()
                            for c in range(2):
                                mm = pe.matmul(banks[:, b, :], xlnT[:, 2 * h + c, :], w[:, c, :],
                                               start=(h + c == 0), stop=(h + c == 2))
                            mm.then_inc(self.sem(("q_half", "t_full")[h]), 1)
                    elif kind == "QTR":
                        b = t_slot(kind, t)
                        pe.wait_ge(self.sem("q_row"), t.at("q_row"))
                        for h in range(4):
                            mm = pe.transpose(banks[:, b, h * P:(h + 1) * P], rows[:, h * P:(h + 1) * P], ident)
                        mm.then_inc(self.sem("t_full"), 1)
                    elif kind == "K":
                        _, _, c = e
                        if c == 0:
                            pe.wait_ge(self.sem("wk_hi"), t.at("wk_hi"))
                            pe.wait_ge(self.sem("wk_lo"), t.at("wk_lo"))
                            if t.local("exps"):
                                pe.wait_ge(self.sem("exps"), t.at("exps"))
                            if not t.local("K"):
                                pe.wait_ge(*reach("ctx_hi", DC + (self.layer == 0)))
                                pe.wait_ge(*reach("ctx_lo", DC + (self.layer == 0)))
                        o, w = self.off[c], self.cuts[c]
                        three_passes(pe, banks[:, c, 0:w],
                                     [(wk_hi[:, d, :], wk_lo[:, d, :], ctx_hi[:, d, o:o + w], ctx_lo[:, d, o:o + w])
                                      for d in range(DC)]).then_inc(self.sem("k_full"), 1)
                    elif kind == "V":
                        b = t_slot(kind, t)
                        if e[1] == 0:
                            pe.wait_ge(self.sem("wv_hi"), t.at("wv_hi"))
                            pe.wait_ge(self.sem("wv_lo"), t.at("wv_lo"))
                        for n, tile in enumerate(range(2 * e[1], min(2 * e[1] + 2, self.tiles))):
                            k = slice(tile * P, (tile + 1) * P)
                            mm = three_passes(pe, banks[:, b, n * 256:(n + 1) * 256],
                                              [(ctx_hi[:, d, k], ctx_lo[:, d, k], wv_hi[:, d, :], wv_lo[:, d, :])
                                               for d in range(DC)])
                        mm.then_inc(self.sem("t_full"), 1)
                    elif kind == "S":
                        _, p, half = e
                        pe.wait_ge(self.sem("q_hi"), t.at("q_hi"))
                        pe.wait_ge(self.sem("q_lo"), t.at("q_lo"))
                        pe.wait_ge(self.sem("k_hi"), t.at("k_hi"))
                        pe.wait_ge(self.sem("k_lo"), t.at("k_lo"))
                        if t.local("exps"):
                            pe.wait_ge(self.sem("exps"), t.at("exps"))
                        h = 2 * (p % 2) + half
                        for c in range(self.nb):
                            k = slice(self.off[c], self.off[c] + self.cuts[c])
                            mm = three_passes(pe, banks[:, c, 0:self.cuts[c]],
                                              [(q_hi[:, h, :], q_lo[:, h, :], k_hi[:, k], k_lo[:, k])])
                            if c == 1:
                                mm.then_inc(self.sem("s_part"), 1)
                        mm.then_inc(self.sem("s_full"), 1)
                    elif kind == "T":
                        _, p, k = e
                        b = t_slot(kind, t)
                        if k == 0:
                            pe.wait_ge(self.sem("exps"), self.pair_exps(t))
                        for n, tile in enumerate(range(2 * k, min(2 * k + 2, self.tiles))):
                            for half in range(2):
                                mm = pe.transpose(banks[:, b, (2 * n + half) * P:(2 * n + half + 1) * P],
                                                  prob[:, 2 * (p % 2) + half, tile * P:(tile + 1) * P], ident)
                        mm.then_inc(self.sem("t_full"), 1)
                    elif kind == "PV":
                        _, p, k = e
                        n = t.local("PV")
                        pe.wait_ge(self.sem("p_hi"), t.at("PV") + 1)
                        pe.wait_ge(self.sem("p_lo"), t.at("PV") + 1)
                        pe.wait_ge(self.sem("v_hi"), t.at("v_hi"))
                        pe.wait_ge(self.sem("v_lo"), t.at("v_lo"))
                        if k == 0:
                            if t.local("heads_out") > 1:
                                pe.wait_ge(self.sem("heads_out"), t.at("heads_out") - 1)
                            if t.local("x_sum"):
                                pe.wait_ge(self.sem("x_sum"), t.at("x_sum"))
                        kv = p // (2 * self.kv_groups)
                        dst = banks[:, PV_BANK, (p % 2) * 256:(p % 2) * 256 + 256]
                        tiles = range(2 * k, min(2 * k + 2, self.tiles))
                        for tt, tile in enumerate(tiles):
                            v = (v_hi[:, tile, kv * P:(kv + 1) * P], v_lo[:, tile, kv * P:(kv + 1) * P])
                            m = slice(tt * 256, (tt + 1) * 256)
                            mm = three_passes(pe, dst, [(*v, pt_hi[:, n % 2, m], pt_lo[:, n % 2, m])],
                                              start=(tile == 0), stop=(tile == self.tiles - 1))
                        mm.then_inc(self.sem("pv"), 1)
                    elif kind == "NORM":
                        b = t_slot(kind, t)
                        pe.wait_ge(self.sem("diag"), t.at("NORM") + 1)
                        pe.matmul(banks[:, b, 0:256], ones, diag[:].rearrange("p h n -> p (h n)"),
                                  start=True, stop=True).then_inc(self.sem("t_full"), 1)
                    elif kind == "WO":
                        pe.wait_ge(self.sem("heads_out"), t.at("heads_out"))
                        for g in range(4):
                            w = ring_item()
                            for h in range(2):
                                mm = pe.matmul(banks[:, PV_BANK, :], heads[:, 2 * g + h, :], w[:, h, :],
                                               start=(g + h == 0), stop=(g == 3 and h == 1))
                            mm.then_inc(self.sem("wo_part" if g < 3 else "wo_full"), 1)

                self.walk(visit)

            def act(self, act):
                def visit(e, t, i):
                    kind, nxt = e[0], t.at("t_full") + 1
                    if kind == "WK":
                        act.wait_ge(self.sem("wk_in"), 16 * (t.at("WK") + 1))
                        if t.local("K"):
                            act.wait_ge(self.sem("k_full"), t.at("k_full"))
                        nc.scalar.activation(wk_hi[:], wk_raw[:], ACT.Copy).then_inc(self.sem("wk_hi"), 1)
                    elif kind == "WV":
                        act.wait_ge(self.sem("wv_in"), 16 * (t.at("WV") + 1))
                        if t.local("V"):
                            act.wait_ge(self.sem("t_full"), t.at("t_full"))
                        nc.scalar.activation(wv_hi[:], wv_raw[:], ACT.Copy).then_inc(self.sem("wv_hi"), 1)
                    elif kind == "QMM":
                        act.wait_ge(self.sem("t_full"), nxt)
                        if t.local("QMM"):
                            act.wait_ge(self.sem("q_lo"), t.at("q_lo"))
                        elif self.layer == 1:
                            act.wait_ge(*reach("bo_added", 1))
                        nc.scalar.activation(rows[:], banks[:, 5 + (t.local("t_full")) % 2, :],
                                             ACT.Copy).then_inc(self.sem("q_row"), 1)
                    elif kind == "QTR":
                        act.wait_ge(self.sem("q_col"), t.at("q_col") + 1)
                        if t.local("S"):
                            act.wait_ge(self.sem("s_full"), t.at("s_full"))
                        nc.scalar.activation(q_hi[:].rearrange("p h n -> p (h n)"), rows[:],
                                             ACT.Copy).then_inc(self.sem("q_hi"), 1)
                    elif kind == "K":
                        _, j, c = e
                        o, w = self.off[c], self.cuts[c]
                        act.wait_ge(self.sem("k_full"), t.at("k_full") + 1)
                        if self.layer == 0:
                            nc.scalar.activation(k_hi[:, o:o + w], banks[:, c, 0:w],
                                                 ACT.Copy).then_inc(self.sem("k_hi"), 1)
                        else:
                            kv = t.local("K") // self.nb
                            nc.scalar.activation(k_hi[:, o:o + w], banks[:, c, 0:w], ACT.Identity,
                                                 bias=bias_k[:, kv:kv + 1]).then_inc(self.sem("k_hi"), 1)
                    elif kind == "V":
                        k = e[1]
                        n = min(2, self.tiles - 2 * k)
                        act.wait_ge(self.sem("t_full"), nxt)
                        nc.scalar.activation(v_hi[:, 2 * k:2 * k + n, :].rearrange("p t n -> p (t n)"),
                                             banks[:, 5 + t.local("t_full") % 2, 0:256 * n],
                                             ACT.Copy).then_inc(self.sem("v_hi"), 1)
                    elif kind == "EXP":
                        _, p, half, c = e
                        slot = 2 * (p % 2) + half
                        o, w = self.off[c], self.cuts[c]
                        act.wait_ge(self.sem("neg_max"), t.at("neg_max"))
                        nc.scalar.activation(prob[:, slot, o:o + w], banks[:, c, 0:w], ACT.Exp,
                                             bias=stat[:, slot, 8:9], accum_out=stat[:, slot, c:c + 1]
                                             ).then_inc(self.sem("exps"), 1)
                    elif kind == "T":
                        n, w = t.local("T"), 256 * min(2, self.tiles - 2 * e[2])
                        act.wait_ge(self.sem("t_full"), nxt)
                        if n >= 2:
                            act.wait_ge(self.sem("pv"), t.at("T") - 1)
                        nc.scalar.activation(pt_hi[:, n % 2, 0:w], banks[:, 5 + t.local("t_full") % 2, 0:w],
                                             ACT.Copy).then_inc(self.sem("p_hi"), 1)
                    elif kind == "NORM":
                        act.wait_ge(self.sem("t_full"), nxt)
                        if t.local("NORM"):
                            act.wait_ge(self.sem("heads_out"), t.at("heads_out"))
                        nc.scalar.activation(inv_row[:], banks[:, 5 + t.local("t_full") % 2, 0:256],
                                             ACT.Copy).then_inc(self.sem("r_row"), 1)

                self.walk(visit)

            def dve(self, dve):
                def minus(out, in0, hi):
                    return nc.vector.tensor_tensor(out, in0, hi.bitcast(F32), ALU.subtract)

                def visit(e, t, i):
                    kind, nxt = e[0], t.at("t_full") + 1
                    if kind == "WK":
                        dve.wait_ge(self.sem("wk_hi"), t.at("wk_hi") + 1)
                        minus(wk_lo[:], wk_raw[:], wk_hi[:]).then_inc(self.sem("wk_lo"), 1)
                    elif kind == "WV":
                        dve.wait_ge(self.sem("wv_hi"), t.at("wv_hi") + 1)
                        minus(wv_lo[:], wv_raw[:], wv_hi[:]).then_inc(self.sem("wv_lo"), 1)
                    elif kind == "QTR":
                        bank, g = banks[:, 5 + t.local("t_full") % 2, :], t.local("QTR")
                        dve.wait_ge(self.sem("t_full"), nxt)
                        if self.layer == 0:
                            ins = nc.vector.tensor_scalar(rows[:], bank, ATT_SCALE, None, ALU.mult)
                        else:
                            ins = nc.vector.scalar_tensor_tensor(
                                rows[:].rearrange("p (h n) -> p h n", h=4), bank.rearrange("p (h n) -> p h n", h=4),
                                ATT_SCALE, bias_q[:, 4 * g:4 * g + 4].unsqueeze(2).broadcast_to([P, 4, P]),
                                ALU.mult, ALU.add)
                        ins.then_inc(self.sem("q_col"), 1)
                        dve.wait_ge(self.sem("q_hi"), t.at("q_hi") + 1)
                        minus(q_lo[:].rearrange("p h n -> p (h n)"), rows[:],
                              q_hi[:].rearrange("p h n -> p (h n)")).then_inc(self.sem("q_lo"), 1)
                    elif kind == "K":
                        _, j, c = e
                        o, w = self.off[c], self.cuts[c]
                        dve.wait_ge(self.sem("k_hi"), t.at("k_hi") + 1)
                        if self.layer == 0:
                            minus(k_lo[:, o:o + w], banks[:, c, 0:w], k_hi[:, o:o + w]).then_inc(self.sem("k_lo"), 1)
                        else:
                            kv = t.local("K") // self.nb
                            nc.vector.scalar_tensor_tensor(
                                k_lo[:, o:o + w], banks[:, c, 0:w], bias_k[:, kv:kv + 1],
                                k_hi[:, o:o + w].bitcast(F32), ALU.add, ALU.subtract).then_inc(self.sem("k_lo"), 1)
                    elif kind == "V":
                        k = e[1]
                        n = min(2, self.tiles - 2 * k)
                        dve.wait_ge(self.sem("v_hi"), t.at("v_hi") + 1)
                        minus(v_lo[:, 2 * k:2 * k + n, :].rearrange("p t n -> p (t n)"),
                              banks[:, 5 + t.local("t_full") % 2, 0:256 * n],
                              v_hi[:, 2 * k:2 * k + n, :].rearrange("p t n -> p (t n)")
                              ).then_inc(self.sem("v_lo"), 1)
                    elif kind == "MAX":
                        _, p, half = e
                        slot = 2 * (p % 2) + half
                        for m, (b0, b1) in enumerate(self.maxima):
                            if m == 0:
                                dve.wait_ge(self.sem("s_part"), t.at("s_part"))
                            elif m == 1:
                                dve.wait_ge(self.sem("s_full"), t.at("s_full"))
                            nc.vector.tensor_reduce(stat[:, slot, 5 + m:6 + m], banks[:, b0:b1, 0:self.cuts[b0]],
                                                    AX.XY, ALU.max).then_inc(self.sem("max_step"), 1)
                        dve.wait_ge(self.sem("max_step"), t.at("max_step") + len(self.maxima))
                        nc.vector.tensor_reduce(stat[:, slot, 8:9], stat[:, slot, 5:5 + len(self.maxima)], AX.X,
                                                ALU.max, negate=True).then_inc(self.sem("neg_max"), 1)
                    elif kind == "T":
                        n, w = t.local("T"), 256 * min(2, self.tiles - 2 * e[2])
                        dve.wait_ge(self.sem("p_hi"), t.at("p_hi") + 1)
                        minus(pt_lo[:, n % 2, 0:w], banks[:, 5 + t.local("t_full") % 2, 0:w],
                              pt_hi[:, n % 2, 0:w]).then_inc(self.sem("p_lo"), 1)
                    elif kind == "RD":
                        p = e[1]
                        dve.wait_ge(self.sem("exps"), self.pair_exps(t))
                        nc.vector.tensor_reduce(inv[:, 0:2], stat[:, 2 * (p % 2):2 * (p % 2) + 2, 0:self.nb], AX.X,
                                                ALU.add).then_inc(self.sem("rd_step"), 1)
                        dve.wait_ge(self.sem("rd_step"), t.at("rd_step") + 1)
                        nc.vector.reciprocal(inv[:, 2:4], inv[:, 0:2]).then_inc(self.sem("rd_step"), 1)
                        dve.wait_ge(self.sem("rd_step"), t.at("rd_step") + 2)
                        for half in range(2):
                            ins = nc.vector.tensor_scalar(diag[:, half, :], ident, inv[:, 2 + half:3 + half], None,
                                                          ALU.mult)
                        ins.then_inc(self.sem("diag"), 1)
                    elif kind == "NORM":
                        p, n = e[1], t.local("NORM")
                        dst = heads[:, 2 * (p % 4):2 * (p % 4) + 2, :].rearrange("p h n -> p (h n)")
                        dve.wait_ge(self.sem("r_row"), t.at("r_row") + 1)
                        dve.wait_ge(self.sem("pv"), t.at("pv"))
                        ins = nc.vector.tensor_tensor(dst, banks[:, PV_BANK, (p % 2) * 256:(p % 2) * 256 + 256],
                                                      inv_row[:], ALU.mult)
                        if self.layer == 1:
                            kv = n // (2 * self.kv_groups)
                            ins.then_inc(self.sem("scaled"), 1)
                            dve.wait_ge(self.sem("scaled"), n + 1)
                            ins = nc.vector.tensor_scalar(dst, dst, bias_v[:, kv:kv + 1], None, ALU.add)
                        ins.then_inc(self.sem("heads_out"), 1)
                    elif kind == "WO":
                        dve.wait_ge(self.sem("wo_full"), t.at("wo_full") + 1)
                        nc.vector.tensor_tensor(x[:], x[:], banks[:, PV_BANK, :], ALU.add).then_inc(self.sem("x_sum"), 1)
                        last = t.local("WO") + 1 == 4 * self.turns * self.kv_groups // 4
                        if last or self.turns:
                            dve.wait_ge(self.sem("x_sum"), t.at("x_sum") + 1)

                self.walk(visit)

        stat = att[:].rearrange("p a b n -> p (a b) n")
        cross = [Cross(0)]
        cross.append(Cross(1, cross[0]))

        MLA_SCALE = P ** -0.5 * (0.1 * math.log(128.0) + 1.0) ** 2
        QUADS = NHEAD // 4
        m_pT = m_wqb[:].rearrange("p (h n) -> p h n", h=NHEAD)
        m_out = m_wkvb[:, 0:4096].rearrange("p (h n) -> p h n", h=NHEAD)
        m_kv_w = m_wkvb[0:32, :].rearrange("p (h n) -> p h n", h=NHEAD)
        cos = const[:, C_COS:C_COS + 32]
        sin = const[:, C_SIN:C_SIN + 32]

        def per_head(ap, n, w):
            return ap.unsqueeze(1).broadcast_to([P, n, w])

        def per_column(ap, n, w):
            return ap.unsqueeze(2).broadcast_to([P, n, w])

        def quad(t, n):
            return t[:, 4 * n:4 * n + 4, :].rearrange("p h n -> p (h n)")

        def mla_sync(sp):
            sp.wait_ge(cross[0].sem("x_sum"), 4)
            sp.dma_start(m_wa[:], a["m_wa"].rearrange("(c p) n -> p c n", p=P)).then_inc(sem("m_wa_in"), 16)
            sp.dma_start(m_lnw[:, 0:1], a["m_lnq"]).then_inc(sem("m_lnw_in"), 16)
            sp.dma_start(m_lnw[0:32, 1:2], a["m_lnkv"]).then_inc(sem("m_lnw_in"), 16)
            sp.dma_start(m_wqb[:], a["m_wqb"]).then_inc(sem("m_wqb_in"), 16)
            sp.dma_start(m_wkvb[0:32, :], a["m_wkvb"]).then_inc(sem("m_wkvb_in"), 16)
            for n in range(16):
                if n >= 4:
                    sp.wait_ge(*reach("m_wo_used", n - 3))
                sp.dma_start(m_ring[:, n % 4, :], a["m_wo"][2 * n * P:2 * (n + 1) * P, :]
                             .rearrange("(c p) n -> p c n", p=P)).then_inc(sem(f"m_wo_in{n % 4}"), 16)

        def mla_pe(pe):
            pe.wait_ge(*reach("m_wa_in", 16))
            for c in range(DC):
                mm = pe.matmul(banks[:, 0, 0:224], xlnT[:, c, :], m_wa[:, c, :], start=(c == 0), stop=(c == 3))
            mm.then_inc(sem("m_latent"), 1)
            pe.wait_ge(*reach("m_a_ready", 1))
            for c in range(3):
                mm = pe.transpose(banks[:, 1, c * P:(c + 1) * P], m_a[:, c * P:(c + 1) * P], ident)
            mm.then_inc(sem("m_aT_full"), 1)
            pe.wait_ge(*reach("m_aT_ready", 1))
            pe.wait_ge(*reach("m_wqb_in", 16))
            pe.wait_ge(*reach("m_wkvb_in", 16))
            for n in range(QUADS):
                if n >= 2:
                    pe.wait_ge(*reach("m_q_ready", n - 1))
                    pe.wait_ge(*reach("m_nope", n - 1))
                    pe.wait_ge(*reach("m_kT_ready", n - 1))
                    pe.wait_ge(*reach("m_v_ready", n - 1))
                pe.matmul(banks[:, 2 + n % 2, :], m_aT[:, 0, :], m_wqb[:, n * 512:(n + 1) * 512],
                          start=True, stop=True).then_inc(sem("m_q_full"), 1)
                for h in range(4):
                    mm = pe.matmul(banks[0:64, 4 + n % 2, h * P:(h + 1) * P], m_kv_w[:, 4 * n + h, 0:64],
                                   m_aT[0:32, 1, :], start=True, stop=True)
                mm.then_inc(sem("m_k_full"), 1)
                pe.matmul(banks[:, 6 + n % 2, :], m_aT[0:32, 1, :], m_kv_w[:, 4 * n:4 * n + 4, 64:192],
                          start=True, stop=True).then_inc(sem("m_v_full"), 1)
            for n in range(QUADS):
                pe.wait_ge(*reach("m_q_ready", n + 1 if n < QUADS - 2 else QUADS))
                pe.wait_ge(*reach("m_nope", n + 1))
                if n >= 2:
                    pe.wait_ge(*reach("m_qT_ready", n - 1))
                elif n == 0:
                    pe.wait_ge(*reach("m_q_ready", QUADS))
                for h in range(4):
                    mm = pe.transpose(banks[:, 2 + n % 2, h * P:(h + 1) * P], m_q[:, 4 * n + h, :], ident)
                mm.then_inc(sem("m_qT_full"), 1)
            pe.wait_ge(*reach("m_kT_ready", QUADS))
            pe.wait_ge(*reach("m_kT_rotary", 1))
            for n in range(QUADS):
                pe.wait_ge(*reach("m_qT_ready", n + 1))
                if n >= 2:
                    pe.wait_ge(*reach("m_masked", n - 1))
                for h in range(4):
                    mm = pe.matmul(banks[:, 4 + n % 2, h * P:(h + 1) * P], m_qT[:, 4 * n + h, :],
                                   m_kT[:, 4 * n + h, :], start=True, stop=True)
                mm.then_inc(sem("m_s_full"), 1)
            pe.wait_ge(*reach("m_v_ready", QUADS))
            for n in range(QUADS):
                pe.wait_ge(*reach("m_probs", n + 1))
                if n >= 2:
                    pe.wait_ge(*reach("m_pT_ready", n - 1))
                for h in range(4):
                    mm = pe.transpose(banks[:, 6 + n % 2, h * P:(h + 1) * P], m_q[:, 4 * n + h, :], ident)
                mm.then_inc(sem("m_pT_full"), 1)
            for n in range(QUADS):
                pe.wait_ge(*reach("m_pT_ready", n + 1))
                if n >= 2:
                    pe.wait_ge(*reach("m_out_ready", n - 1))
                for h in range(4):
                    mm = pe.matmul(banks[:, n % 2, h * P:(h + 1) * P], m_v[:, 4 * n + h, :],
                                   m_pT[:, 4 * n + h, :], start=True, stop=True)
                mm.then_inc(sem("m_out_full"), 1)
            pe.wait_ge(*reach("m_out_ready", QUADS))
            for n in range(16):
                pe.wait_ge(sem(f"m_wo_in{n % 4}"), 16 * (n // 4 + 1))
                for h in range(2):
                    mm = pe.matmul(banks[:, 2, :], m_out[:, 2 * n + h, :], m_ring[:, n % 4, h * 512:(h + 1) * 512],
                                   start=(n + h == 0), stop=(n == 15 and h == 1))
                mm.then_inc(sem("m_wo_used"), 1)

        def mla_act(act):
            act.wait_ge(*reach("m_latent", 1))
            nc.scalar.activation(m_rot[:, 0], banks[:, 0, 0:P], ACT.Square,
                                 accum_out=ln[:, 12:13]).then_inc(sem("m_sq"), 1)
            nc.scalar.activation(m_rot[:, 1, 0, :], banks[:, 0, P:P + 32], ACT.Square,
                                 accum_out=ln[:, 13:14]).then_inc(sem("m_sq"), 1)
            rsqrt_act(act, "m_var", 1, ln[:, 14:16], ln[:, 16:18])
            act.wait_ge(*reach("m_aT_full", 1))
            act.wait_ge(*reach("m_lnw_in", 32))
            nc.scalar.activation(m_aT[:, 0, :], banks[:, 1, 0:P], ACT.Copy, scale=m_lnw[:, 0:1])
            nc.scalar.activation(m_aT[0:32, 1, :], banks[0:32, 1, P:2 * P], ACT.Copy, scale=m_lnw[0:32, 1:2])
            nc.scalar.activation(m_aT[64:128, 2, :], banks[64:128, 1, 2 * P:3 * P],
                                 ACT.Copy).then_inc(sem("m_aT_ready"), 1)
            for n in range(QUADS):
                act.wait_ge(*reach("m_q_full", n + 1))
                nc.scalar.activation(m_q[:, 4 * n:4 * n + 4, 0:64],
                                     banks[:, 2 + n % 2, :].rearrange("p (h n) -> p h n", h=4)[:, :, 0:64],
                                     ACT.Copy).then_inc(sem("m_nope"), 1)
                act.wait_ge(*reach("m_k_full", n + 1))
                nc.scalar.activation(quad(m_kT, n)[0:64, :], banks[0:64, 4 + n % 2, :],
                                     ACT.Copy).then_inc(sem("m_kT_ready"), 1)
                act.wait_ge(*reach("m_v_full", n + 1))
                nc.scalar.activation(quad(m_v, n), banks[:, 6 + n % 2, :], ACT.Copy).then_inc(sem("m_v_ready"), 1)
            for n in range(QUADS):
                act.wait_ge(*reach("m_qT_full", n + 1))
                nc.scalar.activation(quad(m_qT, n), banks[:, 2 + n % 2, :], ACT.Copy).then_inc(sem("m_qT_ready"), 1)
            for n in range(QUADS):
                act.wait_ge(*reach("m_neg_max", n + 1))
                for h in range(4 * n, 4 * n + 4):
                    ins = nc.scalar.activation(m_q[:, h, :], m_q[:, h, :], ACT.Exp, bias=m_st[:, 0, h:h + 1],
                                               accum_out=m_st[:, 1, h:h + 1])
                    ins.then_inc(sem("m_exps"), 1)
            for n in range(QUADS):
                act.wait_ge(*reach("m_pT_full", n + 1))
                nc.scalar.activation(quad(m_pT, n), banks[:, 6 + n % 2, :], ACT.Copy).then_inc(sem("m_pT_ready"), 1)

        def rotate(dve, even, odd, first, second, heads, count):
            t = [m_rot[:, k, 0:heads, :] for k in range(4)]
            for k, (v, w) in enumerate(((even, cos), (odd, sin), (odd, cos), (even, sin))):
                ins = nc.vector.tensor_tensor(t[k], v, per_head(w, heads, 32), ALU.mult)
            ins.then_inc(sem("m_turned"), 1)
            dve.wait_ge(*reach("m_turned", count + 1))
            nc.vector.tensor_tensor(first, t[0], t[1], ALU.subtract)
            return nc.vector.tensor_tensor(second, t[2], t[3], ALU.add)

        def mla_dve(dve):
            nc.vector.memset(m_a[:], 0.0).then_inc(sem("m_a_clear"), 1)
            dve.wait_ge(*reach("m_sq", 2))
            nc.vector.tensor_scalar(ln[:, 14:15], ln[:, 12:13], 1.0 / 128, RMS_EPS, ALU.mult, ALU.add)
            nc.vector.tensor_scalar(ln[:, 15:16], ln[:, 13:14], 1.0 / 32, RMS_EPS, ALU.mult,
                                    ALU.add).then_inc(sem("m_var"), 1)
            dve.wait_ge(*reach("m_var", 1))
            rsqrt_dve(dve, ln[:, 14:16], ln[:, 16:18], ln[:, 18:20])
            dve.wait_ge(*reach("m_a_clear", 1))
            nc.vector.tensor_scalar(m_a[:, 0:P], banks[:, 0, 0:P], ln[:, 16:17], None, ALU.mult)
            nc.vector.tensor_scalar(m_a[:, P:P + 32], banks[:, 0, P:P + 32], ln[:, 17:18], None, ALU.mult)
            rotate(dve, banks[:, 0, 160:224:2].unsqueeze(1), banks[:, 0, 161:224:2].unsqueeze(1),
                   m_a[:, 320:352].unsqueeze(1), m_a[:, 352:384].unsqueeze(1), 1, 0).then_inc(sem("m_a_ready"), 1)
            dve.wait_ge(*reach("m_a_ready", 1))
            for n in range(QUADS):
                dve.wait_ge(*reach("m_nope", n + 1))
                if n:
                    dve.wait_ge(*reach("m_q_ready", n))
                pe_part = banks[:, 2 + n % 2, :].rearrange("p (h n) -> p h n", h=4)
                rotate(dve, pe_part[:, :, 64:128:2], pe_part[:, :, 65:128:2], m_q[:, 4 * n:4 * n + 4, 64:96],
                       m_q[:, 4 * n:4 * n + 4, 96:128], 4, n + 1).then_inc(sem("m_q_ready"), 1)

            def inverse(n):
                dve.wait_ge(*reach("m_exps", 4 * n + 4))
                nc.vector.reciprocal(m_st[:, 2, 4 * n:4 * n + 4],
                                     m_st[:, 1, 4 * n:4 * n + 4]).then_inc(sem("m_inv"), 1)
                dve.wait_ge(*reach("m_inv", n + 1))
                nc.vector.tensor_tensor(m_q[:, 4 * n:4 * n + 4, :], m_q[:, 4 * n:4 * n + 4, :],
                                        per_column(m_st[:, 2, 4 * n:4 * n + 4], 4, P),
                                        ALU.mult).then_inc(sem("m_probs"), 1)

            for n in range(QUADS):
                dve.wait_ge(*reach("m_s_full", n + 1))
                nc.vector.scalar_tensor_tensor(
                    m_q[:, 4 * n:4 * n + 4, :], banks[:, 4 + n % 2, :].rearrange("p (h n) -> p h n", h=4), MLA_SCALE,
                    per_head(const[:, C_CAUSAL:C_CAUSAL + P], 4, P), ALU.mult, ALU.add).then_inc(sem("m_masked"), 1)
                dve.wait_ge(*reach("m_masked", n + 1))
                nc.vector.tensor_reduce(m_st[:, 0, 4 * n:4 * n + 4], m_q[:, 4 * n:4 * n + 4, :], AX.X, ALU.max,
                                        negate=True).then_inc(sem("m_neg_max"), 1)
                if n:
                    inverse(n - 1)
            inverse(QUADS - 1)
            for n in range(QUADS):
                dve.wait_ge(*reach("m_out_full", n + 1))
                nc.vector.tensor_copy(quad(m_out, n), banks[:, n % 2, :]).then_inc(sem("m_out_ready"), 1)
            dve.wait_ge(*reach("m_wo_used", 16))
            nc.vector.tensor_tensor(x[:], x[:], banks[:, 2, :], ALU.add).then_inc(sem("m_x_sum"), 1)
            dve.wait_ge(*reach("m_x_sum", 1))

        def mla_pool(pool):
            pool.wait_ge(*reach("m_aT_ready", 1))
            nc.gpsimd.tensor_copy(m_kT[64:128, :, :],
                                  m_aT[64:128, 2, :].unsqueeze(1).broadcast_to([64, NHEAD, P])
                                  ).then_inc(sem("m_kT_rotary"), 1)

        EXPERT = (ACT.Tanh, ACT.Gelu, ACT.Silu)
        ratio_row = e_row[0:1, 8 + 3 * D:8 + 3 * D + P]

        def moe_sync(sp):
            sp.wait_ge(*reach("m_x_sum", 1))
            sp.dma_start(e_gw[:, :, 0:3], a["e_gw"][0:D, :].rearrange("(c p) n -> p c n", p=P)
                         ).then_inc(sem("e_small_in"), 16)
            sp.dma_start(e_row[0:1, 0:3], a["e_gw"][D:D + 1, :]).then_inc(sem("e_small_in"), 16)
            sp.dma_start(e_row[0:1, 4:7], a["e_gb"]).then_inc(sem("e_small_in"), 16)
            sp.dma_start(e_row[0:1, 8:8 + 3 * D], a["e_b2"]).then_inc(sem("e_small_in"), 16)
            sp.dma_start(e_b1[:], a["e_b1"]).then_inc(sem("e_small_in"), 16)
            for e in range(3):
                sp.dma_start(e_w1[:, e], a["e_w1"][e].rearrange("(c p) n -> p c n", p=P)).then_inc(sem(f"e_w1_in{e}"), 16)
            for e in range(3):
                sp.dma_start(e_w2[:, e], a["e_w2"][e].rearrange("(c p) n -> p c n", p=P)).then_inc(sem(f"e_w2_in{e}"), 16)

        def moe_pe(pe):
            for e in range(3):
                pe.wait_ge(sem(f"e_w1_in{e}"), 16)
                for f in range(DC):
                    for c in range(DC):
                        mm = pe.matmul(banks[:, 3 + e, f * P:(f + 1) * P], e_w1[:, e, c, f * P:(f + 1) * P],
                                       xlnT[:, c, :], start=(c == 0), stop=(c == 3))
                mm.then_inc(sem("e_pre"), 1)
                if e == 0:
                    pe.wait_ge(*reach("e_weighed", 1))
                    pe.matmul(banks[:, 0, 0:2], ones, e_s[:, 2:4], start=True, stop=True).then_inc(sem("e_means"), 1)
            pe.wait_ge(*reach("e_small_in", 80))
            for c in range(DC):
                pe.matmul(banks[:, 1, 0:3], xlnT[:, c, :], e_gw[:, c, 0:3], start=(c == 0), stop=False)
            pe.matmul(banks[:, 1, 0:3], ones[0:1, :], e_row[0:1, 4:7], start=False, stop=False)
            pe.wait_ge(*reach("e_ratio", 1))
            pe.matmul(banks[:, 1, 0:3], ratio_row, e_row[0:1, 0:3], start=False, stop=True).then_inc(sem("e_logits"), 1)
            for e in range(3):
                pe.wait_ge(*reach("e_hidden", 4 * (e + 1)))
                pe.wait_ge(sem(f"e_w2_in{e}"), 16)
                bank = (6, 7, 3)[e]
                for f in range(DC):
                    pe.matmul(banks[:, bank, :], e_act[:, e, f, :], e_w2[:, e, f, :], start=(f == 0), stop=False)
                pe.matmul(banks[:, bank, :], ones[0:1, :], e_row[0:1, 8 + e * D:8 + (e + 1) * D],
                          start=False, stop=True).then_inc(sem("e_out"), 1)
                if e == 0:
                    pe.wait_ge(*reach("e_choice", 1))
                    pe.matmul(banks[:, 2, 0:6], ones[0:1, :], e_s[0:1, 40:46], start=True,
                              stop=True).then_inc(sem("e_chosen"), 1)

        def moe_act(act):
            act.wait_ge(*reach("xln_ready", 3))
            nc.scalar.activation(e_act[:, 0].rearrange("p c n -> p (c n)"), xln[:], ACT.Abs,
                                 accum_out=e_s[:, 0:1]).then_inc(sem("e_abs"), 1)
            ln_act_tail(act, 2)
            act.wait_ge(*reach("e_small_in", 80))
            act.wait_ge(*reach("e_abs", 1))

            def hidden(e):
                act.wait_ge(*reach("e_pre", e + 1))
                for f in range(DC):
                    nc.scalar.activation(e_act[:, e, f, :], banks[:, 3 + e, f * P:(f + 1) * P], EXPERT[e],
                                         bias=e_b1[:, 4 * e + f:4 * e + f + 1]).then_inc(sem("e_hidden"), 1)

            hidden(0)
            act.wait_ge(*reach("e_neg_max", 1))
            nc.scalar.activation(e_s[:, 8:11], banks[:, 1, 0:3], ACT.Exp, bias=e_s[:, 5:6],
                                 accum_out=e_s[:, 6:7]).then_inc(sem("e_exp"), 1)
            hidden(1)
            hidden(2)

        def moe_dve(dve):
            def then(ins):
                own_steps[0] += 1
                ins.then_inc(sem("dve_own"), 1)
                dve.wait_ge(*reach("dve_own", own_steps[0]))

            def tt(o, i0, i1, op):
                return nc.vector.tensor_tensor(e_s[:, o:o + 1], e_s[:, i0:i0 + 1], e_s[:, i1:i1 + 1], op)

            dve.wait_ge(*reach("e_abs", 1))
            nc.vector.tensor_scalar(e_s[:, 2:4], const[:, C_MEANS:C_MEANS + 2], e_s[:, 0:1], None,
                                    ALU.mult).then_inc(sem("e_weighed"), 1)
            dve.wait_ge(*reach("e_means", 1))
            then(nc.vector.tensor_scalar(e_s[:, 4:5], banks[:, 0, 1:2], 1e-8, None, ALU.add))
            then(nc.vector.reciprocal(e_s[:, 4:5], e_s[:, 4:5]))
            then(nc.vector.tensor_tensor(e_s[:, 4:5], e_s[:, 4:5], banks[:, 0, 0:1], ALU.mult))
            nc.vector.tensor_scalar(ratio_row, ones[0:1, :], e_s[0:1, 4:5], None, ALU.mult).then_inc(sem("e_ratio"), 1)
            dve.wait_ge(*reach("e_logits", 1))
            nc.vector.tensor_reduce(e_s[:, 5:6], banks[:, 1, 0:3], AX.X, ALU.max, negate=True
                                    ).then_inc(sem("e_neg_max"), 1)
            dve.wait_ge(*reach("e_exp", 1))
            then(nc.vector.reciprocal(e_s[:, 7:8], e_s[:, 6:7]))
            then(nc.vector.tensor_scalar(e_s[:, 12:15], e_s[:, 8:11], e_s[:, 7:8], None, ALU.mult))
            tt(20, 13, 12, ALU.is_gt), tt(21, 14, 12, ALU.is_gt)
            tt(22, 12, 13, ALU.is_ge), tt(23, 14, 13, ALU.is_gt)
            tt(24, 12, 14, ALU.is_ge)
            then(tt(25, 13, 14, ALU.is_ge))
            then(nc.vector.tensor_tensor(e_s[:, 28:31], e_s[:, 20:25:2], e_s[:, 21:26:2], ALU.add))
            nc.vector.tensor_scalar(e_s[:, 40:43], e_s[:, 28:31], 0.0, None, ALU.is_equal)
            nc.vector.tensor_scalar(e_s[:, 43:46], e_s[:, 28:31], 1.0, None, ALU.is_equal).then_inc(sem("e_choice"), 1)
            tt(16, 12, 13, ALU.max)
            then(tt(17, 12, 13, ALU.min))
            tt(32, 16, 14, ALU.max)
            then(tt(18, 16, 14, ALU.min))
            then(tt(33, 17, 18, ALU.max))
            then(tt(34, 32, 33, ALU.add))
            then(nc.vector.tensor_scalar(e_s[:, 34:35], e_s[:, 34:35], 1e-8, None, ALU.add))
            then(nc.vector.reciprocal(e_s[:, 35:36], e_s[:, 34:35]))
            then(nc.vector.tensor_scalar(e_s[:, 36:38], e_s[:, 32:34], e_s[:, 35:36], None, ALU.mult))
            dve.wait_ge(*reach("e_chosen", 1))
            then(nc.vector.tensor_scalar(e_s[:, 48:51], banks[:, 2, 0:3], e_s[:, 36:37], None, ALU.mult))
            then(nc.vector.scalar_tensor_tensor(e_s[:, 52:55], banks[:, 2, 3:6], e_s[:, 37:38], e_s[:, 48:51],
                                                ALU.mult, ALU.add))
            for e in range(3):
                dve.wait_ge(*reach("e_out", e + 1))
                ins = nc.vector.scalar_tensor_tensor(x[:], banks[:, (6, 7, 3)[e], :], e_s[:, 52 + e:53 + e], x[:],
                                                     ALU.mult, ALU.add)
                if e < 2:
                    then(ins)
            ins.then_inc(sem("e_x_sum"), 1)
            dve.wait_ge(*reach("e_x_sum", 1))

        s_items = [("dt", 18432, 128)] + [("conv", 16384 + 512 * m, 512) for m in range(4)]
        for b_ in range(16):
            s_items += [("conv", 8192 + 512 * b_, 512), ("gate", 512 * b_, 512)]
        n_in = len(s_items)
        upto = const[:, C_UPTO:C_UPTO + P]
        after = const[:, C_AFTER:C_AFTER + P]

        def ssm_sync(sp):
            sp.wait_ge(cross[1].sem("x_sum"), 8)
            for k, name in enumerate(("s_dtb", "s_alog", "s_D")):
                sp.dma_start(s_row[0:1, k * P:(k + 1) * P], a[name]).then_inc(sem("s_rows_in"), 16)
            sp.dma_start(s_cw[:], a["s_cw"]).then_inc(sem("s_cw_in"), 16)
            sp.dma_start(s_cbias[:], a["s_cb"]).then_inc(sem("s_cw_in"), 16)
            sp.dma_start(s_nw[:], a["s_nw"]).then_inc(sem("s_nw_in"), 16)
            for n in range(n_in + 16):
                if n >= NSLOT:
                    sp.wait_ge(*reach("s_used", n - NSLOT + 1))
                dst = s_w[:, n % NSLOT]
                if n < n_in:
                    _, col, w = s_items[n]
                    dst, src = dst[:, :, 0:w], a["s_in"][:, col:col + w]
                else:
                    src = a["s_out"][(n - n_in) * 512:(n - n_in + 1) * 512, :]
                sp.dma_start(dst, src.rearrange("(c p) n -> p c n", p=P)).then_inc(sem(f"s_w_in{n % NSLOT}"), 16)

        def ssm_pe(pe):
            at = [0]

            def weights():
                n = at[0]
                at[0] += 1
                pe.wait_ge(sem(f"s_w_in{n % NSLOT}"), 16 * (n // NSLOT + 1))
                return s_w[:, n % NSLOT]

            w = weights()
            for c in range(DC):
                mm = pe.matmul(banks[:, 0, 0:P], xlnT[:, c, :], w[:, c, 0:P], start=(c == 0), stop=False)
            mm.then_inc(sem("s_used"), 1)
            pe.wait_ge(*reach("s_rows_in", 48))
            pe.matmul(banks[:, 0, 0:P], ones[0:1, :], s_row[0:1, 0:P], start=False, stop=True)
            pe.matmul(banks[:, 0, P:3 * P], ones[0:1, :], s_row[0:1, P:3 * P], start=True,
                      stop=True).then_inc(sem("s_dt_full"), 1)

            def conv_proj(m):
                w = weights()
                if m >= 2:
                    pe.wait_ge(*reach("s_conv_done", m - 1))
                for t in range(4):
                    for c in range(DC):
                        mm = pe.matmul(banks[:, 3 + m % 2, t * P:(t + 1) * P], w[:, c, t * P:(t + 1) * P],
                                       xlnT[:, c, :], start=(c == 0), stop=(c == 3))
                mm.then_inc(sem("s_used"), 1)

            for m in range(4):
                conv_proj(m)
                for n in range(8 * m, 8 * m + 8):
                    pe.wait_ge(*reach("s_seg_in", n + 1))
                    if n >= 2:
                        pe.wait_ge(*reach("s_decay_ready", n - 1))
                    pe.matmul(banks[:, 1 + n % 2, :], after, s_seg[:, n % 2].rearrange("p h n -> p (h n)"),
                              start=True, stop=True).then_inc(sem("s_seg_full"), 1)
            pe.wait_ge(*reach("s_conv_act", 4))
            for q in range(2):
                for g in range(4 * q, 4 * q + 4):
                    mm = pe.matmul(banks[:, 5 + q, (g % 4) * P:(g % 4 + 1) * P], s_bT[:, g, :], s_cT[:, g, :],
                                   start=True, stop=True)
                mm.then_inc(sem("s_cb_full"), 1)

            def head_block(b):
                pe.wait_ge(*reach("s_conv_act", b + 5))
                if b == 0:
                    pe.wait_ge(*reach("s_cb_ready", 2))
                else:
                    pe.wait_ge(*reach("s_hs_ready", b))
                for t in range(4):
                    mm = pe.transpose(banks[:, 5, t * P:(t + 1) * P], s_chan[:, b % 2, t, :], ident)
                mm.then_inc(sem("s_hs_full"), 1)

            def mix_block(b):
                pe.wait_ge(*reach("s_mixed", b + 1))
                pe.wait_ge(*reach("s_hs_ready", b + 1))
                if b:
                    pe.wait_ge(*reach("s_y_read", b))
                for j in range(8):
                    mm = pe.matmul(banks[:, 7, 64 * j:64 * j + 64], s_mix[:, b % 2, j, :],
                                   s_hs[:, b % 2, 64 * j:64 * j + 64], start=True, stop=True)
                mm.then_inc(sem("s_y_full"), 1)

            for b in range(16):
                conv_proj(4 + b)
                w = weights()
                if b:
                    pe.wait_ge(*reach("s_gate_ready", b))
                else:
                    pe.wait_ge(*reach("s_cb_ready", 2))
                for c in range(DC):
                    mm = pe.matmul(banks[:, 6, :], xlnT[:, c, :], w[:, c, :], start=(c == 0), stop=(c == 3))
                mm.then_inc(sem("s_used"), 1)
                if b:
                    head_block(b - 1)
                    mix_block(b - 1)
            head_block(15)
            mix_block(15)
            for b in range(16):
                pe.wait_ge(*reach("s_scaled", b + 1))
                if b >= 2:
                    pe.wait_ge(*reach("s_gT_ready", b - 1))
                for t in range(4):
                    mm = pe.transpose(banks[:, 1 + b % 2, t * P:(t + 1) * P],
                                      s_g[:, (4 * b + t) * P:(4 * b + t + 1) * P], ident)
                mm.then_inc(sem("s_gT_full"), 1)
                if b:
                    out_block(pe, b - 1, weights())
            out_block(pe, 15, weights())

        def out_block(pe, b, w):
            pe.wait_ge(*reach("s_gT_ready", b + 1))
            for t in range(4):
                mm = pe.matmul(banks[:, 0, :], s_chan[:, b % 2, t, :], w[:, t, :], start=(b + t == 0),
                               stop=(b == 15 and t == 3))
            mm.then_inc(sem("s_used"), 1)

        used_by_conv = [k + 1 for k, (kind, _, _) in enumerate(s_items) if kind == "conv"]
        used_by_gate = [k + 1 for k, (kind, _, _) in enumerate(s_items) if kind == "gate"]
        conv_tile = [64, 68, 72, 76] + [4 * b_ for b_ in range(16)]

        def ssm_act(act):
            act.wait_ge(*reach("s_dt_full", 1))
            nc.scalar.activation(s_dt[:, 4, :], banks[:, 0, 0:P], ACT.Abs).then_inc(sem("s_dt_abs"), 1)
            act.wait_ge(*reach("s_dt_abs", 1))
            nc.scalar.activation(s_dt[:, 4, :], s_dt[:, 4, :], ACT.Exp, scale=-1.0).then_inc(sem("s_dt_exp"), 1)
            nc.scalar.activation(s_dt[:, 1, :], banks[:, 0, P:2 * P], ACT.Exp).then_inc(sem("s_a_exp"), 1)
            act.wait_ge(*reach("s_dt_u", 1))
            nc.scalar.activation(s_dt[:, 6, :], s_dt[:, 5, :], ACT.Ln).then_inc(sem("s_dt_ln"), 1)

            def conv_first(m):
                act.wait_ge(*reach("s_used", used_by_conv[m]))
                if m == 0:
                    act.wait_ge(*reach("s_cw_in", 32))
                if m >= 2:
                    act.wait_ge(*reach("s_conv_act", m - 1))
                for t in range(4):
                    k = conv_tile[m] + t
                    ins = nc.scalar.activation(s_conv[:, m % 2, t, :], banks[:, 3 + m % 2, t * P:(t + 1) * P],
                                               ACT.Identity, bias=s_cbias[:, k:k + 1], scale=s_cw[:, k, 3:4])
                ins.then_inc(sem("s_conv_first"), 1)

            def conv_tanh(m):
                act.wait_ge(*reach("s_conv_done", m + 1))
                if m >= 2:
                    act.wait_ge(*reach("s_conv_act", m - 1))
                nc.scalar.activation(s_tanh[:, m % 2], s_conv[:, m % 2], ACT.Tanh, scale=0.5
                                     ).then_inc(sem("s_conv_tanh"), 1)

            for m in range(4):
                conv_first(m)
                for n in range(8 * m, 8 * m + 8):
                    act.wait_ge(*reach("s_seg_full", n + 1))
                    nc.scalar.activation(s_decay[:, 4 * n:4 * n + 4, :].rearrange("p h n -> p (h n)"),
                                         banks[:, 1 + n % 2, :], ACT.Exp).then_inc(sem("s_decay_ready"), 1)
                    if n % 8 == 3:
                        conv_tanh(m)

            def hs_copy(b):
                act.wait_ge(*reach("s_hs_full", b + 1))
                if b >= 2:
                    act.wait_ge(*reach("s_y_read", b - 1))
                nc.scalar.activation(s_hs[:, b % 2, :], banks[:, 5, :], ACT.Copy, scale=0.5
                                     ).then_inc(sem("s_hs_ready"), 1)

            def square(b):
                act.wait_ge(*reach("s_g_ready", b + 1))
                if b:
                    act.wait_ge(*reach("s_squares", b))
                nc.scalar.activation(s_sq[:], s_g[:, b * 512:(b + 1) * 512], ACT.Square,
                                     accum_out=s_var[:, 0, b:b + 1]).then_inc(sem("s_squares"), 1)

            for b in range(16):
                conv_first(4 + b)
                act.wait_ge(*reach("s_used", used_by_gate[b]))
                if b >= 2:
                    act.wait_ge(*reach("s_g_ready", b - 1))
                nc.scalar.activation(s_gate[:, b % 2, :], banks[:, 6, :], ACT.Tanh, scale=0.5
                                     ).then_inc(sem("s_gate_tanh"), 1)
                conv_tanh(4 + b)
                if b:
                    hs_copy(b - 1)
                    if b > 1:
                        square(b - 2)
            hs_copy(15)
            square(14)
            square(15)
            rsqrt_act(act, "s_var_ready", 1, s_var[:, 1, 0:8], s_var[:, 2, 0:8])
            act.wait_ge(*reach("s_nw_in", 16))
            for b in range(16):
                act.wait_ge(*reach("s_gT_full", b + 1))
                if b >= 2:
                    act.wait_ge(*reach("s_used", n_in + b - 1))
                for t in range(4):
                    ins = nc.scalar.activation(s_chan[:, b % 2, t, :], banks[:, 1 + b % 2, t * P:(t + 1) * P],
                                               ACT.Copy, scale=s_nw[:, 4 * b + t:4 * b + t + 1])
                ins.then_inc(sem("s_gT_ready"), 1)

        def ssm_dve(dve):
            def then(ins):
                own_steps[0] += 1
                ins.then_inc(sem("dve_own"), 1)
                dve.wait_ge(*reach("dve_own", own_steps[0]))

            d = s_dt
            dve.wait_ge(*reach("s_dt_exp", 1))
            nc.vector.tensor_scalar(d[:, 5, :], d[:, 4, :], 1.0, None, ALU.add).then_inc(sem("s_dt_u"), 1)
            dve.wait_ge(*reach("s_dt_u", 1))
            then(nc.vector.tensor_scalar(d[:, 7, :], d[:, 5, :], -1.0, None, ALU.add))
            then(nc.vector.tensor_scalar(d[:, 2, :], d[:, 7, :], 0.0, None, ALU.is_equal))
            then(nc.vector.tensor_tensor(d[:, 7, :], d[:, 7, :], d[:, 2, :], ALU.add))
            then(nc.vector.reciprocal(d[:, 7, :], d[:, 7, :]))
            dve.wait_ge(*reach("s_dt_ln", 1))
            then(nc.vector.tensor_tensor(d[:, 7, :], d[:, 7, :], d[:, 6, :], ALU.mult))
            then(nc.vector.tensor_tensor(d[:, 7, :], d[:, 7, :], d[:, 2, :], ALU.add))
            then(nc.vector.tensor_tensor(d[:, 7, :], d[:, 7, :], d[:, 4, :], ALU.mult))
            then(nc.vector.scalar_tensor_tensor(d[:, 0, :], banks[:, 0, 0:P], 0.0, d[:, 7, :], ALU.max, ALU.add))
            then(nc.vector.tensor_scalar(d[:, 0, :], d[:, 0, :], 100.0, 0.0, ALU.min, ALU.max))
            dve.wait_ge(*reach("s_a_exp", 1))
            then(nc.vector.scalar_tensor_tensor(d[:, 2, :], d[:, 0, :], -1.0, d[:, 1, :], ALU.mult, ALU.mult))
            then(nc.vector.tensor_copy(d[:, 3, :], banks[:, 0, 2 * P:3 * P]))

            def taps(m):
                for k in range(1, 4):
                    if k == 1:
                        dve.wait_ge(*reach("s_conv_first", m + 1))
                    else:
                        dve.wait_ge(*reach("s_tap", 2 * m + k - 1))
                    for t in range(4):
                        ins = nc.vector.scalar_tensor_tensor(
                            s_conv[:, m % 2, t, k:P], banks[:, 3 + m % 2, t * P:(t + 1) * P - k],
                            s_cw[:, conv_tile[m] + t, 3 - k:4 - k], s_conv[:, m % 2, t, k:P], ALU.mult, ALU.add)
                    ins.then_inc(sem("s_tap" if k < 3 else "s_conv_done"), 1)

            def silu(m):
                dve.wait_ge(*reach("s_conv_tanh", m + 1))
                dst = (s_bT[:, 4 * m:4 * m + 4, :] if m < 2 else s_cT[:, 4 * m - 8:4 * m - 4, :] if m < 4
                       else s_chan[:, m % 2])
                if m >= 6:
                    dve.wait_ge(*reach("s_hs_full", m - 5))
                nc.vector.scalar_tensor_tensor(dst.rearrange("p t n -> p (t n)"),
                                               s_tanh[:, m % 2].rearrange("p t n -> p (t n)"), 1.0,
                                               s_conv[:, m % 2].rearrange("p t n -> p (t n)"), ALU.add,
                                               ALU.mult).then_inc(sem("s_conv_act"), 1)

            for m in range(4):
                for n in range(8 * m, 8 * m + 8):
                    if n >= 2:
                        dve.wait_ge(*reach("s_seg_full", n - 1))
                    nc.vector.tensor_tensor(s_seg[:, n % 2], per_head(upto, 4, P),
                                            per_column(d[:, 2, 4 * n:4 * n + 4], 4, P),
                                            ALU.mult).then_inc(sem("s_seg_in"), 1)
                    if n % 8 == 1:
                        taps(m)
                    if n % 8 == 6:
                        silu(m)
            for q in range(2):
                dve.wait_ge(*reach("s_cb_full", q + 1))
                nc.vector.scalar_tensor_tensor(
                    s_cb[:, 4 * q:4 * q + 4, :], banks[:, 5 + q, :].rearrange("p (g n) -> p g n", g=4), 0.25,
                    per_head(upto, 4, P), ALU.mult, ALU.mult).then_inc(sem("s_cb_ready"), 1)
            dve.wait_ge(*reach("s_cb_ready", 2))
            dve.wait_ge(*reach("s_decay_ready", 32))

            def mix(b):
                if b >= 2:
                    dve.wait_ge(*reach("s_y_full", b - 1))
                for j in range(8):
                    h = 8 * b + j
                    ins = nc.vector.scalar_tensor_tensor(s_mix[:, b % 2, j, :], s_decay[:, h, :], d[:, 0, h:h + 1],
                                                         s_cb[:, b // 2, :], ALU.mult, ALU.mult)
                ins.then_inc(sem("s_mixed"), 1)

            def finish(b):
                dve.wait_ge(*reach("s_hs_ready", b + 1))
                nc.vector.tensor_tensor(s_y[:, b % 2, :].rearrange("p (h n) -> p h n", h=8),
                                        s_hs[:, b % 2, :].rearrange("p (h n) -> p h n", h=8),
                                        per_column(d[:, 3, 8 * b:8 * b + 8], 8, 64), ALU.mult
                                        ).then_inc(sem("s_skip"), 1)
                dve.wait_ge(*reach("s_skip", b + 1))
                dve.wait_ge(*reach("s_y_full", b + 1))
                nc.vector.tensor_tensor(s_y[:, b % 2, :], s_y[:, b % 2, :], banks[:, 7, :], ALU.add
                                        ).then_inc(sem("s_y_read"), 1)
                dve.wait_ge(*reach("s_y_read", b + 1))
                nc.vector.scalar_tensor_tensor(s_g[:, b * 512:(b + 1) * 512], s_y[:, b % 2, :], 0.5,
                                               s_gate[:, b % 2, :], ALU.mult, ALU.mult).then_inc(sem("s_g_ready"), 1)

            for b in range(16):
                mix(b)
                taps(4 + b)
                dve.wait_ge(*reach("s_gate_tanh", b + 1))
                nc.vector.scalar_tensor_tensor(s_gate[:, b % 2, :], s_gate[:, b % 2, :], 1.0, banks[:, 6, :],
                                               ALU.add, ALU.mult).then_inc(sem("s_gate_ready"), 1)
                silu(4 + b)
                if b:
                    finish(b - 1)
            finish(15)
            dve.wait_ge(*reach("s_squares", 16))
            then(nc.vector.tensor_tensor(s_var[:, 1, 0:8], s_var[:, 0, 0:16:2], s_var[:, 0, 1:16:2], ALU.add))
            nc.vector.tensor_scalar(s_var[:, 1, 0:8], s_var[:, 1, 0:8], 1.0 / 1024, EPS, ALU.mult, ALU.add
                                    ).then_inc(sem("s_var_ready"), 1)
            rsqrt_dve(dve, s_var[:, 1, 0:8], s_var[:, 2, 0:8], s_var[:, 3, 0:8])
            for b in range(16):
                nc.vector.tensor_scalar(s_g[:, b * 512:(b + 1) * 512], s_g[:, b * 512:(b + 1) * 512],
                                        s_var[:, 2, b // 2:b // 2 + 1], None, ALU.mult).then_inc(sem("s_scaled"), 1)
            dve.wait_ge(*reach("s_used", n_in + 16))
            nc.vector.tensor_tensor(x[:], x[:], banks[:, 0, :], ALU.add).then_inc(sem("s_x_sum"), 1)
            dve.wait_ge(*reach("s_x_sum", 1))

        def ffn_sync(sp):
            sp.wait_ge(*reach("s_x_sum", 1))
            sp.dma_start(f_gw[:], a["f_gw"].rearrange("(c p) n -> p c n", p=P)).then_inc(sem("f_gw_in"), 16)
            sp.dma_start(f_w[:], a["f_w"].rearrange("(c p) n -> p c n", p=P)).then_inc(sem("f_w_in"), 16)
            sp.dma_start(f_scale[:, 0, :], a["f_in"]).then_inc(sem("f_scale_in"), 16)
            sp.dma_start(f_scale[:, 1, :], a["f_out"]).then_inc(sem("f_scale_in"), 16)
            sp.dma_start(f_bias[:], a["f_b"].broadcast_to([P, D])).then_inc(sem("f_bias_in"), 16)

        def ffn_pe(pe):
            pe.wait_ge(*reach("f_gw_in", 16))
            for c in range(DC):
                mm = pe.matmul(banks[:, 0, 0:8], xlnT[:, c, :], f_gw[:, c, :], start=(c == 0), stop=(c == 3))
            mm.then_inc(sem("f_logits"), 1)
            pe.wait_ge(*reach("f_routing", 1))
            pe.transpose(banks[0:8, 1, 0:P], f_r[:, 8:16], ident).then_inc(sem("f_rT_full"), 1)
            pe.wait_ge(*reach("f_rT_ready", 1))
            pe.wait_ge(*reach("f_scale_in", 32))
            for k in range(2):
                pe.matmul(banks[:, 2 + k, :], f_rT[:], f_scale[:, k, :], start=True, stop=True
                          ).then_inc(sem("f_scales"), 1)
            pe.wait_ge(*reach("f_scaled", 1))
            for c in range(DC):
                mm = pe.transpose(banks[:, 4, c * P:(c + 1) * P], f_xs[:, c * P:(c + 1) * P], ident)
            mm.then_inc(sem("f_xT_full"), 1)
            pe.wait_ge(*reach("f_xT_ready", 1))
            for c in range(DC):
                mm = pe.matmul(banks[:, 5, :], f_xT[:, c, :], f_sign[:, c, :], start=(c == 0), stop=(c == 3))
            mm.then_inc(sem("f_out_full"), 1)

        def ffn_act(act):
            act.wait_ge(*reach("f_w_in", 16))
            nc.scalar.activation(f_sign[:], f_w[:], ACT.Sign).then_inc(sem("f_sign_ready"), 1)
            act.wait_ge(*reach("f_neg_max", 1))
            nc.scalar.activation(f_r[:, 0:8], banks[:, 0, 0:8], ACT.Exp, bias=f_r[:, 16:17],
                                 accum_out=f_r[:, 17:18]).then_inc(sem("f_exp"), 1)
            act.wait_ge(*reach("f_rT_full", 1))
            nc.scalar.activation(f_rT[:], banks[0:8, 1, 0:P], ACT.Copy).then_inc(sem("f_rT_ready"), 1)
            act.wait_ge(*reach("f_scales", 2))
            nc.scalar.activation(f_os[:], banks[:, 3, :], ACT.Copy).then_inc(sem("f_os_ready"), 1)
            act.wait_ge(*reach("f_xT_full", 1))
            act.wait_ge(*reach("f_sign_ready", 1))
            nc.scalar.activation(f_xT[:].rearrange("p c n -> p (c n)"), banks[:, 4, :],
                                 ACT.Copy).then_inc(sem("f_xT_ready"), 1)

        def ffn_dve(dve):
            dve.wait_ge(*reach("f_logits", 1))
            nc.vector.tensor_reduce(f_r[:, 16:17], banks[:, 0, 0:8], AX.X, ALU.max, negate=True
                                    ).then_inc(sem("f_neg_max"), 1)
            dve.wait_ge(*reach("f_exp", 1))
            nc.vector.reciprocal(f_r[:, 18:19], f_r[:, 17:18]).then_inc(sem("f_inv"), 1)
            dve.wait_ge(*reach("f_inv", 1))
            nc.vector.tensor_scalar(f_r[:, 8:16], f_r[:, 0:8], f_r[:, 18:19], None, ALU.mult
                                    ).then_inc(sem("f_routing"), 1)
            dve.wait_ge(*reach("f_scales", 1))
            nc.vector.tensor_tensor(f_xs[:], xln[:], banks[:, 2, :], ALU.mult).then_inc(sem("f_scaled"), 1)
            dve.wait_ge(*reach("f_bias_in", 16))
            nc.vector.tensor_tensor(x[:], x[:], f_bias[:], ALU.add).then_inc(sem("f_biased"), 1)
            dve.wait_ge(*reach("f_out_full", 1))
            dve.wait_ge(*reach("f_os_ready", 1))
            dve.wait_ge(*reach("f_biased", 1))
            nc.vector.tensor_tensor(f_os[:], f_os[:], banks[:, 5, :], ALU.mult).then_inc(sem("f_y"), 1)
            dve.wait_ge(*reach("f_y", 1))
            nc.vector.tensor_tensor(x[:], x[:], f_os[:], ALU.add).then_inc(sem("f_x_sum"), 1)

        block = ctx.enter_context(nc.Block())

        @block.sync
        def _(sp):
            sp.dma_start(x[:], a["x"]).then_inc(sem("x_in"), 16)
            sp.dma_start(const[:], a["const"]).then_inc(sem("const_in"), 16)
            ctx_sync(sp)
            cross[0].sync(sp)
            mla_sync(sp)
            moe_sync(sp)
            sp.wait_ge(*reach("e_x_sum", 1))
            sp.dma_start(bias_q[:], a["bq1"]).then_inc(sem("biases_in"), 16)
            sp.dma_start(bias_k[:], a["bkv1"][:, 0:8]).then_inc(sem("biases_in"), 16)
            sp.dma_start(bias_v[:], a["bkv1"][:, 8:16]).then_inc(sem("biases_in"), 16)
            sp.wait_ge(*reach("xlnT_ready", 4))
            sp.dma_start(rows[:], a["bo1"].broadcast_to([P, D])).then_inc(sem("bo_in"), 16)
            cross[1].sync(sp)
            ssm_sync(sp)
            ffn_sync(sp)
            sp.wait_ge(*reach("f_x_sum", 1))
            sp.dma_start(out, x[:]).then_inc(sem("out_written"), 16)
            sp.wait_ge(*reach("out_written", 16))

        @block.gpsimd
        def _(pool):
            mla_pool(pool)

        @block.tensor
        def _(pe):
            pe.wait_ge(*reach("const_in", 16))
            ln_pe(pe, 0)
            cross[0].pe(pe)
            ln_pe(pe, 1)
            mla_pe(pe)
            ln_pe(pe, 2)
            moe_pe(pe)
            ln_pe(pe, 3)
            cross[1].pe(pe)
            ln_pe(pe, 4)
            ssm_pe(pe)
            ln_pe(pe, 5)
            ffn_pe(pe)

        @block.scalar
        def _(act):
            ln_act(act, 0)
            ctx_act(act)
            act.wait_ge(*reach("xlnT_ready", 1))
            nc.scalar.activation(ctx_hi[:, :, CTX:KMAX], xlnT[:], ACT.Copy).then_inc(sem("ctx_hi"), 1)
            cross[0].act(act)
            ln_act(act, 1)
            mla_act(act)
            ln_act_head(act, 2)
            moe_act(act)
            ln_act(act, 3)
            act.wait_ge(*reach("biases_in", 48))
            cross[1].act(act)
            ln_act(act, 4)
            ssm_act(act)
            ln_act(act, 5)
            ffn_act(act)

        @block.vector
        def _(dve):
            dve.wait_ge(*reach("x_in", 16))
            dve.wait_ge(*reach("const_in", 16))
            ln_dve(dve, 0)
            ctx_dve(dve)
            dve.wait_ge(*reach("ctx_hi", DC + 1))
            nc.vector.tensor_tensor(ctx_lo[:, :, CTX:KMAX], xlnT[:], ctx_hi[:, :, CTX:KMAX].bitcast(F32),
                                    ALU.subtract).then_inc(sem("ctx_lo"), 1)
            cross[0].dve(dve)
            ln_dve(dve, 1)
            mla_dve(dve)
            ln_dve(dve, 2)
            moe_dve(dve)
            ln_dve(dve, 3)
            dve.wait_ge(*reach("biases_in", 48))
            nc.vector.tensor_scalar(bias_q[:], bias_q[:], ATT_SCALE, None, ALU.mult).then_inc(sem("bq_scaled"), 1)
            dve.wait_ge(*reach("bo_in", 16))
            nc.vector.tensor_tensor(x[:], x[:], rows[:], ALU.add).then_inc(sem("bo_added"), 1)
            dve.wait_ge(*reach("bo_added", 1))
            dve.wait_ge(*reach("bq_scaled", 1))
            cross[1].dve(dve)
            ln_dve(dve, 4)
            ssm_dve(dve)
            ln_dve(dve, 5)
            ffn_dve(dve)


_OUT = (1, 128, 512)


def kernel(**inputs):
    import numpy as np
    import concourse.bacc as bacc
    from concourse.bass_utils import run_bass_kernel_spmd

    t, arrays = _layout(np, inputs)
    nc = bacc.Bacc("TRN2", target_bir_lowering=False, num_devices=1)
    aps = {n: nc.dram_tensor(n, v.shape, mybir.dt.from_np(v.dtype), kind="ExternalInput").ap()
           for n, v in arrays.items()}
    out = nc.dram_tensor("y", (128, 512), mybir.dt.float32, kind="ExternalOutput").ap()
    build(nc, aps, out)
    r = run_bass_kernel_spmd(nc, [arrays], core_ids=[0])
    return r.results[0]["y"].reshape(_OUT)


def _layout(np, i):
    c = np.ascontiguousarray
    i = {k: np.asarray(v) for k, v in i.items()}
    ar = {
        "x": c(i["x"][0]),
        "ctxT": c(i["ctx_4096"][0].T),
        "const": _constants(np),
        "Wq0": i["L0_xattn_Wq"], "Wk0": i["L0_xattn_Wk"], "Wv0": i["L0_xattn_Wv"], "Wo0": i["L0_xattn_Wo"],
        "Wq1": i["L1_xattn_Wq"], "Wk1": c(i["L1_xattn_Wkv"][:, :1024]), "Wv1": c(i["L1_xattn_Wkv"][:, 1024:]),
        "Wo1": i["L1_xattn_Wo"], "bq1": c(i["L1_xattn_bq"].reshape(32, 128).T),
        "bkv1": c(i["L1_xattn_bkv"].reshape(16, 128).T), "bo1": c(i["L1_xattn_bo"].reshape(1, 512)),
        "m_wa": c(np.concatenate([i["L0_attn_wq_a"], i["L0_attn_wkv_a"]]).T),
        "m_lnq": c(i["L0_attn_q_a_ln_w"].reshape(128, 1)), "m_lnkv": c(i["L0_attn_kv_a_ln_w"].reshape(32, 1)),
        "m_wqb": c(i["L0_attn_wq_b"].T), "m_wkvb": c(i["L0_attn_wkv_b"].T), "m_wo": c(i["L0_attn_wo"].T),
        "e_gw": i["L0_ffn_gate_w"], "e_gb": c(i["L0_ffn_gate_b"].reshape(1, 3)),
        "e_w1": i["L0_ffn_w1"], "e_b1": c(i["L0_ffn_b1"].reshape(12, 128).T),
        "e_w2": i["L0_ffn_w2"], "e_b2": c(i["L0_ffn_b2"].reshape(1, 1536)),
        "s_in": c(i["L1_attn_in_proj_w"].T),
        "s_cw": c(i["L1_attn_conv_w"].reshape(80, 128, 4).transpose(1, 0, 2)),
        "s_cb": c(i["L1_attn_conv_b"].reshape(80, 128).T),
        "s_dtb": c(i["L1_attn_dt_bias"].reshape(1, 128)), "s_alog": c(i["L1_attn_A_log"].reshape(1, 128)),
        "s_D": c(i["L1_attn_D"].reshape(1, 128)), "s_nw": c(i["L1_attn_norm_w"].reshape(64, 128).T),
        "s_out": c(i["L1_attn_out_proj_w"].T),
        "f_w": c(i["L1_ffn_weight"].T), "f_b": c(i["L1_ffn_bias"].reshape(1, 512)),
        "f_gw": c(i["L1_ffn_gate_w"].T), "f_in": i["L1_ffn_in_channel_scale"],
        "f_out": i["L1_ffn_out_channel_scale"],
    }
    return i, {k: c(v) for k, v in ar.items()}


def _constants(np):
    import math
    n = np.arange(128)
    k, m = n[:, None], n[None, :]
    dim, base, factor, orig = 64, 10000.0, 128.0, 1024
    turn = lambda r: dim * math.log(orig / (r * 2 * math.pi)) / (2 * math.log(base))
    low, high = max(math.floor(turn(32.0)), 0), min(math.ceil(turn(1.0)), dim - 1)
    hi = high + 0.001 if low == high else float(high)
    keep = 1.0 - np.clip((np.arange(dim // 2, dtype=np.float32) - low) / (hi - low), 0.0, 1.0)
    extra = 1.0 / base ** (np.arange(0, dim, 2, dtype=np.float32) / dim)
    freq = extra / factor * (1.0 - keep) + extra * keep
    angle = np.outer(np.arange(128, dtype=np.float32), freq)
    vision = int(128 * 0.3)
    return np.concatenate([
        (k == m), np.ones((128, 128)), (k <= m), (k > m), np.where(m <= k, 0.0, MASKED),
        np.cos(angle), np.sin(angle),
        (k >= vision) / ((128 - vision) * 512.0), (k < vision) / (vision * 512.0),
    ], axis=1).astype(np.float32)
```

```python
import math
from contextlib import ExitStack

import concourse.bass as bass
from concourse import mybir

ALU = mybir.AluOpType
ACT = mybir.ActivationFunctionType
AX = mybir.AxisListType
F32 = mybir.dt.float32
F32R = mybir.dt.float32r

P = 128
TOK = 128
D = 512
DC = D // P
CTX = 2048
NHEAD = 32
EPS = 1e-5
RMS_EPS = 1e-6
ATT_SCALE = 1.0 / float(P) ** 0.5
MASKED = -1.0e30
C_IDENT, C_ONES, C_UPTO, C_AFTER, C_CAUSAL, C_COS, C_SIN, C_MEANS = 0, 128, 256, 384, 512, 640, 672, 704
C_WIDTH = 706


class Tally:

    def __init__(self, before=()):
        self.before, self.count, self.turn, self.step = dict(before), {}, 0, None

    def add(self, name, by=1):
        self.count[name] = self.count.get(name, 0) + by

    def local(self, name):
        return self.count.get(name, 0)

    def at(self, name, back=0):
        value = self.before.get(name, 0) + self.count.get(name, 0) - back
        if self.step is None:
            return value
        return value + self.turn * self.step.get(name, 0)


RING = 5
LAG = 2


def attention_plan(kv_groups, key_tiles, cuts):
    pairs = 4 * kv_groups
    nb = len(cuts)
    steps = (key_tiles + 1) // 2
    last_key = [sum(cuts[:c + 1]) for c in range(nb)]
    cost = {"K": 4, "S": 1, "EXP": 0}

    def scores_of(p, keys, exps_before):
        first = [("S", p, 0, c) for c in range(nb)]
        if keys:
            k = [("K", c) for c in range(nb)]
            first = k[:3] + [e for c in range(3, nb) for e in (first[c - 3], k[c])] + first[nb - 3:]
        before, side = list(exps_before), []
        for e in first:
            n = 2 if e[0] == "K" else 1
            side += before[:n] + [e]
            before = before[n:]
            if e[0] == "S":
                side.append(("MAX", *e[1:]))
        side += before + [("NEG", p, 0), ("WAIT",), ("EXP", p, 0, 0)]
        for c in range(nb):
            if c + 1 < nb:
                side.append(("EXP", p, 0, c + 1))
            side += [("S", p, 1, c), ("MAX", p, 1, c)]
        return side + [("NEG", p, 1), ("WAIT",)]

    def exps(p):
        return [("EXP", p, 1, c) for c in range(nb)] + [("RD", p)]

    def weave(main, side, needed=()):
        out, side = [], list(side)
        work, waits = sum(cost.get(e[0], 0) for e in side), side.count(("WAIT",))
        pause = 1.3 * work / (len(main) - waits)
        total, spent, n_exp = work + waits * pause, 0, 0
        for k, (before, after) in enumerate(main):
            share = []
            while side and (spent < (k + 1) / len(main) * total - 1e-9 or side[0][0] in ("MAX", "NEG", "RD")
                            or (needed and n_exp < needed[k])):
                e = side.pop(0)
                spent += pause if e[0] == "WAIT" else cost.get(e[0], 0)
                n_exp += e[0] == "EXP"
                if e[0] != "WAIT":
                    share.append(e)
            lead = next((i for i, e in enumerate(share) if e[0] == "NEG"), len(share))
            early = [e for e in share[:lead] if e[0] == "EXP"]
            out += early + before + after + [e for e in share if e not in early]
        return out + [e for e in side if e[0] != "WAIT"]

    needed = [1 + next(c for c in range(nb) if min(256 * k + 256, last_key[-1]) <= last_key[c])
              for k in range(steps)]

    def turn(first, last):
        o = []
        for p in range(pairs):
            more = p < pairs - 1 or not last
            more2 = p + 2 < pairs or not last
            keys = (p + 1) % (2 * kv_groups) == 0 and more
            keys2 = (p + 2) % (2 * kv_groups) == 0 and more2
            values = p == pairs - 1 and not last
            main = []
            for k in range(steps):
                before, after = [("T", p, k)], []
                if k >= LAG:
                    before.append(("PV", p, k - LAG))
                    if values:
                        before.append(("V", k - LAG))
                elif p > 0 or not first:
                    before.insert(0 if k == 0 else 1, ("PV", (p - 1) % pairs, steps - LAG + k))
                    if p == 0:
                        before.insert(1 if k == 0 else 2, ("V", steps - LAG + k))
                    if k == LAG - 1:
                        before.append(("OUT", (p - 1) % pairs))
                if k == 3 and p % 4 == 0 and (p > 0 or not first):
                    before.append(("WO",))
                if k == 1 and keys2:
                    before.append(("WK",))
                if k == 2 and p == pairs - 2 and not last:
                    before.append(("WV",))
                if k == steps - 1:
                    before.append(("NORM", p))
                if p % 2 == 0 and more2:
                    before += {3: [("QMM",)], 5: [("QTR",), ("QHALF", 0)]}.get(k, [])
                if p % 2 == 1 and more:
                    before += {1: [("QHALF", 1)]}.get(k, [])
                main.append((before, after))
            side = exps(p) if not more else scores_of((p + 1) % pairs, keys, exps(p))
            o += weave(main, side, needed)
        if last:
            o += [("PV", pairs - 1, k) for k in range(steps - LAG, steps)]
            o += [("OUT", pairs - 1), ("WO",)]
        return o

    prologue = [("WK",), ("CTX", 0), ("QMM",), ("CTX", 1), ("K", 0), ("CTX", 2), ("CTX", 3), ("QTR",), ("K", 1),
                ("QHALF", 0), ("QHALF", 1), ("CTX", 4), ("WV",), ("K", 2), ("K", 3), ("V", 0)]
    prologue += [("K", 4)] if nb > 4 else []
    prologue += weave([([], [("V", k)]) for k in range(1, steps)], scores_of(0, False, []))
    return prologue, turn(True, False), turn(False, False), turn(False, True)


SIGNALS = {
    "CTX": {},
    "WK": {"wk_hi": 1, "wk_lo": 1},
    "WV": {"wv_hi": 2, "wv_lo": 2},
    "QMM": {"q_part": 3, "t_full": 1, "q_row": 1},
    "QTR": {"t_full": 1, "q_col": 1},
    "QHALF": {"q_hi": 1, "q_lo": 1},
    "K": {"k_full": 1, "k_hi": 1, "k_lo": 1},
    "V": {"t_full": 1, "v_hi": 1, "v_lo": 1},
    "S": {"s_full": 1},
    "MAX": {"max_step": 1},
    "NEG": {"neg_max": 1},
    "EXP": {"exps": 1},
    "T": {"t_full": 1, "p_hi": 1, "p_lo": 1},
    "PV": {"pv": 1},
    "RD": {"rd_step": 2, "diag": 1},
    "NORM": {"t_full": 1, "r_row": 1},
    "OUT": {"heads_out": 1},
    "WO": {"wo_part": 7, "t_full": 1, "x_sum": 1},
}
ITEMS = {"WK": 1, "WV": 2, "QMM": 4, "WO": 8}
T_READ = {"QMM": "q_row", "QTR": "q_col", "V": "v_lo", "T": "p_lo", "NORM": "r_row", "WO": "x_sum"}


STEPS = {
    "pe_steps": [("m_latent", 1), ("m_aT_full", 1), ("e_means", 1), ("e_logits", 1), ("e_chosen", 1),
                 ("s_dt_full", 1), ("s_cb_full", 2), ("f_logits", 1), ("f_rT_full", 1), ("f_scales", 2),
                 ("f_xT_full", 1), ("f_out_full", 1)],
    "act_steps": [("m_sq", 2), ("m_aT_ready", 1), ("e_abs", 1), ("e_exp", 1), ("s_dt_abs", 1), ("s_dt_exp", 1), ("s_a_exp", 1), ("s_dt_ln", 1),
                  ("f_sign_ready", 1), ("f_exp", 1), ("f_rT_ready", 1), ("f_os_ready", 1), ("f_xT_ready", 1)],
    "dve_steps": [("m_a_clear", 1), ("m_var", 1), ("m_a_ready", 1), ("m_x_sum", 1),
                  ("e_weighed", 1), ("e_ratio", 1), ("e_neg_max", 1), ("e_choice", 1), ("e_x_sum", 1),
                  ("bq_scaled", 1), ("bo_added", 1), ("s_dt_u", 1), ("s_cb_ready", 2),
                  ("s_x_sum", 1), ("f_neg_max", 1), ("f_inv", 1), ("f_routing", 1),
                  ("f_scaled", 1), ("f_biased", 1), ("f_y", 1), ("f_x_sum", 1)],
}
SHARED = {}
for _carrier, _signals in STEPS.items():
    _before = 0
    for _name, _times in _signals:
        SHARED[_name] = (_carrier, _before)
        _before += _times


def build(nc, a, out):
    where = [-(-nc.sbuf_base // 64) * 64]

    def place(name, shape, dt=F32, at=None):
        size = 4
        for n in shape[1:]:
            size *= n
        offset = where[0] if at is None else at
        t = nc.alloc_sbuf_tensor_at(name, shape, dt, offset=offset)
        assert offset + size <= nc.sbuf_usable_end, (name, offset + size)
        if at is None:
            where[0] = offset + -(-size // 32) * 32
        return t

    with ExitStack() as ctx:
        sems = {}

        def sem(name):
            name = SHARED.get(name, (name, 0))[0]
            if name not in sems:
                sems[name] = ctx.enter_context(nc.semaphore(name))
            return sems[name]

        def reach(name, times=1):
            return sem(name), SHARED.get(name, (name, 0))[1] + times

        banks = ctx.enter_context(nc.psum_tensor("banks", [P, 8, 512], F32))
        PV_BANK = 7

        const = place("const", [P, C_WIDTH])
        ident = const[:, C_IDENT:C_IDENT + P]
        ones = const[:, C_ONES:C_ONES + P]
        x = place("x", [TOK, D])
        xlnT = place("xlnT", [P, DC, TOK])
        ln = place("ln", [TOK, 24])
        minus_half = place("minus_half", [TOK, 8])
        rows = place("rows", [TOK, D])
        xln = rows
        shared = where[0]

        KMAX = CTX + TOK
        ctx_hi = place("ctx_hi", [P, DC, KMAX], F32R)
        ctx_lo = place("ctx_lo", [P, DC, KMAX], F32R)
        attn_base = where[0]
        v_hi = place("v_hi", [P, 17, 256], F32R)
        v_lo = place("v_lo", [P, 17, 256], F32R)
        k_hi = place("k_hi", [P, KMAX], F32R)
        k_lo = place("k_lo", [P, KMAX], F32R)
        prob = place("prob", [TOK, 4, KMAX])
        q_hi = place("q_hi", [P, 4, TOK], F32R)
        q_lo = place("q_lo", [P, 4, TOK], F32R)
        heads = place("heads", [P, 8, TOK])
        pt_hi = place("pt_hi", [P, 3, 512], F32R)
        pt_lo = place("pt_lo", [P, 3, 512], F32R)
        ring = place("ring", [P, RING, 512])
        wk_hi = place("wk_hi", [P, DC, P], F32R)
        wk_lo = place("wk_lo", [P, DC, P], F32R)
        wv_hi = place("wv_hi", [P, DC, 256], F32R)
        wv_lo = place("wv_lo", [P, DC, 256], F32R)
        inv_row = place("inv_row", [P, 256])
        diag = place("diag", [P, 2, P])
        stat = place("stat", [P, 4, 5 + 5 + 1])
        inv = place("inv", [P, 4])
        bias_q = place("bias_q", [P, NHEAD])
        bias_k = place("bias_k", [P, 8])
        bias_v = place("bias_v", [P, 8])


        where[0] = attn_base
        m_wa = place("m_wa", [P, DC, 224])
        m_wqb = place("m_wqb", [P, 4096])
        m_wkvb = place("m_wkvb", [P, 6144])
        m_a = place("m_a", [TOK, 384])
        m_aT = place("m_aT", [P, 3, TOK])
        m_q = place("m_q", [TOK, NHEAD, P])
        m_v = place("m_v", [TOK, NHEAD, P])
        m_qT = place("m_qT", [P, NHEAD, TOK])
        m_kT = place("m_kT", [P, NHEAD, TOK])
        m_st = place("m_st", [TOK, 4, NHEAD])
        m_rot = place("m_rot", [TOK, 4, 4, 32])
        m_lnw = place("m_lnw", [P, 2])
        m_ring = place("m_ring", [P, 4, 1024])

        where[0] = attn_base
        e_w1 = place("e_w1", [P, 3, DC, D])
        e_w2 = place("e_w2", [P, 3, DC, D])
        e_act = place("e_act", [P, 3, DC, TOK])
        e_gw = place("e_gw", [P, DC, 4])
        e_row = place("e_row", [1, 8 + 3 * D + P])
        e_b1 = place("e_b1", [P, 12])
        e_s = place("e_s", [TOK, 64])

        where[0] = shared
        NSLOT = 5
        s_w = place("s_w", [P, NSLOT, DC, D])
        decay_base = where[0]
        s_decay = place("s_decay", [TOK, 128, P])
        s_g = place("s_g", [TOK, 8192])
        s_mix = place("s_mix", [TOK, 2, 8, P])
        s_conv = place("s_conv", [P, 2, DC, TOK])
        s_tanh = place("s_tanh", [P, 2, DC, TOK])
        s_chan = place("s_chan", [P, 2, DC, TOK])
        s_hs = place("s_hs", [TOK, 2, 512])
        s_gate = place("s_gate", [TOK, 2, 512])
        s_bT = place("s_bT", [P, 8, TOK])
        s_cT = place("s_cT", [P, 8, TOK])
        s_cb = place("s_cb", [TOK, 8, TOK])
        s_seg = place("s_seg", [TOK, 4, 4, P])
        s_cw = place("s_cw", [P, 80, 4])
        s_cbias = place("s_cbias", [P, 80])
        s_dt = place("s_dt", [TOK, 8, 128])
        s_row = place("s_row", [1, 3 * 128])
        s_nw = place("s_nw", [P, 64])
        s_var = place("s_var", [TOK, 4, 16])
        s_y = place("s_y", [TOK, 2, 512])
        s_sq = place("s_sq", [TOK, 512])

        where[0] = decay_base
        f_w = place("f_w", [P, DC, D])
        f_sign = place("f_sign", [P, DC, D])
        f_gw = place("f_gw", [P, DC, 8])
        f_scale = place("f_scale", [8, 2, D])
        f_bias = place("f_bias", [TOK, D])
        f_xs = place("f_xs", [TOK, D])
        f_xT = place("f_xT", [P, DC, TOK])
        f_r = place("f_r", [TOK, 24])
        f_rT = place("f_rT", [8, TOK])
        f_os = place("f_os", [TOK, D])

        def ln_dve(dve, n):
            nc.vector.bn_stats(ln[:, 0:6], x[:]).then_inc(sem("ln_stats"), 1)
            dve.wait_ge(*reach("ln_stats", n + 1))
            nc.vector.bn_aggr(ln[:, 6:8], ln[:, 0:6]).then_inc(sem("ln_aggr"), 1)
            dve.wait_ge(*reach("ln_aggr", n + 1))
            nc.vector.tensor_scalar(ln[:, 8:9], ln[:, 7:8], EPS, None, ALU.add).then_inc(sem("ln_var"), 1)
            rsqrt_dve(dve, ln[:, 8:9], ln[:, 9:10], ln[:, 11:12])
            nc.vector.tensor_scalar(xln[:], x[:], ln[:, 6:7], ln[:, 9:10], ALU.subtract,
                                    ALU.mult).then_inc(sem("xln_ready"), 1)

        roots = [0]
        own_steps = [0]

        def rsqrt_pool(pool, ready, count, v, y):
            pool.wait_ge(*reach(ready, count))
            nc.gpsimd.tensor_tensor(y, v, minus_half[:, 0:v.shape[1]], ALU.pow).then_inc(sem("root_guess"), 1)

        def rsqrt_dve(dve, v, y, t):
            n = roots[0]
            roots[0] += 1
            dve.wait_ge(*reach("root_guess", n + 1))
            nc.vector.tensor_tensor(t, y, y, ALU.mult).then_inc(sem("root_step"), 1)
            dve.wait_ge(*reach("root_step", 4 * n + 1))
            nc.vector.tensor_tensor(t, t, v, ALU.mult).then_inc(sem("root_step"), 1)
            dve.wait_ge(*reach("root_step", 4 * n + 2))
            nc.vector.tensor_scalar(t, t, -0.5, 1.5, ALU.mult, ALU.add).then_inc(sem("root_step"), 1)
            dve.wait_ge(*reach("root_step", 4 * n + 3))
            nc.vector.tensor_tensor(y, y, t, ALU.mult).then_inc(sem("root_step"), 1)
            dve.wait_ge(*reach("root_step", 4 * n + 4))

        def ln_pool(pool, n):
            rsqrt_pool(pool, "ln_var", n + 1, ln[:, 8:9], ln[:, 9:10])

        def ln_act(act, n):
            act.wait_ge(*reach("xln_turned", n + 1))
            nc.scalar.activation(xlnT[:], banks[:, PV_BANK, :], ACT.Copy).then_inc(sem("xlnT_ready"), 1)

        def ln_pe(pe, n):
            pe.wait_ge(*reach("xln_ready", n + 1))
            for c in range(DC):
                mm = pe.transpose(banks[:, PV_BANK, c * P:(c + 1) * P], xln[:, c * P:(c + 1) * P], ident)
            mm.then_inc(sem("xln_turned"), 1)
            pe.wait_ge(*reach("xlnT_ready", n + 1))

        def three_passes(pe, dst, pairs, start=True, stop=True):
            for n, (w_hi, w_lo, m_hi, m_lo) in enumerate(pairs):
                pe.matmul(dst, w_hi, m_hi, start=start and n == 0, stop=False)
                pe.matmul(dst, w_hi, m_lo, start=False, stop=False)
                mm = pe.matmul(dst, w_lo, m_hi, start=False, stop=stop and n == len(pairs) - 1)
            return mm

        ctx_cuts = [(0, 448), (448, 896), (896, 1344), (1344, 1792), (1792, CTX)]

        def ctx_load(sp, n):
            lo, hi = ctx_cuts[n]
            sp.dma_start(prob[:, :, lo:hi], a["ctxT"][:, lo:hi].rearrange("(c p) n -> p c n", p=P)
                         ).then_inc(sem(f"ctx_in{n}"), 16)

        def ctx_act(act):
            act.wait_ge(*reach("xlnT_ready", 1))
            nc.scalar.activation(ctx_hi[:, :, CTX:KMAX], xlnT[:], ACT.Copy).then_inc(sem("ctx_hi"), 1)

        def ctx_act_block(act, n):
            lo, hi = ctx_cuts[n]
            act.wait_ge(sem(f"ctx_in{n}"), 16)
            nc.scalar.activation(ctx_hi[:, :, lo:hi], prob[:, :, lo:hi], ACT.Copy).then_inc(sem("ctx_hi"), 1)

        def ctx_dve(dve):
            dve.wait_ge(*reach("ctx_hi", 1))
            nc.vector.tensor_tensor(ctx_lo[:, :, CTX:KMAX], xlnT[:], ctx_hi[:, :, CTX:KMAX].bitcast(F32),
                                    ALU.subtract).then_inc(sem("ctx_lo"), 1)

        def ctx_dve_block(dve, n):
            lo, hi = ctx_cuts[n]
            dve.wait_ge(*reach("ctx_hi", n + 2))
            nc.vector.tensor_tensor(ctx_lo[:, :, lo:hi], prob[:, :, lo:hi], ctx_hi[:, :, lo:hi].bitcast(F32),
                                    ALU.subtract).then_inc(sem("ctx_lo"), 1)

        class Cross:
            def __init__(self, layer, before=None):
                self.layer = layer
                self.kv_groups, self.tiles, self.turns = ((2, 17, 2), (1, 16, 4))[layer]
                self.cuts = ([448, 448, 448, 448, 384], [512] * 4)[layer]
                self.nb = len(self.cuts)
                self.off = [sum(self.cuts[:c]) for c in range(self.nb)]
                self.t_banks = ((5, 6), (4, 5, 6))[layer]
                self.plan = attention_plan(self.kv_groups, self.tiles, self.cuts)
                self.Wq, self.Wo = a[f"Wq{layer}"], a[f"Wo{layer}"]
                self.before = before.totals() if before else {}
                items = sum(by * self.before.get(kind, 0) for kind, by in ITEMS.items())
                self.slot_before = [(items + RING - 1 - s) // RING for s in range(RING)]

            def sem(self, name):
                return sem("x_" + name)

            def t_bank(self, t):
                return self.t_banks[t.local("t_full") % len(self.t_banks)]

            def item(self, t, number=0):
                n = sum(by * t.local(kind) for kind, by in ITEMS.items()) + number
                loads = n // RING + 1 + self.slot_before[n % RING]
                return ring[:, n % RING, :], (self.sem(f"ring_in{n % RING}"), 16 * loads)

            def totals(self):
                last = []
                self.walk(lambda e, t: last.append(t))
                return last[-1].count

            def walk(self, visit):
                prologue, first, body, last = self.plan
                tally = Tally(self.before)
                for e in prologue + first + body * (self.turns - 2) + last:
                    visit(e, tally)
                    for name, by in SIGNALS[e[0]].items():
                        tally.add(name, by)
                    tally.add(e[0])

            def sync(self, sp):
                L = self.layer
                Wk, Wv = a[f"Wk{L}"], a[f"Wv{L}"]
                used = []

                def between(n):
                    if L == 0:
                        for block in range(5) if n == RING else ():
                            ctx_load(sp, block)
                    elif n == RING:
                        sp.wait_ge(*reach("xlnT_ready", 4))
                        sp.dma_start(rows[:], a["bo1"].broadcast_to([P, D])).then_inc(sem("bo_in"), 16)

                def load(src, user, value):
                    n = len(used)
                    if n >= RING:
                        sp.wait_ge(self.sem(used[n - RING][0]), used[n - RING][1])
                    used.append((user, value))
                    c, w = src.shape[0] // P, src.shape[1]
                    sp.dma_start(ring[:, n % RING, :].rearrange("p (c n) -> p c n", c=c),
                                 src.rearrange("(c p) n -> p c n", p=P)).then_inc(self.sem(f"ring_in{n % RING}"), 16)
                    between(n + 1)

                def visit(e, t):
                    n = t.local(e[0])
                    if e[0] == "WK":
                        load(Wk[:, n * P:(n + 1) * P], "wk_lo", t.at("wk_lo") + 1)
                    elif e[0] == "WV":
                        for h in range(2):
                            load(Wv[h * 256:(h + 1) * 256, n * 256:(n + 1) * 256], "wv_lo", t.at("wv_lo") + h + 1)
                    elif e[0] == "QMM":
                        for c in range(4):
                            load(self.Wq[c * P:(c + 1) * P, n * 512:(n + 1) * 512],
                                 *(("q_part", t.at("q_part") + c + 1) if c < 3 else ("t_full", t.at("t_full") + 1)))
                    elif e[0] == "WO":
                        for h in range(8):
                            load(self.Wo[(n * 8 + h) * P:(n * 8 + h + 1) * P, :],
                                 *(("wo_part", t.at("wo_part") + h + 1) if h < 7 else ("t_full", t.at("t_full") + 1)))

                self.walk(visit)

            def pe(self, pe):
                t_users = []
                bank_read = {}
                exp_done = {}
                v_done = {}

                def t_slot(e, t):
                    n = len(self.t_banks)
                    if len(t_users) >= n:
                        pe.wait_ge(self.sem(t_users[-n][0]), t_users[-n][1])
                    t_users.append((T_READ[e], t.at(T_READ[e]) + 1))
                    return banks[:, self.t_bank(t), :]

                def ring_item(t, number):
                    weights, landed = self.item(t, number)
                    pe.wait_ge(*landed)
                    return weights

                def visit(e, t):
                    kind = e[0]
                    if kind == "QMM":
                        bank = t_slot(kind, t)
                        for c in range(4):
                            w = ring_item(t, c)
                            pe.matmul(bank, xlnT[:, c, :], w, start=(c == 0), stop=(c == 3)
                                      ).then_inc(self.sem("q_part" if c < 3 else "t_full"), 1)
                    elif kind == "QTR":
                        bank = t_slot(kind, t)
                        pe.wait_ge(self.sem("q_row"), t.at("q_row"))
                        for h in range(4):
                            mm = pe.transpose(bank[:, h * P:(h + 1) * P], rows[:, h * P:(h + 1) * P], ident)
                        mm.then_inc(self.sem("t_full"), 1)
                    elif kind == "K":
                        c = e[1]
                        if c == 0:
                            pe.wait_ge(self.sem("wk_lo"), t.at("wk_lo"))
                        if self.layer == 0 and t.local("K") < self.nb:
                            pe.wait_ge(*reach("ctx_lo", c + 2))
                        if c in bank_read:
                            pe.wait_ge(*bank_read[c])
                        bank_read[c] = (self.sem("k_lo"), t.at("k_lo") + 1)
                        k = slice(self.off[c], self.off[c] + self.cuts[c])
                        three_passes(pe, banks[:, c, 0:self.cuts[c]],
                                     [(wk_hi[:, d, :], wk_lo[:, d, :], ctx_hi[:, d, k], ctx_lo[:, d, k])
                                      for d in range(DC)]).then_inc(self.sem("k_full"), 1)
                    elif kind == "V":
                        bank = t_slot(kind, t)
                        if e[1] == 0:
                            pe.wait_ge(self.sem("wv_lo"), t.at("wv_lo"))
                        for n, tile in enumerate(range(2 * e[1], min(2 * e[1] + 2, self.tiles))):
                            k = slice(tile * P, (tile + 1) * P)
                            mm = three_passes(pe, bank[:, n * 256:(n + 1) * 256],
                                              [(ctx_hi[:, d, k], ctx_lo[:, d, k], wv_hi[:, d, :], wv_lo[:, d, :])
                                               for d in range(DC)])
                        mm.then_inc(self.sem("t_full"), 1)
                        v_done[e[1]] = t.at("v_lo") + 1
                    elif kind == "S":
                        _, p, half, c = e
                        if c == 0:
                            pe.wait_ge(self.sem("q_lo"), t.at("q_lo"))
                        pe.wait_ge(*bank_read[c])
                        h = 2 * (p % 2) + half
                        k = slice(self.off[c], self.off[c] + self.cuts[c])
                        three_passes(pe, banks[:, c, 0:self.cuts[c]],
                                     [(q_hi[:, h, :], q_lo[:, h, :], k_hi[:, k], k_lo[:, k])]
                                     ).then_inc(self.sem("s_full"), 1)
                    elif kind == "EXP":
                        exp_done[e[1:]] = t.at("exps") + 1
                        bank_read[e[3]] = (self.sem("exps"), t.at("exps") + 1)
                    elif kind == "T":
                        _, p, k = e
                        tiles = range(2 * k, min(2 * k + 2, self.tiles))
                        c = max(c for c in range(self.nb) if self.off[c] < (tiles[-1] + 1) * P)
                        bank = t_slot(kind, t)
                        pe.wait_ge(self.sem("exps"), exp_done[p, 1, c])
                        for n, tile in enumerate(tiles):
                            for half in range(2):
                                mm = pe.transpose(bank[:, (2 * n + half) * P:(2 * n + half + 1) * P],
                                                  prob[:, 2 * (p % 2) + half, tile * P:(tile + 1) * P], ident)
                        mm.then_inc(self.sem("t_full"), 1)
                    elif kind == "PV":
                        _, p, k = e
                        pe.wait_ge(self.sem("p_lo"), t.at("PV") + 1)
                        if p == 0:
                            pe.wait_ge(self.sem("v_lo"), v_done[k])
                        if k == 0 and t.local("OUT"):
                            if self.layer == 0:
                                pe.wait_ge(self.sem("heads_out"), t.at("heads_out"))
                            else:
                                pe.wait_ge(self.sem("scaled"), t.local("OUT"))
                        kv = p // (2 * self.kv_groups)
                        dst = banks[:, PV_BANK, (p % 2) * 256:(p % 2) * 256 + 256]
                        buf = t.local("PV") % 3
                        for n, tile in enumerate(range(2 * k, min(2 * k + 2, self.tiles))):
                            v = (v_hi[:, tile, kv * P:(kv + 1) * P], v_lo[:, tile, kv * P:(kv + 1) * P])
                            m = slice(n * 256, (n + 1) * 256)
                            mm = three_passes(pe, dst, [(*v, pt_hi[:, buf, m], pt_lo[:, buf, m])],
                                              start=(tile == 0), stop=(tile == self.tiles - 1))
                        mm.then_inc(self.sem("pv"), 1)
                    elif kind == "NORM":
                        bank = t_slot(kind, t)
                        pe.wait_ge(self.sem("diag"), t.at("diag"))
                        pe.matmul(bank[:, 0:256], ones, diag[:].rearrange("p h n -> p (h n)"),
                                  start=True, stop=True).then_inc(self.sem("t_full"), 1)
                    elif kind == "WO":
                        bank = t_slot(kind, t)
                        pe.wait_ge(self.sem("heads_out"), t.at("heads_out"))
                        for h in range(8):
                            w = ring_item(t, h)
                            pe.matmul(bank, heads[:, h, :], w, start=(h == 0), stop=(h == 7)
                                      ).then_inc(self.sem("wo_part" if h < 7 else "t_full"), 1)

                self.walk(visit)

            def act(self, act):
                def visit(e, t):
                    kind, nxt = e[0], t.at("t_full") + 1
                    bank = banks[:, self.t_bank(t), :]
                    if self.layer == 0 and kind == "CTX":
                        ctx_act_block(act, e[1])
                    elif kind == "WK":
                        weights, landed = self.item(t)
                        act.wait_ge(*landed)
                        if t.local("K"):
                            act.wait_ge(self.sem("k_full"), t.at("k_full"))
                        nc.scalar.activation(wk_hi[:].rearrange("p c n -> p (c n)"), weights,
                                             ACT.Copy).then_inc(self.sem("wk_hi"), 1)
                    elif kind == "WV":
                        if t.local("V"):
                            act.wait_ge(self.sem("t_full"), t.at("t_full"))
                        for h in range(2):
                            weights, landed = self.item(t, h)
                            act.wait_ge(*landed)
                            nc.scalar.activation(wv_hi[:, 2 * h:2 * h + 2, :].rearrange("p c n -> p (c n)"), weights,
                                                 ACT.Copy).then_inc(self.sem("wv_hi"), 1)
                    elif kind == "QMM":
                        act.wait_ge(self.sem("t_full"), nxt)
                        if t.local("QMM"):
                            act.wait_ge(self.sem("q_lo"), t.at("q_lo"))
                        elif self.layer == 1:
                            act.wait_ge(*reach("bo_added", 1))
                        nc.scalar.activation(rows[:], bank, ACT.Copy).then_inc(self.sem("q_row"), 1)
                    elif kind == "QHALF":
                        h = 2 * e[1]
                        act.wait_ge(self.sem("q_col"), t.at("q_col"))
                        if t.local("S"):
                            act.wait_ge(self.sem("s_full"), t.at("s_full"))
                        nc.scalar.activation(q_hi[:, h:h + 2, :].rearrange("p h n -> p (h n)"),
                                             rows[:, h * P:(h + 2) * P], ACT.Copy).then_inc(self.sem("q_hi"), 1)
                    elif kind == "K":
                        c = e[1]
                        o, w = self.off[c], self.cuts[c]
                        act.wait_ge(self.sem("k_full"), t.at("k_full") + 1)
                        if self.layer == 0:
                            nc.scalar.activation(k_hi[:, o:o + w], banks[:, c, 0:w],
                                                 ACT.Copy).then_inc(self.sem("k_hi"), 1)
                        else:
                            kv = t.local("K") // self.nb
                            nc.scalar.activation(k_hi[:, o:o + w], banks[:, c, 0:w], ACT.Identity,
                                                 bias=bias_k[:, kv:kv + 1]).then_inc(self.sem("k_hi"), 1)
                    elif kind == "V":
                        k = e[1]
                        n = min(2, self.tiles - 2 * k)
                        act.wait_ge(self.sem("t_full"), nxt)
                        nc.scalar.activation(v_hi[:, 2 * k:2 * k + n, :].rearrange("p t n -> p (t n)"),
                                             bank[:, 0:256 * n], ACT.Copy).then_inc(self.sem("v_hi"), 1)
                    elif kind == "EXP":
                        _, p, half, c = e
                        slot = 2 * (p % 2) + half
                        o, w = self.off[c], self.cuts[c]
                        if c == 0:
                            act.wait_ge(self.sem("neg_max"), t.at("neg_max"))
                        nc.scalar.activation(prob[:, slot, o:o + w], banks[:, c, 0:w], ACT.Exp,
                                             bias=stat[:, slot, 10:11], accum_out=stat[:, slot, c:c + 1]
                                             ).then_inc(self.sem("exps"), 1)
                    elif kind == "T":
                        n, w = t.local("T"), 256 * min(2, self.tiles - 2 * e[2])
                        act.wait_ge(self.sem("t_full"), nxt)
                        if n >= 3:
                            act.wait_ge(self.sem("pv"), t.at("T", back=2))
                        nc.scalar.activation(pt_hi[:, n % 3, 0:w], bank[:, 0:w],
                                             ACT.Copy).then_inc(self.sem("p_hi"), 1)
                    elif kind == "NORM":
                        act.wait_ge(self.sem("t_full"), nxt)
                        if t.local("NORM"):
                            act.wait_ge(self.sem("heads_out"), t.at("heads_out"))
                        nc.scalar.activation(inv_row[:], bank[:, 0:256], ACT.Copy).then_inc(self.sem("r_row"), 1)

                self.walk(visit)

            def dve(self, dve):
                def minus(out, in0, hi):
                    return nc.vector.tensor_tensor(out, in0, hi.bitcast(F32), ALU.subtract)

                def visit(e, t):
                    kind, nxt = e[0], t.at("t_full") + 1
                    bank = banks[:, self.t_bank(t), :]
                    if self.layer == 0 and kind == "CTX":
                        ctx_dve_block(dve, e[1])
                    elif kind == "WK":
                        dve.wait_ge(self.sem("wk_hi"), t.at("wk_hi") + 1)
                        minus(wk_lo[:].rearrange("p c n -> p (c n)"), self.item(t)[0],
                              wk_hi[:].rearrange("p c n -> p (c n)")).then_inc(self.sem("wk_lo"), 1)
                    elif kind == "WV":
                        for h in range(2):
                            dve.wait_ge(self.sem("wv_hi"), t.at("wv_hi") + h + 1)
                            minus(wv_lo[:, 2 * h:2 * h + 2, :].rearrange("p c n -> p (c n)"), self.item(t, h)[0],
                                  wv_hi[:, 2 * h:2 * h + 2, :].rearrange("p c n -> p (c n)")
                                  ).then_inc(self.sem("wv_lo"), 1)
                    elif kind == "QMM":
                        if self.layer == 1 and not t.local("QMM"):
                            dve.wait_ge(*reach("bo_in", 16))
                            nc.vector.tensor_tensor(x[:], x[:], rows[:], ALU.add).then_inc(sem("bo_added"), 1)
                            dve.wait_ge(*reach("bo_added", 1))
                    elif kind == "QTR":
                        g = t.local("QTR")
                        dve.wait_ge(self.sem("t_full"), nxt)
                        if self.layer == 0:
                            ins = nc.vector.tensor_scalar(rows[:], bank, ATT_SCALE, None, ALU.mult)
                        else:
                            ins = nc.vector.scalar_tensor_tensor(
                                rows[:].rearrange("p (h n) -> p h n", h=4), bank.rearrange("p (h n) -> p h n", h=4),
                                ATT_SCALE, bias_q[:, 4 * g:4 * g + 4].unsqueeze(2).broadcast_to([P, 4, P]),
                                ALU.mult, ALU.add)
                        ins.then_inc(self.sem("q_col"), 1)
                    elif kind == "QHALF":
                        h = 2 * e[1]
                        dve.wait_ge(self.sem("q_hi"), t.at("q_hi") + 1)
                        minus(q_lo[:, h:h + 2, :].rearrange("p h n -> p (h n)"), rows[:, h * P:(h + 2) * P],
                              q_hi[:, h:h + 2, :].rearrange("p h n -> p (h n)")).then_inc(self.sem("q_lo"), 1)
                    elif kind == "K":
                        c = e[1]
                        o, w = self.off[c], self.cuts[c]
                        dve.wait_ge(self.sem("k_hi"), t.at("k_hi") + 1)
                        if self.layer == 0:
                            minus(k_lo[:, o:o + w], banks[:, c, 0:w], k_hi[:, o:o + w]).then_inc(self.sem("k_lo"), 1)
                        else:
                            kv = t.local("K") // self.nb
                            nc.vector.scalar_tensor_tensor(
                                k_lo[:, o:o + w], banks[:, c, 0:w], bias_k[:, kv:kv + 1],
                                k_hi[:, o:o + w].bitcast(F32), ALU.add, ALU.subtract).then_inc(self.sem("k_lo"), 1)
                    elif kind == "V":
                        k = e[1]
                        n = min(2, self.tiles - 2 * k)
                        dve.wait_ge(self.sem("v_hi"), t.at("v_hi") + 1)
                        minus(v_lo[:, 2 * k:2 * k + n, :].rearrange("p t n -> p (t n)"), bank[:, 0:256 * n],
                              v_hi[:, 2 * k:2 * k + n, :].rearrange("p t n -> p (t n)")
                              ).then_inc(self.sem("v_lo"), 1)
                    elif kind == "MAX":
                        _, p, half, c = e
                        slot = 2 * (p % 2) + half
                        dve.wait_ge(self.sem("s_full"), t.at("s_full"))
                        nc.vector.tensor_reduce(stat[:, slot, 5 + c:6 + c], banks[:, c, 0:self.cuts[c]],
                                                AX.X, ALU.max).then_inc(self.sem("max_step"), 1)
                    elif kind == "NEG":
                        _, p, half = e
                        slot = 2 * (p % 2) + half
                        dve.wait_ge(self.sem("max_step"), t.at("max_step"))
                        nc.vector.tensor_reduce(stat[:, slot, 10:11], stat[:, slot, 5:5 + self.nb], AX.X,
                                                ALU.max, negate=True).then_inc(self.sem("neg_max"), 1)
                    elif kind == "T":
                        n, w = t.local("T"), 256 * min(2, self.tiles - 2 * e[2])
                        dve.wait_ge(self.sem("p_hi"), t.at("p_hi") + 1)
                        minus(pt_lo[:, n % 3, 0:w], bank[:, 0:w], pt_hi[:, n % 3, 0:w]).then_inc(self.sem("p_lo"), 1)
                    elif kind == "RD":
                        p = e[1]
                        dve.wait_ge(self.sem("exps"), exp_done[p])
                        nc.vector.tensor_reduce(inv[:, 0:2], stat[:, 2 * (p % 2):2 * (p % 2) + 2, 0:self.nb], AX.X,
                                                ALU.add).then_inc(self.sem("rd_step"), 1)
                        dve.wait_ge(self.sem("rd_step"), t.at("rd_step") + 1)
                        nc.vector.reciprocal(inv[:, 2:4], inv[:, 0:2]).then_inc(self.sem("rd_step"), 1)
                        dve.wait_ge(self.sem("rd_step"), t.at("rd_step") + 2)
                        if t.local("NORM"):
                            dve.wait_ge(self.sem("r_row"), t.at("r_row"))
                        for half in range(2):
                            ins = nc.vector.tensor_scalar(diag[:, half, :], ident, inv[:, 2 + half:3 + half], None,
                                                          ALU.mult)
                        ins.then_inc(self.sem("diag"), 1)
                    elif kind == "EXP":
                        exp_done[e[1]] = t.at("exps") + 1
                    elif kind == "OUT":
                        p, n = e[1], t.local("OUT")
                        dst = heads[:, 2 * (p % 4):2 * (p % 4) + 2, :].rearrange("p h n -> p (h n)")
                        dve.wait_ge(self.sem("r_row"), t.at("r_row"))
                        dve.wait_ge(self.sem("pv"), t.at("pv"))
                        ins = nc.vector.tensor_tensor(dst, banks[:, PV_BANK, (p % 2) * 256:(p % 2) * 256 + 256],
                                                      inv_row[:], ALU.mult)
                        if self.layer == 1:
                            kv = n // (2 * self.kv_groups)
                            ins.then_inc(self.sem("scaled"), 1)
                            dve.wait_ge(self.sem("scaled"), n + 1)
                            ins = nc.vector.tensor_scalar(dst, dst, bias_v[:, kv:kv + 1], None, ALU.add)
                        ins.then_inc(self.sem("heads_out"), 1)
                    elif kind == "WO":
                        dve.wait_ge(self.sem("t_full"), nxt)
                        if t.local("WO"):
                            dve.wait_ge(self.sem("x_sum"), t.at("x_sum"))
                        nc.vector.tensor_tensor(x[:], x[:], bank, ALU.add).then_inc(self.sem("x_sum"), 1)

                exp_done = {}
                self.walk(visit)
                dve.wait_ge(self.sem("x_sum"), self.before.get("x_sum", 0) + NHEAD // 8)

        cross = [Cross(0)]
        cross.append(Cross(1, cross[0]))

        MLA_SCALE = P ** -0.5 * (0.1 * math.log(128.0) + 1.0) ** 2
        QUADS = NHEAD // 4
        m_pT = m_wqb[:].rearrange("p (h n) -> p h n", h=NHEAD)
        m_out = m_wkvb[:, 0:4096].rearrange("p (h n) -> p h n", h=NHEAD)
        m_kv_w = m_wkvb[0:32, :].rearrange("p (h n) -> p h n", h=NHEAD)
        cos = const[:, C_COS:C_COS + 32]
        sin = const[:, C_SIN:C_SIN + 32]

        def per_head(ap, n, w):
            return ap.unsqueeze(1).broadcast_to([P, n, w])

        def per_column(ap, n, w):
            return ap.unsqueeze(2).broadcast_to([P, n, w])

        def quad(t, n):
            return t[:, 4 * n:4 * n + 4, :].rearrange("p h n -> p (h n)")

        def mla_sync(sp):
            sp.wait_ge(cross[0].sem("x_sum"), 4)
            sp.dma_start(m_wa[:], a["m_wa"].rearrange("(c p) n -> p c n", p=P)).then_inc(sem("m_wa_in"), 16)
            sp.dma_start(m_lnw[:, 0:1], a["m_lnq"]).then_inc(sem("m_lnw_in"), 16)
            sp.dma_start(m_lnw[0:32, 1:2], a["m_lnkv"]).then_inc(sem("m_lnw_in"), 16)
            sp.dma_start(m_wqb[:], a["m_wqb"]).then_inc(sem("m_wqb_in"), 16)
            sp.dma_start(m_wkvb[0:32, :], a["m_wkvb"]).then_inc(sem("m_wkvb_in"), 16)
            for n in range(16):
                if n >= 4:
                    sp.wait_ge(*reach("m_wo_used", n - 3))
                sp.dma_start(m_ring[:, n % 4, :], a["m_wo"][2 * n * P:2 * (n + 1) * P, :]
                             .rearrange("(c p) n -> p c n", p=P)).then_inc(sem(f"m_wo_in{n % 4}"), 16)

        def mla_pe(pe):
            pe.wait_ge(*reach("m_wa_in", 16))
            for c in range(DC):
                mm = pe.matmul(banks[:, 0, 0:224], xlnT[:, c, :], m_wa[:, c, :], start=(c == 0), stop=(c == 3))
            mm.then_inc(sem("m_latent"), 1)
            pe.wait_ge(*reach("m_a_ready", 1))
            for c in range(3):
                mm = pe.transpose(banks[:, 1, c * P:(c + 1) * P], m_a[:, c * P:(c + 1) * P], ident)
            mm.then_inc(sem("m_aT_full"), 1)
            pe.wait_ge(*reach("m_aT_ready", 1))
            pe.wait_ge(*reach("m_wqb_in", 16))
            pe.wait_ge(*reach("m_wkvb_in", 16))
            for n in range(QUADS):
                if n >= 2:
                    pe.wait_ge(*reach("m_q_ready", n - 1))
                    pe.wait_ge(*reach("m_nope", n - 1))
                    pe.wait_ge(*reach("m_kT_ready", n - 1))
                    pe.wait_ge(*reach("m_v_ready", n - 1))
                pe.matmul(banks[:, 2 + n % 2, :], m_aT[:, 0, :], m_wqb[:, n * 512:(n + 1) * 512],
                          start=True, stop=True).then_inc(sem("m_q_full"), 1)
                for h in range(4):
                    mm = pe.matmul(banks[0:64, 4 + n % 2, h * P:(h + 1) * P], m_kv_w[:, 4 * n + h, 0:64],
                                   m_aT[0:32, 1, :], start=True, stop=True)
                mm.then_inc(sem("m_k_full"), 1)
                pe.matmul(banks[:, 6 + n % 2, :], m_aT[0:32, 1, :], m_kv_w[:, 4 * n:4 * n + 4, 64:192],
                          start=True, stop=True).then_inc(sem("m_v_full"), 1)
            pe.wait_ge(*reach("m_q_ready", QUADS))
            pe.wait_ge(*reach("m_nope", QUADS))
            pe.wait_ge(*reach("m_kT_ready", QUADS))
            pe.wait_ge(*reach("m_v_ready", QUADS))

            def queries(n):
                if n >= 2:
                    pe.wait_ge(*reach("m_qT_ready", n - 1))
                for h in range(4):
                    mm = pe.transpose(banks[:, 2 + n % 2, h * P:(h + 1) * P], m_q[:, 4 * n + h, :], ident)
                mm.then_inc(sem("m_qT_full"), 1)

            def scores(n):
                pe.wait_ge(*reach("m_qT_ready", n + 1))
                if n == 0:
                    pe.wait_ge(*reach("m_kT_rotary", 1))
                elif n >= 2:
                    pe.wait_ge(*reach("m_masked", n - 1))
                for h in range(4):
                    mm = pe.matmul(banks[:, 4 + n % 2, h * P:(h + 1) * P], m_qT[:, 4 * n + h, :],
                                   m_kT[:, 4 * n + h, :], start=True, stop=True)
                mm.then_inc(sem("m_s_full"), 1)

            def turn_probs(n):
                pe.wait_ge(*reach("m_probs", n + 1))
                if n >= 2:
                    pe.wait_ge(*reach("m_pT_ready", n - 1))
                for h in range(4):
                    mm = pe.transpose(banks[:, 6 + n % 2, h * P:(h + 1) * P], m_q[:, 4 * n + h, :], ident)
                mm.then_inc(sem("m_pT_full"), 1)

            def outputs(n):
                pe.wait_ge(*reach("m_pT_ready", n + 1))
                if n:
                    pe.wait_ge(*reach("m_out_ready", n))
                for h in range(4):
                    mm = pe.matmul(banks[:, 0, h * P:(h + 1) * P], m_v[:, 4 * n + h, :],
                                   m_pT[:, 4 * n + h, :], start=True, stop=True)
                mm.then_inc(sem("m_out_full"), 1)

            def project(q):
                pe.wait_ge(*reach("m_out_ready", q + 1))
                for n in (2 * q, 2 * q + 1):
                    pe.wait_ge(sem(f"m_wo_in{n % 4}"), 16 * (n // 4 + 1))
                    for h in range(2):
                        mm = pe.matmul(banks[:, 1, :], m_out[:, 2 * n + h, :],
                                       m_ring[:, n % 4, h * 512:(h + 1) * 512],
                                       start=(n + h == 0), stop=(n == 15 and h == 1))
                    mm.then_inc(sem("m_wo_used"), 1)

            for n in range(QUADS + 5):
                for stage, lag in ((queries, 0), (scores, 1), (turn_probs, 3), (outputs, 4), (project, 5)):
                    if 0 <= n - lag < QUADS:
                        stage(n - lag)

        def mla_act(act):
            act.wait_ge(*reach("m_latent", 1))
            nc.scalar.activation(m_rot[:, 0], banks[:, 0, 0:P], ACT.Square,
                                 accum_out=ln[:, 12:13]).then_inc(sem("m_sq"), 1)
            nc.scalar.activation(m_rot[:, 1, 0, :], banks[:, 0, P:P + 32], ACT.Square,
                                 accum_out=ln[:, 13:14]).then_inc(sem("m_sq"), 1)
            act.wait_ge(*reach("m_aT_full", 1))
            act.wait_ge(*reach("m_lnw_in", 32))
            nc.scalar.activation(m_aT[:, 0, :], banks[:, 1, 0:P], ACT.Copy, scale=m_lnw[:, 0:1])
            nc.scalar.activation(m_aT[0:32, 1, :], banks[0:32, 1, P:2 * P], ACT.Copy, scale=m_lnw[0:32, 1:2])
            nc.scalar.activation(m_aT[64:128, 2, :], banks[64:128, 1, 2 * P:3 * P],
                                 ACT.Copy).then_inc(sem("m_aT_ready"), 1)
            for n in range(QUADS):
                act.wait_ge(*reach("m_q_full", n + 1))
                nc.scalar.activation(m_q[:, 4 * n:4 * n + 4, 0:64],
                                     banks[:, 2 + n % 2, :].rearrange("p (h n) -> p h n", h=4)[:, :, 0:64],
                                     ACT.Copy).then_inc(sem("m_nope"), 1)
                act.wait_ge(*reach("m_k_full", n + 1))
                nc.scalar.activation(quad(m_kT, n)[0:64, :], banks[0:64, 4 + n % 2, :],
                                     ACT.Copy).then_inc(sem("m_kT_ready"), 1)
                act.wait_ge(*reach("m_v_full", n + 1))
                nc.scalar.activation(quad(m_v, n), banks[:, 6 + n % 2, :], ACT.Copy).then_inc(sem("m_v_ready"), 1)
            for n in range(QUADS + 3):
                if n < QUADS:
                    act.wait_ge(*reach("m_qT_full", n + 1))
                    nc.scalar.activation(quad(m_qT, n), banks[:, 2 + n % 2, :],
                                         ACT.Copy).then_inc(sem("m_qT_ready"), 1)
                if 0 <= n - 1 < QUADS:
                    act.wait_ge(*reach("m_neg_max", n))
                    for h in range(4 * n - 4, 4 * n):
                        nc.scalar.activation(m_q[:, h, :], m_q[:, h, :], ACT.Exp, bias=m_st[:, 0, h:h + 1],
                                             accum_out=m_st[:, 1, h:h + 1]).then_inc(sem("m_exps"), 1)
                if 0 <= n - 3 < QUADS:
                    act.wait_ge(*reach("m_pT_full", n - 2))
                    nc.scalar.activation(quad(m_pT, n - 3), banks[:, 6 + (n - 3) % 2, :],
                                         ACT.Copy).then_inc(sem("m_pT_ready"), 1)

        def rotate(dve, even, odd, first, second, heads, count):
            t = [m_rot[:, k, 0:heads, :] for k in range(4)]
            for k, (v, w) in enumerate(((even, cos), (odd, sin), (odd, cos), (even, sin))):
                ins = nc.vector.tensor_tensor(t[k], v, per_head(w, heads, 32), ALU.mult)
            ins.then_inc(sem("m_turned"), 1)
            dve.wait_ge(*reach("m_turned", count + 1))
            nc.vector.tensor_tensor(first, t[0], t[1], ALU.subtract)
            return nc.vector.tensor_tensor(second, t[2], t[3], ALU.add)

        def mla_dve(dve):
            nc.vector.memset(m_a[:], 0.0).then_inc(sem("m_a_clear"), 1)
            dve.wait_ge(*reach("m_sq", 2))
            nc.vector.tensor_scalar(ln[:, 14:15], ln[:, 12:13], 1.0 / 128, RMS_EPS, ALU.mult, ALU.add)
            nc.vector.tensor_scalar(ln[:, 15:16], ln[:, 13:14], 1.0 / 32, RMS_EPS, ALU.mult,
                                    ALU.add).then_inc(sem("m_var"), 1)
            dve.wait_ge(*reach("m_var", 1))
            rsqrt_dve(dve, ln[:, 14:16], ln[:, 16:18], ln[:, 18:20])
            dve.wait_ge(*reach("m_a_clear", 1))
            nc.vector.tensor_scalar(m_a[:, 0:P], banks[:, 0, 0:P], ln[:, 16:17], None, ALU.mult)
            nc.vector.tensor_scalar(m_a[:, P:P + 32], banks[:, 0, P:P + 32], ln[:, 17:18], None, ALU.mult)
            rotate(dve, banks[:, 0, 160:224:2].unsqueeze(1), banks[:, 0, 161:224:2].unsqueeze(1),
                   m_a[:, 320:352].unsqueeze(1), m_a[:, 352:384].unsqueeze(1), 1, 0).then_inc(sem("m_a_ready"), 1)
            dve.wait_ge(*reach("m_a_ready", 1))
            for n in range(QUADS):
                dve.wait_ge(*reach("m_nope", n + 1))
                if n:
                    dve.wait_ge(*reach("m_q_ready", n))
                pe_part = banks[:, 2 + n % 2, :].rearrange("p (h n) -> p h n", h=4)
                rotate(dve, pe_part[:, :, 64:128:2], pe_part[:, :, 65:128:2], m_q[:, 4 * n:4 * n + 4, 64:96],
                       m_q[:, 4 * n:4 * n + 4, 96:128], 4, n + 1).then_inc(sem("m_q_ready"), 1)

            def inverse(n):
                dve.wait_ge(*reach("m_exps", 4 * n + 4))
                nc.vector.reciprocal(m_st[:, 2, 4 * n:4 * n + 4],
                                     m_st[:, 1, 4 * n:4 * n + 4]).then_inc(sem("m_inv"), 1)
                dve.wait_ge(*reach("m_inv", n + 1))
                nc.vector.tensor_tensor(m_q[:, 4 * n:4 * n + 4, :], m_q[:, 4 * n:4 * n + 4, :],
                                        per_column(m_st[:, 2, 4 * n:4 * n + 4], 4, P),
                                        ALU.mult).then_inc(sem("m_probs"), 1)

            def copy_out(n):
                dve.wait_ge(*reach("m_out_full", n + 1))
                nc.vector.tensor_copy(quad(m_out, n), banks[:, 0, :]).then_inc(sem("m_out_ready"), 1)

            for n in range(QUADS):
                dve.wait_ge(*reach("m_s_full", n + 1))
                nc.vector.scalar_tensor_tensor(
                    m_q[:, 4 * n:4 * n + 4, :], banks[:, 4 + n % 2, :].rearrange("p (h n) -> p h n", h=4), MLA_SCALE,
                    per_head(const[:, C_CAUSAL:C_CAUSAL + P], 4, P), ALU.mult, ALU.add).then_inc(sem("m_masked"), 1)
                dve.wait_ge(*reach("m_masked", n + 1))
                nc.vector.tensor_reduce(m_st[:, 0, 4 * n:4 * n + 4], m_q[:, 4 * n:4 * n + 4, :], AX.X, ALU.max,
                                        negate=True).then_inc(sem("m_neg_max"), 1)
                if n:
                    inverse(n - 1)
                if n >= 3:
                    copy_out(n - 3)
            inverse(QUADS - 1)
            for n in range(QUADS - 3, QUADS):
                copy_out(n)
            dve.wait_ge(*reach("m_wo_used", 16))
            nc.vector.tensor_tensor(x[:], x[:], banks[:, 1, :], ALU.add).then_inc(sem("m_x_sum"), 1)
            dve.wait_ge(*reach("m_x_sum", 1))

        def mla_pool(pool):
            pool.wait_ge(*reach("m_aT_ready", 1))
            nc.gpsimd.tensor_copy(m_kT[64:128, :, :],
                                  m_aT[64:128, 2, :].unsqueeze(1).broadcast_to([64, NHEAD, P])
                                  ).then_inc(sem("m_kT_rotary"), 1)

        EXPERT = (ACT.Tanh, ACT.Gelu, ACT.Silu)
        ratio_row = e_row[0:1, 8 + 3 * D:8 + 3 * D + P]

        def moe_sync(sp):
            sp.wait_ge(*reach("m_x_sum", 1))
            sp.dma_start(e_gw[:, :, 0:3], a["e_gw"][0:D, :].rearrange("(c p) n -> p c n", p=P)
                         ).then_inc(sem("e_small_in"), 16)
            sp.dma_start(e_row[0:1, 0:3], a["e_gw"][D:D + 1, :]).then_inc(sem("e_small_in"), 16)
            sp.dma_start(e_row[0:1, 4:7], a["e_gb"]).then_inc(sem("e_small_in"), 16)
            sp.dma_start(e_row[0:1, 8:8 + 3 * D], a["e_b2"]).then_inc(sem("e_small_in"), 16)
            sp.dma_start(e_b1[:], a["e_b1"]).then_inc(sem("e_small_in"), 16)
            for e in range(3):
                sp.dma_start(e_w1[:, e], a["e_w1"][e].rearrange("(c p) n -> p c n", p=P)).then_inc(sem(f"e_w1_in{e}"), 16)
            for e in range(3):
                sp.dma_start(e_w2[:, e], a["e_w2"][e].rearrange("(c p) n -> p c n", p=P)).then_inc(sem(f"e_w2_in{e}"), 16)

        def moe_pe(pe):
            for e in range(3):
                pe.wait_ge(sem(f"e_w1_in{e}"), 16)
                for f in range(DC):
                    for c in range(DC):
                        mm = pe.matmul(banks[:, 3 + e, f * P:(f + 1) * P], e_w1[:, e, c, f * P:(f + 1) * P],
                                       xlnT[:, c, :], start=(c == 0), stop=(c == 3))
                mm.then_inc(sem("e_pre"), 1)
                if e == 0:
                    pe.wait_ge(*reach("e_weighed", 1))
                    pe.matmul(banks[:, 0, 0:2], ones, e_s[:, 2:4], start=True, stop=True).then_inc(sem("e_means"), 1)
            pe.wait_ge(*reach("e_small_in", 80))
            for c in range(DC):
                pe.matmul(banks[:, 1, 0:3], xlnT[:, c, :], e_gw[:, c, 0:3], start=(c == 0), stop=False)
            pe.matmul(banks[:, 1, 0:3], ones[0:1, :], e_row[0:1, 4:7], start=False, stop=False)
            pe.wait_ge(*reach("e_ratio", 1))
            pe.matmul(banks[:, 1, 0:3], ratio_row, e_row[0:1, 0:3], start=False, stop=True).then_inc(sem("e_logits"), 1)
            for e in range(3):
                pe.wait_ge(*reach("e_hidden", 4 * (e + 1)))
                pe.wait_ge(sem(f"e_w2_in{e}"), 16)
                bank = (6, 7, 3)[e]
                for f in range(DC):
                    pe.matmul(banks[:, bank, :], e_act[:, e, f, :], e_w2[:, e, f, :], start=(f == 0), stop=False)
                pe.matmul(banks[:, bank, :], ones[0:1, :], e_row[0:1, 8 + e * D:8 + (e + 1) * D],
                          start=False, stop=True).then_inc(sem("e_out"), 1)
                if e == 0:
                    pe.wait_ge(*reach("e_choice", 1))
                    pe.matmul(banks[:, 2, 0:6], ones[0:1, :], e_s[0:1, 40:46], start=True,
                              stop=True).then_inc(sem("e_chosen"), 1)

        def moe_act(act):
            act.wait_ge(*reach("xln_ready", 3))
            nc.scalar.activation(e_act[:, 0].rearrange("p c n -> p (c n)"), xln[:], ACT.Abs,
                                 accum_out=e_s[:, 0:1]).then_inc(sem("e_abs"), 1)
            ln_act(act, 2)
            act.wait_ge(*reach("e_small_in", 80))
            act.wait_ge(*reach("e_abs", 1))

            def hidden(e):
                act.wait_ge(*reach("e_pre", e + 1))
                for f in range(DC):
                    nc.scalar.activation(e_act[:, e, f, :], banks[:, 3 + e, f * P:(f + 1) * P], EXPERT[e],
                                         bias=e_b1[:, 4 * e + f:4 * e + f + 1]).then_inc(sem("e_hidden"), 1)

            hidden(0)
            act.wait_ge(*reach("e_neg_max", 1))
            nc.scalar.activation(e_s[:, 8:11], banks[:, 1, 0:3], ACT.Exp, bias=e_s[:, 5:6],
                                 accum_out=e_s[:, 6:7]).then_inc(sem("e_exp"), 1)
            hidden(1)
            hidden(2)

        def moe_dve(dve):
            def then(ins):
                own_steps[0] += 1
                ins.then_inc(sem("dve_own"), 1)
                dve.wait_ge(*reach("dve_own", own_steps[0]))

            def tt(o, i0, i1, op):
                return nc.vector.tensor_tensor(e_s[:, o:o + 1], e_s[:, i0:i0 + 1], e_s[:, i1:i1 + 1], op)

            dve.wait_ge(*reach("e_abs", 1))
            nc.vector.tensor_scalar(e_s[:, 2:4], const[:, C_MEANS:C_MEANS + 2], e_s[:, 0:1], None,
                                    ALU.mult).then_inc(sem("e_weighed"), 1)
            dve.wait_ge(*reach("e_means", 1))
            then(nc.vector.tensor_scalar(e_s[:, 4:5], banks[:, 0, 1:2], 1e-8, None, ALU.add))
            then(nc.vector.reciprocal(e_s[:, 4:5], e_s[:, 4:5]))
            then(nc.vector.tensor_tensor(e_s[:, 4:5], e_s[:, 4:5], banks[:, 0, 0:1], ALU.mult))
            nc.vector.tensor_scalar(ratio_row, ones[0:1, :], e_s[0:1, 4:5], None, ALU.mult).then_inc(sem("e_ratio"), 1)
            dve.wait_ge(*reach("e_logits", 1))
            nc.vector.tensor_reduce(e_s[:, 5:6], banks[:, 1, 0:3], AX.X, ALU.max, negate=True
                                    ).then_inc(sem("e_neg_max"), 1)
            dve.wait_ge(*reach("e_exp", 1))
            then(nc.vector.reciprocal(e_s[:, 7:8], e_s[:, 6:7]))
            then(nc.vector.tensor_scalar(e_s[:, 12:15], e_s[:, 8:11], e_s[:, 7:8], None, ALU.mult))
            tt(20, 13, 12, ALU.is_gt), tt(21, 14, 12, ALU.is_gt)
            tt(22, 12, 13, ALU.is_ge), tt(23, 14, 13, ALU.is_gt)
            tt(24, 12, 14, ALU.is_ge)
            then(tt(25, 13, 14, ALU.is_ge))
            then(nc.vector.tensor_tensor(e_s[:, 28:31], e_s[:, 20:25:2], e_s[:, 21:26:2], ALU.add))
            nc.vector.tensor_scalar(e_s[:, 40:43], e_s[:, 28:31], 0.0, None, ALU.is_equal)
            nc.vector.tensor_scalar(e_s[:, 43:46], e_s[:, 28:31], 1.0, None, ALU.is_equal).then_inc(sem("e_choice"), 1)
            tt(16, 12, 13, ALU.max)
            then(tt(17, 12, 13, ALU.min))
            tt(32, 16, 14, ALU.max)
            then(tt(18, 16, 14, ALU.min))
            then(tt(33, 17, 18, ALU.max))
            then(tt(34, 32, 33, ALU.add))
            then(nc.vector.tensor_scalar(e_s[:, 34:35], e_s[:, 34:35], 1e-8, None, ALU.add))
            then(nc.vector.reciprocal(e_s[:, 35:36], e_s[:, 34:35]))
            then(nc.vector.tensor_scalar(e_s[:, 36:38], e_s[:, 32:34], e_s[:, 35:36], None, ALU.mult))
            dve.wait_ge(*reach("e_chosen", 1))
            then(nc.vector.tensor_scalar(e_s[:, 48:51], banks[:, 2, 0:3], e_s[:, 36:37], None, ALU.mult))
            then(nc.vector.scalar_tensor_tensor(e_s[:, 52:55], banks[:, 2, 3:6], e_s[:, 37:38], e_s[:, 48:51],
                                                ALU.mult, ALU.add))
            for e in range(3):
                dve.wait_ge(*reach("e_out", e + 1))
                ins = nc.vector.scalar_tensor_tensor(x[:], banks[:, (6, 7, 3)[e], :], e_s[:, 52 + e:53 + e], x[:],
                                                     ALU.mult, ALU.add)
                if e < 2:
                    then(ins)
            ins.then_inc(sem("e_x_sum"), 1)
            dve.wait_ge(*reach("e_x_sum", 1))

        s_items = [("dt", 18432, 128)] + [("conv", 16384 + 512 * m, 512) for m in range(4)]
        for b_ in range(16):
            s_items += [("conv", 8192 + 512 * b_, 512), ("gate", 512 * b_, 512)]
        n_in = len(s_items)
        upto = const[:, C_UPTO:C_UPTO + P]
        after = const[:, C_AFTER:C_AFTER + P]

        SEG_BANKS = (1, 2, 7)

        def ssm_sync(sp):
            sp.wait_ge(cross[1].sem("x_sum"), 8)
            for k, name in enumerate(("s_dtb", "s_alog", "s_D")):
                sp.dma_start(s_row[0:1, k * P:(k + 1) * P], a[name]).then_inc(sem("s_rows_in"), 16)
            sp.dma_start(s_cw[:], a["s_cw"]).then_inc(sem("s_cw_in"), 16)
            sp.dma_start(s_cbias[:], a["s_cb"]).then_inc(sem("s_cw_in"), 16)
            sp.dma_start(s_nw[:], a["s_nw"]).then_inc(sem("s_nw_in"), 16)
            for n in range(n_in + 16):
                if n == n_in + 4:
                    sp.wait_ge(*reach("s_mixed", 16))
                    ffn_sync(sp)
                if n >= NSLOT:
                    sp.wait_ge(*reach("s_used", n - NSLOT + 1))
                dst = s_w[:, n % NSLOT]
                if n < n_in:
                    _, col, w = s_items[n]
                    dst, src = dst[:, :, 0:w], a["s_in"][:, col:col + w]
                else:
                    src = a["s_out"][(n - n_in) * 512:(n - n_in + 1) * 512, :]
                sp.dma_start(dst, src.rearrange("(c p) n -> p c n", p=P)).then_inc(sem(f"s_w_in{n % NSLOT}"), 16)

        def ssm_pe(pe):
            at = [0]

            def weights():
                n = at[0]
                at[0] += 1
                pe.wait_ge(sem(f"s_w_in{n % NSLOT}"), 16 * (n // NSLOT + 1))
                return s_w[:, n % NSLOT]

            w = weights()
            for c in range(DC):
                mm = pe.matmul(banks[:, 0, 0:P], xlnT[:, c, :], w[:, c, 0:P], start=(c == 0), stop=False)
            mm.then_inc(sem("s_used"), 1)
            pe.wait_ge(*reach("s_rows_in", 48))
            pe.matmul(banks[:, 0, 0:P], ones[0:1, :], s_row[0:1, 0:P], start=False, stop=True)
            pe.matmul(banks[:, 0, P:3 * P], ones[0:1, :], s_row[0:1, P:3 * P], start=True,
                      stop=True).then_inc(sem("s_dt_full"), 1)

            def conv_proj(m):
                w = weights()
                if m >= 2:
                    pe.wait_ge(*reach("s_conv_done", m - 1))
                for t in range(4):
                    for c in range(DC):
                        mm = pe.matmul(banks[:, 3 + m % 2, t * P:(t + 1) * P], w[:, c, t * P:(t + 1) * P],
                                       xlnT[:, c, :], start=(c == 0), stop=(c == 3))
                mm.then_inc(sem("s_used"), 1)

            conv_proj(0)
            for m in range(4):
                for n in range(8 * m, 8 * m + 8):
                    pe.wait_ge(*reach(("s_seg_even", "s_seg_odd")[n % 2], n // 2 + 1))
                    if n >= 3:
                        pe.wait_ge(*reach("s_decay_ready", n - 2))
                    pe.matmul(banks[:, SEG_BANKS[n % 3], :], after, s_seg[:, n % 4].rearrange("p h n -> p (h n)"),
                              start=True, stop=True).then_inc(sem("s_seg_full"), 1)
                    if n % 8 == 3:
                        conv_proj(m + 1)
            pe.wait_ge(*reach("s_conv_act", 4))
            for q in range(2):
                for g in range(4 * q, 4 * q + 4):
                    mm = pe.matmul(banks[:, 5 + q, (g % 4) * P:(g % 4 + 1) * P], s_bT[:, g, :], s_cT[:, g, :],
                                   start=True, stop=True)
                mm.then_inc(sem("s_cb_full"), 1)

            def head_block(b):
                pe.wait_ge(*reach("s_conv_act", b + 5))
                if b == 0:
                    pe.wait_ge(*reach("s_cb_ready", 2))
                else:
                    pe.wait_ge(*reach("s_hs_ready", b))
                for t in range(4):
                    mm = pe.transpose(banks[:, 5, t * P:(t + 1) * P], s_chan[:, b % 2, t, :], ident)
                mm.then_inc(sem("s_hs_full"), 1)

            def mix_block(b):
                pe.wait_ge(*reach("s_mixed", b + 1))
                pe.wait_ge(*reach("s_hs_ready", b + 1))
                if b:
                    pe.wait_ge(*reach("s_y_read", b))
                for j in range(8):
                    mm = pe.matmul(banks[:, 7, 64 * j:64 * j + 64], s_mix[:, b % 2, j, :],
                                   s_hs[:, b % 2, 64 * j:64 * j + 64], start=True, stop=True)
                mm.then_inc(sem("s_y_full"), 1)

            for b in range(16):
                if b:
                    conv_proj(4 + b)
                if b >= 2:
                    mix_block(b - 2)
                w = weights()
                if b:
                    pe.wait_ge(*reach("s_gate_ready", b))
                else:
                    pe.wait_ge(*reach("s_cb_ready", 2))
                for c in range(DC):
                    mm = pe.matmul(banks[:, 6, :], xlnT[:, c, :], w[:, c, :], start=(c == 0), stop=(c == 3))
                mm.then_inc(sem("s_used"), 1)
                if b:
                    head_block(b - 1)
            mix_block(14)
            head_block(15)
            mix_block(15)
            for b in range(16):
                pe.wait_ge(*reach("s_scaled", b + 1))
                if b >= 2:
                    pe.wait_ge(*reach("s_gT_ready", b - 1))
                for t in range(4):
                    mm = pe.transpose(banks[:, 1 + b % 2, t * P:(t + 1) * P],
                                      s_g[:, (4 * b + t) * P:(4 * b + t + 1) * P], ident)
                mm.then_inc(sem("s_gT_full"), 1)
                if b:
                    out_block(pe, b - 1, weights())
            out_block(pe, 15, weights())

        def out_block(pe, b, w):
            pe.wait_ge(*reach("s_gT_ready", b + 1))
            for t in range(4):
                mm = pe.matmul(banks[:, 0, :], s_chan[:, b % 2, t, :], w[:, t, :], start=(b + t == 0),
                               stop=(b == 15 and t == 3))
            mm.then_inc(sem("s_used"), 1)

        used_by_conv = [k + 1 for k, (kind, _, _) in enumerate(s_items) if kind == "conv"]
        used_by_gate = [k + 1 for k, (kind, _, _) in enumerate(s_items) if kind == "gate"]
        conv_tile = [64, 68, 72, 76] + [4 * b_ for b_ in range(16)]

        def ssm_act(act):
            act.wait_ge(*reach("s_dt_full", 1))
            nc.scalar.activation(s_dt[:, 4, :], banks[:, 0, 0:P], ACT.Abs).then_inc(sem("s_dt_abs"), 1)
            act.wait_ge(*reach("s_dt_abs", 1))
            nc.scalar.activation(s_dt[:, 4, :], s_dt[:, 4, :], ACT.Exp, scale=-1.0).then_inc(sem("s_dt_exp"), 1)
            nc.scalar.activation(s_dt[:, 1, :], banks[:, 0, P:2 * P], ACT.Exp).then_inc(sem("s_a_exp"), 1)
            act.wait_ge(*reach("s_dt_u", 1))
            nc.scalar.activation(s_dt[:, 6, :], s_dt[:, 5, :], ACT.Ln).then_inc(sem("s_dt_ln"), 1)

            def conv_first(m):
                act.wait_ge(*reach("s_used", used_by_conv[m]))
                if m == 0:
                    act.wait_ge(*reach("s_cw_in", 32))
                if m >= 2:
                    act.wait_ge(*reach("s_conv_act", m - 1))
                for t in range(4):
                    k = conv_tile[m] + t
                    ins = nc.scalar.activation(s_conv[:, m % 2, t, :], banks[:, 3 + m % 2, t * P:(t + 1) * P],
                                               ACT.Identity, bias=s_cbias[:, k:k + 1], scale=s_cw[:, k, 3:4])
                ins.then_inc(sem("s_conv_first"), 1)

            def conv_tanh(m):
                act.wait_ge(*reach("s_conv_done", m + 1))
                if m >= 2:
                    act.wait_ge(*reach("s_conv_act", m - 1))
                nc.scalar.activation(s_tanh[:, m % 2], s_conv[:, m % 2], ACT.Tanh, scale=0.5
                                     ).then_inc(sem("s_conv_tanh"), 1)

            conv_first(0)
            for m in range(4):
                for n in range(8 * m, 8 * m + 8):
                    act.wait_ge(*reach("s_seg_full", n + 1))
                    nc.scalar.activation(s_decay[:, 4 * n:4 * n + 4, :].rearrange("p h n -> p (h n)"),
                                         banks[:, SEG_BANKS[n % 3], :], ACT.Exp).then_inc(sem("s_decay_ready"), 1)
                    if n % 8 == 4:
                        conv_first(m + 1)
                    if n % 8 == 6:
                        conv_tanh(m)

            def hs_copy(b):
                act.wait_ge(*reach("s_hs_full", b + 1))
                if b >= 2:
                    act.wait_ge(*reach("s_y_read", b - 1))
                nc.scalar.activation(s_hs[:, b % 2, :], banks[:, 5, :], ACT.Copy, scale=0.5
                                     ).then_inc(sem("s_hs_ready"), 1)

            def square(b):
                act.wait_ge(*reach("s_g_ready", b + 1))
                if b:
                    act.wait_ge(*reach("s_squares", b))
                nc.scalar.activation(s_sq[:], s_g[:, b * 512:(b + 1) * 512], ACT.Square,
                                     accum_out=s_var[:, 0, b:b + 1]).then_inc(sem("s_squares"), 1)

            for b in range(17):
                if b >= 2:
                    hs_copy(b - 2)
                if b:
                    act.wait_ge(*reach("s_used", used_by_gate[b - 1]))
                    if b >= 3:
                        act.wait_ge(*reach("s_g_ready", b - 2))
                    nc.scalar.activation(s_gate[:, (b - 1) % 2, :], banks[:, 6, :], ACT.Tanh, scale=0.5
                                         ).then_inc(sem("s_gate_tanh"), 1)
                if b >= 3:
                    square(b - 3)
                if b:
                    conv_tanh(3 + b)
                    if b < 16:
                        conv_first(4 + b)
            hs_copy(15)
            square(14)
            act.wait_ge(*reach("s_nw_in", 16))
            for b in range(16):
                if b == 2:
                    square(15)
                if b == 14:
                    act.wait_ge(*reach("f_w_in", 16))
                    nc.scalar.activation(f_sign[:], f_w[:], ACT.Sign).then_inc(sem("f_sign_ready"), 1)
                act.wait_ge(*reach("s_gT_full", b + 1))
                if b >= 2:
                    act.wait_ge(*reach("s_used", n_in + b - 1))
                for t in range(4):
                    ins = nc.scalar.activation(s_chan[:, b % 2, t, :], banks[:, 1 + b % 2, t * P:(t + 1) * P],
                                               ACT.Copy, scale=s_nw[:, 4 * b + t:4 * b + t + 1])
                ins.then_inc(sem("s_gT_ready"), 1)

        def ssm_pool(pool):
            pool.wait_ge(*reach("s_dA_ready", 1))
            for n in range(0, 32, 2):
                if n >= 4:
                    pool.wait_ge(*reach("s_seg_full", n - 3))
                nc.gpsimd.tensor_tensor(s_seg[:, n % 4], per_head(upto, 4, P),
                                        per_column(s_dt[:, 2, 4 * n:4 * n + 4], 4, P),
                                        ALU.mult).then_inc(sem("s_seg_even"), 1)

        def ssm_dve(dve):
            def then(ins):
                own_steps[0] += 1
                ins.then_inc(sem("dve_own"), 1)
                dve.wait_ge(*reach("dve_own", own_steps[0]))

            d = s_dt
            dve.wait_ge(*reach("s_dt_exp", 1))
            nc.vector.tensor_scalar(d[:, 5, :], d[:, 4, :], 1.0, None, ALU.add).then_inc(sem("s_dt_u"), 1)
            dve.wait_ge(*reach("s_dt_u", 1))
            then(nc.vector.tensor_scalar(d[:, 7, :], d[:, 5, :], -1.0, None, ALU.add))
            then(nc.vector.tensor_scalar(d[:, 2, :], d[:, 7, :], 0.0, None, ALU.is_equal))
            then(nc.vector.tensor_tensor(d[:, 7, :], d[:, 7, :], d[:, 2, :], ALU.add))
            then(nc.vector.reciprocal(d[:, 7, :], d[:, 7, :]))
            dve.wait_ge(*reach("s_dt_ln", 1))
            then(nc.vector.tensor_tensor(d[:, 7, :], d[:, 7, :], d[:, 6, :], ALU.mult))
            then(nc.vector.tensor_tensor(d[:, 7, :], d[:, 7, :], d[:, 2, :], ALU.add))
            then(nc.vector.tensor_tensor(d[:, 7, :], d[:, 7, :], d[:, 4, :], ALU.mult))
            then(nc.vector.scalar_tensor_tensor(d[:, 0, :], banks[:, 0, 0:P], 0.0, d[:, 7, :], ALU.max, ALU.add))
            then(nc.vector.tensor_scalar(d[:, 0, :], d[:, 0, :], 100.0, 0.0, ALU.min, ALU.max))
            dve.wait_ge(*reach("s_a_exp", 1))
            nc.vector.scalar_tensor_tensor(d[:, 2, :], d[:, 0, :], -1.0, d[:, 1, :], ALU.mult, ALU.mult
                                           ).then_inc(sem("s_dA_ready"), 1)
            dve.wait_ge(*reach("s_dA_ready", 1))
            then(nc.vector.tensor_copy(d[:, 3, :], banks[:, 0, 2 * P:3 * P]))

            def taps(m, which=range(1, 4)):
                for k in which:
                    if k == 1:
                        dve.wait_ge(*reach("s_conv_first", m + 1))
                    else:
                        dve.wait_ge(*reach("s_tap", 2 * m + k - 1))
                    for t in range(4):
                        ins = nc.vector.scalar_tensor_tensor(
                            s_conv[:, m % 2, t, k:P], banks[:, 3 + m % 2, t * P:(t + 1) * P - k],
                            s_cw[:, conv_tile[m] + t, 3 - k:4 - k], s_conv[:, m % 2, t, k:P], ALU.mult, ALU.add)
                    ins.then_inc(sem("s_tap" if k < 3 else "s_conv_done"), 1)

            def silu(m):
                dve.wait_ge(*reach("s_conv_tanh", m + 1))
                dst = (s_bT[:, 4 * m:4 * m + 4, :] if m < 2 else s_cT[:, 4 * m - 8:4 * m - 4, :] if m < 4
                       else s_chan[:, m % 2])
                if m >= 6:
                    dve.wait_ge(*reach("s_hs_full", m - 5))
                nc.vector.scalar_tensor_tensor(dst.rearrange("p t n -> p (t n)"),
                                               s_tanh[:, m % 2].rearrange("p t n -> p (t n)"), 1.0,
                                               s_conv[:, m % 2].rearrange("p t n -> p (t n)"), ALU.add,
                                               ALU.mult).then_inc(sem("s_conv_act"), 1)

            for m in range(4):
                for n in range(8 * m + 1, 8 * m + 8, 2):
                    if n >= 4:
                        dve.wait_ge(*reach("s_seg_full", n - 3))
                    nc.vector.tensor_tensor(s_seg[:, n % 4], per_head(upto, 4, P),
                                            per_column(d[:, 2, 4 * n:4 * n + 4], 4, P),
                                            ALU.mult).then_inc(sem("s_seg_odd"), 1)
                    if n % 8 == 1 and m:
                        silu(m - 1)
                    if n % 8 < 7:
                        taps(m, (n % 8 // 2 + 1,))
            silu(3)
            for q in range(2):
                dve.wait_ge(*reach("s_cb_full", q + 1))
                nc.vector.scalar_tensor_tensor(
                    s_cb[:, 4 * q:4 * q + 4, :], banks[:, 5 + q, :].rearrange("p (g n) -> p g n", g=4), 0.25,
                    per_head(upto, 4, P), ALU.mult, ALU.mult).then_inc(sem("s_cb_ready"), 1)
            dve.wait_ge(*reach("s_cb_ready", 2))
            dve.wait_ge(*reach("s_decay_ready", 32))

            def mix(b):
                if b >= 2:
                    dve.wait_ge(*reach("s_y_full", b - 1))
                for j in range(8):
                    h = 8 * b + j
                    ins = nc.vector.scalar_tensor_tensor(s_mix[:, b % 2, j, :], s_decay[:, h, :], d[:, 0, h:h + 1],
                                                         s_cb[:, b // 2, :], ALU.mult, ALU.mult)
                ins.then_inc(sem("s_mixed"), 1)

            def finish(b):
                dve.wait_ge(*reach("s_hs_ready", b + 1))
                nc.vector.tensor_tensor(s_y[:, b % 2, :].rearrange("p (h n) -> p h n", h=8),
                                        s_hs[:, b % 2, :].rearrange("p (h n) -> p h n", h=8),
                                        per_column(d[:, 3, 8 * b:8 * b + 8], 8, 64), ALU.mult
                                        ).then_inc(sem("s_skip"), 1)
                dve.wait_ge(*reach("s_skip", b + 1))
                dve.wait_ge(*reach("s_y_full", b + 1))
                nc.vector.tensor_tensor(s_y[:, b % 2, :], s_y[:, b % 2, :], banks[:, 7, :], ALU.add
                                        ).then_inc(sem("s_y_read"), 1)
                dve.wait_ge(*reach("s_y_read", b + 1))
                nc.vector.scalar_tensor_tensor(s_g[:, b * 512:(b + 1) * 512], s_y[:, b % 2, :], 0.5,
                                               s_gate[:, b % 2, :], ALU.mult, ALU.mult).then_inc(sem("s_g_ready"), 1)

            for b in range(16):
                taps(4 + b)
                dve.wait_ge(*reach("s_gate_tanh", b + 1))
                nc.vector.scalar_tensor_tensor(s_gate[:, b % 2, :], s_gate[:, b % 2, :], 1.0, banks[:, 6, :],
                                               ALU.add, ALU.mult).then_inc(sem("s_gate_ready"), 1)
                mix(b)
                silu(4 + b)
                if b:
                    finish(b - 1)

            def roots_of(g0, g1):
                dve.wait_ge(*reach("s_squares", 2 * g1))
                v = s_var[:, 1, g0:g1]
                then(nc.vector.tensor_tensor(v, s_var[:, 0, 2 * g0:2 * g1:2], s_var[:, 0, 2 * g0 + 1:2 * g1:2],
                                             ALU.add))
                nc.vector.tensor_scalar(v, v, 1.0 / 1024, EPS, ALU.mult, ALU.add).then_inc(sem("s_var_ready"), 1)
                rsqrt_dve(dve, v, s_var[:, 2, g0:g1], s_var[:, 3, g0:g1])

            def scale(b):
                nc.vector.tensor_scalar(s_g[:, b * 512:(b + 1) * 512], s_g[:, b * 512:(b + 1) * 512],
                                        s_var[:, 2, b // 2:b // 2 + 1], None, ALU.mult).then_inc(sem("s_scaled"), 1)

            roots_of(0, 7)
            scale(0)
            scale(1)
            finish(15)
            for b in range(2, 6):
                scale(b)
            roots_of(7, 8)
            for b in range(6, 16):
                scale(b)
            dve.wait_ge(*reach("s_used", n_in + 16))
            nc.vector.tensor_tensor(x[:], x[:], banks[:, 0, :], ALU.add).then_inc(sem("s_x_sum"), 1)
            dve.wait_ge(*reach("s_x_sum", 1))

        def ffn_sync(sp):
            sp.dma_start(f_gw[:], a["f_gw"].rearrange("(c p) n -> p c n", p=P)).then_inc(sem("f_gw_in"), 16)
            sp.dma_start(f_w[:], a["f_w"].rearrange("(c p) n -> p c n", p=P)).then_inc(sem("f_w_in"), 16)
            sp.dma_start(f_scale[:, 0, :], a["f_in"]).then_inc(sem("f_scale_in"), 16)
            sp.dma_start(f_scale[:, 1, :], a["f_out"]).then_inc(sem("f_scale_in"), 16)
            sp.dma_start(f_bias[:], a["f_b"].broadcast_to([P, D])).then_inc(sem("f_bias_in"), 16)

        def ffn_pe(pe):
            pe.wait_ge(*reach("f_gw_in", 16))
            for c in range(DC):
                mm = pe.matmul(banks[:, 0, 0:8], xlnT[:, c, :], f_gw[:, c, :], start=(c == 0), stop=(c == 3))
            mm.then_inc(sem("f_logits"), 1)
            pe.wait_ge(*reach("f_routing", 1))
            pe.transpose(banks[0:8, 1, 0:P], f_r[:, 8:16], ident).then_inc(sem("f_rT_full"), 1)
            pe.wait_ge(*reach("f_rT_ready", 1))
            pe.wait_ge(*reach("f_scale_in", 32))
            for k in range(2):
                pe.matmul(banks[:, 2 + k, :], f_rT[:], f_scale[:, k, :], start=True, stop=True
                          ).then_inc(sem("f_scales"), 1)
            pe.wait_ge(*reach("f_scaled", 1))
            for c in range(DC):
                mm = pe.transpose(banks[:, 4, c * P:(c + 1) * P], f_xs[:, c * P:(c + 1) * P], ident)
            mm.then_inc(sem("f_xT_full"), 1)
            pe.wait_ge(*reach("f_xT_ready", 1))
            for c in range(DC):
                mm = pe.matmul(banks[:, 5, :], f_xT[:, c, :], f_sign[:, c, :], start=(c == 0), stop=(c == 3))
            mm.then_inc(sem("f_out_full"), 1)

        def ffn_act(act):
            act.wait_ge(*reach("f_neg_max", 1))
            nc.scalar.activation(f_r[:, 0:8], banks[:, 0, 0:8], ACT.Exp, bias=f_r[:, 16:17],
                                 accum_out=f_r[:, 17:18]).then_inc(sem("f_exp"), 1)
            act.wait_ge(*reach("f_rT_full", 1))
            nc.scalar.activation(f_rT[:], banks[0:8, 1, 0:P], ACT.Copy).then_inc(sem("f_rT_ready"), 1)
            act.wait_ge(*reach("f_scales", 2))
            nc.scalar.activation(f_os[:], banks[:, 3, :], ACT.Copy).then_inc(sem("f_os_ready"), 1)
            act.wait_ge(*reach("f_xT_full", 1))
            act.wait_ge(*reach("f_sign_ready", 1))
            nc.scalar.activation(f_xT[:].rearrange("p c n -> p (c n)"), banks[:, 4, :],
                                 ACT.Copy).then_inc(sem("f_xT_ready"), 1)

        def ffn_dve(dve):
            dve.wait_ge(*reach("f_logits", 1))
            nc.vector.tensor_reduce(f_r[:, 16:17], banks[:, 0, 0:8], AX.X, ALU.max, negate=True
                                    ).then_inc(sem("f_neg_max"), 1)
            dve.wait_ge(*reach("f_exp", 1))
            nc.vector.reciprocal(f_r[:, 18:19], f_r[:, 17:18]).then_inc(sem("f_inv"), 1)
            dve.wait_ge(*reach("f_inv", 1))
            nc.vector.tensor_scalar(f_r[:, 8:16], f_r[:, 0:8], f_r[:, 18:19], None, ALU.mult
                                    ).then_inc(sem("f_routing"), 1)
            dve.wait_ge(*reach("f_scales", 1))
            nc.vector.tensor_tensor(f_xs[:], xln[:], banks[:, 2, :], ALU.mult).then_inc(sem("f_scaled"), 1)
            dve.wait_ge(*reach("f_bias_in", 16))
            nc.vector.tensor_tensor(x[:], x[:], f_bias[:], ALU.add).then_inc(sem("f_biased"), 1)
            dve.wait_ge(*reach("f_out_full", 1))
            dve.wait_ge(*reach("f_os_ready", 1))
            dve.wait_ge(*reach("f_biased", 1))
            nc.vector.tensor_tensor(f_os[:], f_os[:], banks[:, 5, :], ALU.mult).then_inc(sem("f_y"), 1)
            dve.wait_ge(*reach("f_y", 1))
            nc.vector.tensor_tensor(x[:], x[:], f_os[:], ALU.add).then_inc(sem("f_x_sum"), 1)

        block = ctx.enter_context(nc.Block())

        @block.sync
        def _(sp):
            sp.dma_start(x[:], a["x"]).then_inc(sem("x_in"), 16)
            sp.dma_start(const[:], a["const"]).then_inc(sem("const_in"), 16)
            cross[0].sync(sp)
            mla_sync(sp)
            moe_sync(sp)
            sp.dma_start(bias_q[:], a["bq1"]).then_inc(sem("biases_in"), 16)
            sp.dma_start(bias_k[:], a["bkv1"][:, 0:8]).then_inc(sem("biases_in"), 16)
            sp.dma_start(bias_v[:], a["bkv1"][:, 8:16]).then_inc(sem("biases_in"), 16)
            cross[1].sync(sp)
            ssm_sync(sp)
            sp.wait_ge(*reach("f_x_sum", 1))
            sp.dma_start(out, x[:]).then_inc(sem("out_written"), 16)
            sp.wait_ge(*reach("out_written", 16))

        @block.gpsimd
        def _(pool):
            nc.gpsimd.memset(minus_half[:], -0.5).then_inc(sem("half_set"), 1)
            pool.wait_ge(*reach("half_set", 1))
            ln_pool(pool, 0)
            ln_pool(pool, 1)
            rsqrt_pool(pool, "m_var", 1, ln[:, 14:16], ln[:, 16:18])
            mla_pool(pool)
            for n in range(2, 5):
                ln_pool(pool, n)
            ssm_pool(pool)
            rsqrt_pool(pool, "s_var_ready", 1, s_var[:, 1, 0:7], s_var[:, 2, 0:7])
            rsqrt_pool(pool, "s_var_ready", 2, s_var[:, 1, 7:8], s_var[:, 2, 7:8])
            ln_pool(pool, 5)

        @block.tensor
        def _(pe):
            pe.wait_ge(*reach("const_in", 16))
            ln_pe(pe, 0)
            cross[0].pe(pe)
            ln_pe(pe, 1)
            mla_pe(pe)
            ln_pe(pe, 2)
            moe_pe(pe)
            ln_pe(pe, 3)
            cross[1].pe(pe)
            ln_pe(pe, 4)
            ssm_pe(pe)
            ln_pe(pe, 5)
            ffn_pe(pe)

        @block.scalar
        def _(act):
            ln_act(act, 0)
            ctx_act(act)
            cross[0].act(act)
            ln_act(act, 1)
            mla_act(act)
            moe_act(act)
            ln_act(act, 3)
            act.wait_ge(*reach("biases_in", 48))
            cross[1].act(act)
            ln_act(act, 4)
            ssm_act(act)
            ln_act(act, 5)
            ffn_act(act)

        @block.vector
        def _(dve):
            dve.wait_ge(*reach("x_in", 16))
            dve.wait_ge(*reach("const_in", 16))
            ln_dve(dve, 0)
            ctx_dve(dve)
            cross[0].dve(dve)
            ln_dve(dve, 1)
            mla_dve(dve)
            ln_dve(dve, 2)
            moe_dve(dve)
            ln_dve(dve, 3)
            dve.wait_ge(*reach("biases_in", 48))
            nc.vector.tensor_scalar(bias_q[:], bias_q[:], ATT_SCALE, None, ALU.mult).then_inc(sem("bq_scaled"), 1)
            dve.wait_ge(*reach("bq_scaled", 1))
            cross[1].dve(dve)
            ln_dve(dve, 4)
            ssm_dve(dve)
            ln_dve(dve, 5)
            ffn_dve(dve)


_OUT = (1, 128, 512)


def kernel(**inputs):
    import numpy as np
    import concourse.bacc as bacc
    from concourse.bass_utils import run_bass_kernel_spmd

    t, arrays = _layout(np, inputs)
    nc = bacc.Bacc("TRN2", target_bir_lowering=False, num_devices=1)
    aps = {n: nc.dram_tensor(n, v.shape, mybir.dt.from_np(v.dtype), kind="ExternalInput").ap()
           for n, v in arrays.items()}
    out = nc.dram_tensor("y", (128, 512), mybir.dt.float32, kind="ExternalOutput").ap()
    build(nc, aps, out)
    r = run_bass_kernel_spmd(nc, [arrays], core_ids=[0])
    return r.results[0]["y"].reshape(_OUT)


def _layout(np, i):
    c = np.ascontiguousarray
    i = {k: np.asarray(v) for k, v in i.items()}
    ar = {
        "x": c(i["x"][0]),
        "ctxT": c(i["ctx_4096"][0].T),
        "const": _constants(np),
        "Wq0": i["L0_xattn_Wq"], "Wk0": i["L0_xattn_Wk"], "Wv0": i["L0_xattn_Wv"], "Wo0": i["L0_xattn_Wo"],
        "Wq1": i["L1_xattn_Wq"], "Wk1": c(i["L1_xattn_Wkv"][:, :1024]), "Wv1": c(i["L1_xattn_Wkv"][:, 1024:]),
        "Wo1": i["L1_xattn_Wo"], "bq1": c(i["L1_xattn_bq"].reshape(32, 128).T),
        "bkv1": c(i["L1_xattn_bkv"].reshape(16, 128).T), "bo1": c(i["L1_xattn_bo"].reshape(1, 512)),
        "m_wa": c(np.concatenate([i["L0_attn_wq_a"], i["L0_attn_wkv_a"]]).T),
        "m_lnq": c(i["L0_attn_q_a_ln_w"].reshape(128, 1)), "m_lnkv": c(i["L0_attn_kv_a_ln_w"].reshape(32, 1)),
        "m_wqb": c(i["L0_attn_wq_b"].T), "m_wkvb": c(i["L0_attn_wkv_b"].T), "m_wo": c(i["L0_attn_wo"].T),
        "e_gw": i["L0_ffn_gate_w"], "e_gb": c(i["L0_ffn_gate_b"].reshape(1, 3)),
        "e_w1": i["L0_ffn_w1"], "e_b1": c(i["L0_ffn_b1"].reshape(12, 128).T),
        "e_w2": i["L0_ffn_w2"], "e_b2": c(i["L0_ffn_b2"].reshape(1, 1536)),
        "s_in": c(i["L1_attn_in_proj_w"].T),
        "s_cw": c(i["L1_attn_conv_w"].reshape(80, 128, 4).transpose(1, 0, 2)),
        "s_cb": c(i["L1_attn_conv_b"].reshape(80, 128).T),
        "s_dtb": c(i["L1_attn_dt_bias"].reshape(1, 128)), "s_alog": c(i["L1_attn_A_log"].reshape(1, 128)),
        "s_D": c(i["L1_attn_D"].reshape(1, 128)), "s_nw": c(i["L1_attn_norm_w"].reshape(64, 128).T),
        "s_out": c(i["L1_attn_out_proj_w"].T),
        "f_w": c(i["L1_ffn_weight"].T), "f_b": c(i["L1_ffn_bias"].reshape(1, 512)),
        "f_gw": c(i["L1_ffn_gate_w"].T), "f_in": i["L1_ffn_in_channel_scale"],
        "f_out": i["L1_ffn_out_channel_scale"],
    }
    return i, {k: c(v) for k, v in ar.items()}


def _constants(np):
    import math
    n = np.arange(128)
    k, m = n[:, None], n[None, :]
    dim, base, factor, orig = 64, 10000.0, 128.0, 1024
    turn = lambda r: dim * math.log(orig / (r * 2 * math.pi)) / (2 * math.log(base))
    low, high = max(math.floor(turn(32.0)), 0), min(math.ceil(turn(1.0)), dim - 1)
    hi = high + 0.001 if low == high else float(high)
    keep = 1.0 - np.clip((np.arange(dim // 2, dtype=np.float32) - low) / (hi - low), 0.0, 1.0)
    extra = 1.0 / base ** (np.arange(0, dim, 2, dtype=np.float32) / dim)
    freq = extra / factor * (1.0 - keep) + extra * keep
    angle = np.outer(np.arange(128, dtype=np.float32), freq)
    vision = int(128 * 0.3)
    return np.concatenate([
        (k == m), np.ones((128, 128)), (k <= m), (k > m), np.where(m <= k, 0.0, MASKED),
        np.cos(angle), np.sin(angle),
        (k >= vision) / ((128 - vision) * 512.0), (k < vision) / (vision * 512.0),
    ], axis=1).astype(np.float32)
```

```python
import math
from contextlib import ExitStack

import concourse.bass as bass
from concourse import mybir

ALU = mybir.AluOpType
ACT = mybir.ActivationFunctionType
AX = mybir.AxisListType
F32 = mybir.dt.float32
F32R = mybir.dt.float32r

P = 128
TOK = 128
D = 512
DC = D // P
CTX = 2048
NHEAD = 32
EPS = 1e-5
RMS_EPS = 1e-6
ATT_SCALE = 1.0 / float(P) ** 0.5
MASKED = -1.0e30
C_IDENT, C_ONES, C_UPTO, C_AFTER, C_CAUSAL, C_COS, C_SIN, C_MEANS = 0, 128, 256, 384, 512, 640, 672, 704
C_WIDTH = 706


class Tally:

    def __init__(self, before=()):
        self.before, self.count = dict(before), {}

    def add(self, name, by=1):
        self.count[name] = self.count.get(name, 0) + by

    def local(self, name):
        return self.count.get(name, 0)

    def at(self, name, back=0):
        return self.before.get(name, 0) + self.count.get(name, 0) - back


class Nth:

    def __init__(self, half, odd):
        self.half, self.odd = half, odd

    @staticmethod
    def of(n):
        return Nth(n // 2, n % 2)

    @property
    def value(self):
        return self.half * 2 + self.odd

    def __add__(self, k):
        carry, odd = divmod(self.odd + k, 2)
        return Nth(self.half + carry if carry else self.half, odd)

    def __sub__(self, k):
        return self + -k


def part(start, size):
    return bass.ds(start, size)


RING = 5
LAG = 2


FILL = {
    2: dict(keys=3, exps=0, rest=(1.3, 1.3), rest_keys=(1.34, 1.3),
            split_keys=1, split_values=2, output=4, queries=3, turn=5),
    1: dict(keys=4, exps=0.2, rest=(1.83, 1.3), rest_keys=(2.15, 1.91),
            split_keys=2, split_values=1, output=3, queries=4, turn=5),
}


def attention_plan(kv_groups, key_tiles, cuts):
    pairs = 4 * kv_groups
    nb = len(cuts)
    steps = (key_tiles + 1) // 2
    last_key = [sum(cuts[:c + 1]) for c in range(nb)]
    fill = FILL[kv_groups]
    cost = {"K": fill["keys"], "S": 1, "EXP": fill["exps"]}

    def scores_of(p, keys, exps_before):
        first = [("S", p, 0, c) for c in range(nb)]
        if keys:
            k = [("K", c) for c in range(nb)]
            first = k[:3] + [e for c in range(3, nb) for e in (first[c - 3], k[c])] + first[nb - 3:]
        before, side = list(exps_before), []
        for e in first:
            n = 2 if e[0] == "K" else 1
            side += before[:n] + [e]
            before = before[n:]
            if e[0] == "S":
                side.append(("MAX", *e[1:]))
        side += before + [("NEG", p, 0), ("REST", 0), ("EXP", p, 0, 0)]
        for c in range(nb):
            if c + 1 < nb:
                side.append(("EXP", p, 0, c + 1))
            side += [("S", p, 1, c), ("MAX", p, 1, c)]
        return side + [("NEG", p, 1), ("REST", 1)]

    def exps(p):
        return [("EXP", p, 1, c) for c in range(nb)] + [("RD", p)]

    def weave(main, side, needed=()):
        out, side = [], list(side)
        rests = [e for e in side if e[0] == "REST"]
        work = sum(cost.get(e[0], 0) for e in side)
        step = work / (len(main) - len(rests))
        rest = [step * r for r in fill["rest_keys" if any(e[0] == "K" for e in side) else "rest"]]
        total, spent, n_exp = work + sum(rest[e[1]] for e in rests), 0, 0
        for k, (before, after) in enumerate(main):
            share = []
            while side and (spent < (k + 1) / len(main) * total - 1e-9 or side[0][0] in ("MAX", "NEG", "RD")
                            or (needed and n_exp < needed[k])):
                e = side.pop(0)
                n_exp += e[0] == "EXP"
                if e[0] == "REST":
                    spent += rest[e[1]]
                else:
                    spent += cost.get(e[0], 0)
                    share.append(e)
            lead = next((i for i, e in enumerate(share) if e[0] in ("NEG", "K")), len(share))
            early = [e for e in share[:lead] if e[0] == "EXP"]
            out += early + before + after + [e for e in share if e not in early]
        return out + [e for e in side if e[0] != "REST"]

    needed = [1 + next(c for c in range(nb) if min(256 * k + 256, last_key[-1]) <= last_key[c])
              for k in range(steps)]

    def turn(first, last):
        o = []
        for p in range(pairs):
            more = p < pairs - 1 or not last
            more2 = p + 2 < pairs or not last
            keys = (p + 1) % (2 * kv_groups) == 0 and more
            keys2 = (p + 2) % (2 * kv_groups) == 0 and more2
            values = p == pairs - 1 and not last
            main = []
            for k in range(steps):
                before, after = [("T", p, k)], []
                if k >= LAG:
                    before.append(("PV", p, k - LAG))
                    if values:
                        before.append(("V", k - LAG))
                elif p > 0 or not first:
                    before.insert(0 if k == 0 else 1, ("PV", (p - 1) % pairs, steps - LAG + k))
                    if p == 0:
                        before.insert(1 if k == 0 else 2, ("V", steps - LAG + k))
                    if k == LAG - 1:
                        before.append(("OUT", (p - 1) % pairs))
                if k == fill["output"] and p % 4 == 0 and (p > 0 or not first):
                    before.append(("WO",))
                if k == fill["split_keys"] and keys2:
                    before.append(("WK",))
                if k == fill["split_values"] and p == pairs - 2 and not last:
                    before.append(("WV",))
                if k == steps - 1:
                    before.append(("NORM", p))
                if p % 2 == 0 and more2:
                    before += {fill["queries"]: [("QMM",)], fill["turn"]: [("QTR",), ("QHALF", 0)]}.get(k, [])
                if p % 2 == 1 and more:
                    before += {1: [("QHALF", 1)]}.get(k, [])
                main.append((before, after))
            side = exps(p) if not more else scores_of((p + 1) % pairs, keys, exps(p))
            o += weave(main, side, needed)
        if last:
            o += [("PV", pairs - 1, k) for k in range(steps - LAG, steps)]
            o += [("OUT", pairs - 1), ("WO",)]
        return o

    prologue = [("WK",), ("CTX", 0), ("QMM",), ("CTX", 1), ("K", 0), ("CTX", 2), ("CTX", 3), ("QTR",), ("K", 1),
                ("QHALF", 0), ("QHALF", 1), ("CTX", 4), ("WV",), ("K", 2), ("K", 3), ("V", 0)]
    prologue += [("K", 4)] if nb > 4 else []
    prologue += weave([([], [("V", k)]) for k in range(1, steps)], scores_of(0, False, []))
    return prologue, turn(True, False), turn(False, False), turn(False, True)


SIGNALS = {
    "CTX": {},
    "WK": {"wk_hi": 1, "wk_lo": 1},
    "WV": {"wv_hi": 2, "wv_lo": 2},
    "QMM": {"q_part": 3, "t_full": 1, "q_row": 1},
    "QTR": {"t_full": 1, "q_col": 1},
    "QHALF": {"q_hi": 1, "q_lo": 1},
    "K": {"k_full": 1, "k_hi": 1, "k_lo": 1},
    "V": {"t_full": 1, "v_hi": 1, "v_lo": 1},
    "S": {"s_full": 1},
    "MAX": {"max_step": 1},
    "NEG": {"neg_max": 1},
    "EXP": {"exps": 1},
    "T": {"t_full": 1, "p_hi": 1, "p_lo": 1},
    "PV": {"pv": 1},
    "RD": {"rd_step": 2, "diag": 1},
    "NORM": {"t_full": 1, "r_row": 1},
    "OUT": {"heads_out": 1},
    "WO": {"wo_part": 7, "t_full": 1, "x_sum": 1},
}
ITEMS = {"WK": 1, "WV": 2, "QMM": 4, "WO": 8}
T_READ = {"QMM": "q_row", "QTR": "q_col", "V": "v_lo", "T": "p_lo", "NORM": "r_row", "WO": "x_sum"}


STEPS = {
    "pe_steps": [("m_latent", 1), ("m_aT_full", 1), ("e_means", 1), ("e_logits", 1), ("e_chosen", 1),
                 ("s_dt_full", 1), ("s_cb_full", 2), ("f_logits", 1), ("f_rT_full", 1), ("f_scales", 2),
                 ("f_xT_full", 1), ("f_out_full", 1)],
    "act_steps": [("m_sq", 2), ("m_aT_ready", 1), ("e_abs", 1), ("e_exp", 1), ("s_dt_abs", 1),
                  ("s_dt_exp", 1), ("s_a_exp", 1), ("s_dt_ln", 1),
                  ("f_sign_ready", 1), ("f_exp", 1), ("f_rT_ready", 1), ("f_os_ready", 1), ("f_xT_ready", 1)],
    "dve_steps": [("m_a_clear", 1), ("m_var", 1), ("m_a_ready", 1), ("m_x_sum", 1),
                  ("e_weighed", 1), ("e_ratio", 1), ("e_neg_max", 1), ("e_choice", 1), ("e_x_sum", 1),
                  ("bq_scaled", 1), ("bo_added", 1), ("s_dt_u", 1), ("s_cb_ready", 2),
                  ("s_x_sum", 1), ("f_neg_max", 1), ("f_inv", 1), ("f_routing", 1),
                  ("f_scaled", 1), ("f_biased", 1), ("f_y", 1), ("f_x_sum", 1)],
}
SHARED = {}
for _carrier, _signals in STEPS.items():
    _before = 0
    for _name, _times in _signals:
        SHARED[_name] = (_carrier, _before)
        _before += _times


def build(nc, a, out):
    where = [-(-nc.sbuf_base // 64) * 64]

    def place(name, shape, dt=F32, at=None):
        size = 4
        for n in shape[1:]:
            size *= n
        offset = where[0] if at is None else at
        t = nc.alloc_sbuf_tensor_at(name, shape, dt, offset=offset)
        assert offset + size <= nc.sbuf_usable_end, (name, offset + size)
        if at is None:
            where[0] = offset + -(-size // 32) * 32
        return t

    with ExitStack() as ctx:
        sems = {}

        def sem(name):
            name = SHARED.get(name, (name, 0))[0]
            if name not in sems:
                sems[name] = ctx.enter_context(nc.semaphore(name))
            return sems[name]

        def reach(name, times=1):
            return sem(name), SHARED.get(name, (name, 0))[1] + times

        banks = ctx.enter_context(nc.psum_tensor("banks", [P, 8, 512], F32))
        PV_BANK = 7

        const = place("const", [P, C_WIDTH])
        ident = const[:, C_IDENT:C_IDENT + P]
        ones = const[:, C_ONES:C_ONES + P]
        x = place("x", [TOK, D])
        xlnT = place("xlnT", [P, DC, TOK])
        ln = place("ln", [TOK, 24])
        minus_half = place("minus_half", [TOK, 8])
        rows = place("rows", [TOK, D])
        xln = rows
        shared = where[0]

        KMAX = CTX + TOK
        ctx_hi = place("ctx_hi", [P, DC, KMAX], F32R)
        ctx_lo = place("ctx_lo", [P, DC, KMAX], F32R)
        attn_base = where[0]
        v_hi = place("v_hi", [P, 17, 256], F32R)
        v_lo = place("v_lo", [P, 17, 256], F32R)
        k_hi = place("k_hi", [P, KMAX], F32R)
        k_lo = place("k_lo", [P, KMAX], F32R)
        prob = place("prob", [TOK, 4, KMAX])
        q_hi = place("q_hi", [P, 4, TOK], F32R)
        q_lo = place("q_lo", [P, 4, TOK], F32R)
        heads = place("heads", [P, 8, TOK])
        pt_hi = place("pt_hi", [P, 3, 512], F32R)
        pt_lo = place("pt_lo", [P, 3, 512], F32R)
        ring = place("ring", [P, RING, 512])
        wk_hi = place("wk_hi", [P, DC, P], F32R)
        wk_lo = place("wk_lo", [P, DC, P], F32R)
        wv_hi = place("wv_hi", [P, DC, 256], F32R)
        wv_lo = place("wv_lo", [P, DC, 256], F32R)
        inv_row = place("inv_row", [P, 256])
        diag = place("diag", [P, 2, P])
        stat = place("stat", [P, 4, 5 + 5 + 1])
        inv = place("inv", [P, 4])
        bias_q = place("bias_q", [P, NHEAD])
        bias_k = place("bias_k", [P, 8])
        bias_v = place("bias_v", [P, 8])

        where[0] = attn_base
        m_wa = place("m_wa", [P, DC, 224])
        m_wqb = place("m_wqb", [P, 4096])
        m_wkvb = place("m_wkvb", [P, 6144])
        m_a = place("m_a", [TOK, 384])
        m_aT = place("m_aT", [P, 3, TOK])
        m_q = place("m_q", [TOK, NHEAD, P])
        m_v = place("m_v", [TOK, NHEAD, P])
        turned_base = where[0]
        m_qT = place("m_qT", [P, NHEAD, TOK])
        m_kT = place("m_kT", [P, NHEAD, TOK])
        m_st = place("m_st", [TOK, 4, NHEAD])
        m_rot = place("m_rot", [TOK, 4, 4, 32])
        m_lnw = place("m_lnw", [P, 2])
        m_ring = place("m_ring", [P, 4, 1024])

        where[0] = attn_base
        e_w1 = place("e_w1", [P, 3, DC, D], at=turned_base)
        e_w2 = place("e_w2", [P, 3, DC, D])
        e_act = place("e_act", [P, 3, DC, TOK])
        e_gw = place("e_gw", [P, DC, 4])
        e_row = place("e_row", [1, 8 + 3 * D + P])
        e_b1 = place("e_b1", [P, 12])
        e_s = place("e_s", [TOK, 64])

        where[0] = shared
        NSLOT = 4
        s_w = place("s_w", [P, NSLOT, DC, D])
        decay_base = where[0]
        s_decay = place("s_decay", [TOK, 128, P])
        g_base = where[0]
        s_g = place("s_g", [TOK, 8192])
        s_mix = place("s_mix", [TOK, 2, 8, P])
        s_conv = place("s_conv", [P, 2, DC, TOK])
        s_tanh = place("s_tanh", [P, 2, DC, TOK])
        s_chan = place("s_chan", [P, 2, DC, TOK])
        s_hs = place("s_hs", [TOK, 2, 512])
        s_gate = place("s_gate", [TOK, 2, 512])
        s_bT = place("s_bT", [P, 8, TOK])
        s_cT = place("s_cT", [P, 8, TOK])
        s_cb = place("s_cb", [TOK, 8, TOK])
        seg_base = where[0]
        seg_hi = place("seg_hi", [TOK, 4, 4, P], F32R)
        s_cw = place("s_cw", [P, 80, 4])
        s_cbias = place("s_cbias", [P, 80])
        s_dt = place("s_dt", [TOK, 8, 128])
        s_row = place("s_row", [1, 3 * 128])
        s_nw = place("s_nw", [P, 64])
        s_var = place("s_var", [TOK, 4, 16])
        s_squares = s_var[:, 0, :]
        y_base = where[0]
        s_y = place("s_y", [TOK, 2, 512])
        s_sq = place("s_sq", [TOK, 512])
        xT_hi = place("xT_hi", [P, DC, TOK], F32R)
        xT_lo = place("xT_lo", [P, DC, TOK], F32R)
        gate_hi = place("gate_hi", [P, DC, D], F32R, at=seg_base)
        s_w_lo = place("s_w_lo", [P, NSLOT, DC, D], F32R, at=shared)
        seg_lo = place("seg_lo", [TOK, 4, 4, P], F32R, at=g_base)
        dA_hi = place("dA_hi", [TOK, P], F32R, at=y_base)
        dA_lo = place("dA_lo", [TOK, P], F32R, at=y_base + 512)
        after_r = place("after_r", [TOK, P], F32R, at=y_base + 1024)

        where[0] = decay_base
        f_w = place("f_w", [P, DC, D])
        f_sign = place("f_sign", [P, DC, D])
        f_gw = place("f_gw", [P, DC, 8])
        f_scale = place("f_scale", [8, 2, D])
        f_bias = place("f_bias", [TOK, D])
        f_xs = place("f_xs", [TOK, D])
        f_xT = place("f_xT", [P, DC, TOK])
        f_r = place("f_r", [TOK, 24])
        f_rT = place("f_rT", [8, TOK])
        f_os = place("f_os", [TOK, D])
        assert where[0] <= decay_base + 32768
        o_hi = place("o_hi", [P, 2, DC, D], F32R, at=decay_base + 32768)
        o_lo = place("o_lo", [P, 2, DC, D], F32R, at=decay_base + 49152)
        g_hi = place("g_hi", [P, 2, DC, TOK], F32R, at=seg_base)
        g_lo = place("g_lo", [P, 2, DC, TOK], F32R, at=seg_base + 4096)

        def ln_dve(dve, n):
            nc.vector.bn_stats(ln[:, 0:6], x[:]).then_inc(sem("ln_stats"), 1)
            dve.wait_ge(*reach("ln_stats", n + 1))
            nc.vector.bn_aggr(ln[:, 6:8], ln[:, 0:6]).then_inc(sem("ln_aggr"), 1)
            dve.wait_ge(*reach("ln_aggr", n + 1))
            nc.vector.tensor_scalar(ln[:, 8:9], ln[:, 7:8], EPS, None, ALU.add).then_inc(sem("ln_var"), 1)
            rsqrt_dve(dve, ln[:, 8:9], ln[:, 9:10], ln[:, 11:12])
            nc.vector.tensor_scalar(xln[:], x[:], ln[:, 6:7], ln[:, 9:10], ALU.subtract,
                                    ALU.mult).then_inc(sem("xln_ready"), 1)

        roots = [0]
        own_steps = [0]

        def rsqrt_pool(pool, ready, count, v, y):
            pool.wait_ge(*reach(ready, count))
            nc.gpsimd.tensor_tensor(y, v, minus_half[:, 0:v.shape[1]], ALU.pow).then_inc(sem("root_guess"), 1)

        def rsqrt_dve(dve, v, y, t):
            n = roots[0]
            roots[0] += 1
            dve.wait_ge(*reach("root_guess", n + 1))
            nc.vector.tensor_tensor(t, y, y, ALU.mult).then_inc(sem("root_step"), 1)
            dve.wait_ge(*reach("root_step", 3 * n + 1))
            nc.vector.scalar_tensor_tensor(t, t, -0.5, v, ALU.mult, ALU.mult).then_inc(sem("root_step"), 1)
            dve.wait_ge(*reach("root_step", 3 * n + 2))
            nc.vector.scalar_tensor_tensor(y, t, 1.5, y, ALU.add, ALU.mult).then_inc(sem("root_step"), 1)
            dve.wait_ge(*reach("root_step", 3 * n + 3))

        def ln_pool(pool, n):
            rsqrt_pool(pool, "ln_var", n + 1, ln[:, 8:9], ln[:, 9:10])

        def ln_act(act, n):
            act.wait_ge(*reach("xln_turned", n + 1))
            nc.scalar.activation(xlnT[:], banks[:, PV_BANK, :], ACT.Copy).then_inc(sem("xlnT_ready"), 1)

        def ln_pe(pe, n):
            pe.wait_ge(*reach("xln_ready", n + 1))
            for c in range(DC):
                mm = pe.transpose(banks[:, PV_BANK, c * P:(c + 1) * P], xln[:, c * P:(c + 1) * P], ident)
            mm.then_inc(sem("xln_turned"), 1)
            pe.wait_ge(*reach("xlnT_ready", n + 1))

        def three_passes(pe, dst, pairs, start=True, stop=True):
            for n, (w_hi, w_lo, m_hi, m_lo) in enumerate(pairs):
                pe.matmul(dst, w_hi, m_hi, start=start and n == 0, stop=False)
                pe.matmul(dst, w_hi, m_lo, start=False, stop=False)
                mm = pe.matmul(dst, w_lo, m_hi, start=False, stop=stop and n == len(pairs) - 1)
            return mm

        ctx_cuts = [(0, 448), (448, 896), (896, 1344), (1344, 1792), (1792, CTX)]

        def ctx_load(sp, n):
            lo, hi = ctx_cuts[n]
            sp.dma_start(prob[:, :, lo:hi], a["ctxT"][:, lo:hi].rearrange("(c p) n -> p c n", p=P)
                         ).then_inc(sem(f"ctx_in{n}"), 16)

        def ctx_act(act):
            act.wait_ge(*reach("xlnT_ready", 1))
            nc.scalar.activation(ctx_hi[:, :, CTX:KMAX], xlnT[:], ACT.Copy).then_inc(sem("ctx_hi"), 1)

        def ctx_act_block(act, n):
            lo, hi = ctx_cuts[n]
            act.wait_ge(sem(f"ctx_in{n}"), 16)
            nc.scalar.activation(ctx_hi[:, :, lo:hi], prob[:, :, lo:hi], ACT.Copy).then_inc(sem("ctx_hi"), 1)

        def ctx_dve(dve):
            dve.wait_ge(*reach("ctx_hi", 1))
            nc.vector.tensor_tensor(ctx_lo[:, :, CTX:KMAX], xlnT[:], ctx_hi[:, :, CTX:KMAX].bitcast(F32),
                                    ALU.subtract).then_inc(sem("ctx_lo"), 1)

        def ctx_dve_block(dve, n):
            lo, hi = ctx_cuts[n]
            dve.wait_ge(*reach("ctx_hi", n + 2))
            nc.vector.tensor_tensor(ctx_lo[:, :, lo:hi], prob[:, :, lo:hi], ctx_hi[:, :, lo:hi].bitcast(F32),
                                    ALU.subtract).then_inc(sem("ctx_lo"), 1)

        class Cross:
            def __init__(self, layer, before=None):
                self.layer = layer
                self.kv_groups, self.tiles, self.turns = ((2, 17, 2), (1, 16, 4))[layer]
                self.cuts = ([448, 448, 448, 448, 384], [512] * 4)[layer]
                self.nb = len(self.cuts)
                self.off = [sum(self.cuts[:c]) for c in range(self.nb)]
                self.t_banks = ((5, 6), (4, 5, 6))[layer]
                self.plan = attention_plan(self.kv_groups, self.tiles, self.cuts)
                self.Wq, self.Wo = a[f"Wq{layer}"], a[f"Wo{layer}"]
                self.before = before.totals() if before else {}
                items = sum(by * self.before.get(kind, 0) for kind, by in ITEMS.items())
                self.slot_before = [(items + RING - 1 - s) // RING for s in range(RING)]

            def sem(self, name):
                return sem("x_" + name)

            def t_bank(self, t):
                return self.t_banks[t.local("t_full") % len(self.t_banks)]

            def item(self, t, number=0):
                n = sum(by * t.local(kind) for kind, by in ITEMS.items()) + number
                loads = n // RING + 1 + self.slot_before[n % RING]
                return ring[:, n % RING, :], (self.sem(f"ring_in{n % RING}"), 16 * loads)

            def totals(self):
                last = []
                self.walk(lambda e, t: last.append(t))
                return last[-1].count

            def walk(self, visit):
                prologue, first, body, last = self.plan
                tally = Tally(self.before)
                for e in prologue + first + body * (self.turns - 2) + last:
                    visit(e, tally)
                    for name, by in SIGNALS[e[0]].items():
                        tally.add(name, by)
                    tally.add(e[0])

            def sync(self, sp):
                L = self.layer
                Wk, Wv = a[f"Wk{L}"], a[f"Wv{L}"]
                used = []

                def between(n):
                    if L == 0:
                        for block in range(5) if n == RING else ():
                            ctx_load(sp, block)
                    elif n == RING:
                        sp.wait_ge(*reach("xlnT_ready", 4))
                        sp.dma_start(rows[:], a["bo1"].broadcast_to([P, D])).then_inc(sem("bo_in"), 16)

                def load(src, user, value):
                    n = len(used)
                    if n >= RING:
                        sp.wait_ge(self.sem(used[n - RING][0]), used[n - RING][1])
                    used.append((user, value))
                    c, w = src.shape[0] // P, src.shape[1]
                    sp.dma_start(ring[:, n % RING, :].rearrange("p (c n) -> p c n", c=c),
                                 src.rearrange("(c p) n -> p c n", p=P)).then_inc(self.sem(f"ring_in{n % RING}"), 16)
                    between(n + 1)

                def visit(e, t):
                    n = t.local(e[0])
                    if e[0] == "WK":
                        load(Wk[:, n * P:(n + 1) * P], "wk_lo", t.at("wk_lo") + 1)
                    elif e[0] == "WV":
                        for h in range(2):
                            load(Wv[h * 256:(h + 1) * 256, n * 256:(n + 1) * 256], "wv_lo", t.at("wv_lo") + h + 1)
                    elif e[0] == "QMM":
                        for c in range(4):
                            load(self.Wq[c * P:(c + 1) * P, n * 512:(n + 1) * 512],
                                 *(("q_part", t.at("q_part") + c + 1) if c < 3 else ("t_full", t.at("t_full") + 1)))
                    elif e[0] == "WO":
                        if L == 1 and n == NHEAD // 8 - 1:
                            sp.wait_ge(self.sem("k_full"), t.at("k_full"))
                            ssm_first_loads(sp)
                        for h in range(8):
                            load(self.Wo[(n * 8 + h) * P:(n * 8 + h + 1) * P, :],
                                 *(("wo_part", t.at("wo_part") + h + 1) if h < 7 else ("t_full", t.at("t_full") + 1)))

                self.walk(visit)

            def pe(self, pe):
                t_users = []
                bank_read = {}
                exp_done = {}
                v_done = {}

                def t_slot(e, t):
                    n = len(self.t_banks)
                    if len(t_users) >= n:
                        pe.wait_ge(self.sem(t_users[-n][0]), t_users[-n][1])
                    t_users.append((T_READ[e], t.at(T_READ[e]) + 1))
                    return banks[:, self.t_bank(t), :]

                def ring_item(t, number):
                    weights, landed = self.item(t, number)
                    pe.wait_ge(*landed)
                    return weights

                def visit(e, t):
                    kind = e[0]
                    if kind == "QMM":
                        bank = t_slot(kind, t)
                        for c in range(4):
                            w = ring_item(t, c)
                            pe.matmul(bank, xlnT[:, c, :], w, start=(c == 0), stop=(c == 3)
                                      ).then_inc(self.sem("q_part" if c < 3 else "t_full"), 1)
                    elif kind == "QTR":
                        bank = t_slot(kind, t)
                        pe.wait_ge(self.sem("q_row"), t.at("q_row"))
                        for h in range(4):
                            mm = pe.transpose(bank[:, h * P:(h + 1) * P], rows[:, h * P:(h + 1) * P], ident)
                        mm.then_inc(self.sem("t_full"), 1)
                    elif kind == "K":
                        c = e[1]
                        if c == 0:
                            pe.wait_ge(self.sem("wk_lo"), t.at("wk_lo"))
                        if self.layer == 0 and t.local("K") < self.nb:
                            pe.wait_ge(*reach("ctx_lo", c + 2))
                        if c in bank_read:
                            pe.wait_ge(*bank_read[c])
                        bank_read[c] = (self.sem("k_lo"), t.at("k_lo") + 1)
                        k = slice(self.off[c], self.off[c] + self.cuts[c])
                        three_passes(pe, banks[:, c, 0:self.cuts[c]],
                                     [(wk_hi[:, d, :], wk_lo[:, d, :], ctx_hi[:, d, k], ctx_lo[:, d, k])
                                      for d in range(DC)]).then_inc(self.sem("k_full"), 1)
                    elif kind == "V":
                        bank = t_slot(kind, t)
                        if e[1] == 0:
                            pe.wait_ge(self.sem("wv_lo"), t.at("wv_lo"))
                        for n, tile in enumerate(range(2 * e[1], min(2 * e[1] + 2, self.tiles))):
                            k = slice(tile * P, (tile + 1) * P)
                            mm = three_passes(pe, bank[:, n * 256:(n + 1) * 256],
                                              [(ctx_hi[:, d, k], ctx_lo[:, d, k], wv_hi[:, d, :], wv_lo[:, d, :])
                                               for d in range(DC)])
                        mm.then_inc(self.sem("t_full"), 1)
                        v_done[e[1]] = t.at("v_lo") + 1
                    elif kind == "S":
                        _, p, half, c = e
                        if c == 0:
                            pe.wait_ge(self.sem("q_lo"), t.at("q_lo"))
                        pe.wait_ge(*bank_read[c])
                        h = 2 * (p % 2) + half
                        k = slice(self.off[c], self.off[c] + self.cuts[c])
                        three_passes(pe, banks[:, c, 0:self.cuts[c]],
                                     [(q_hi[:, h, :], q_lo[:, h, :], k_hi[:, k], k_lo[:, k])]
                                     ).then_inc(self.sem("s_full"), 1)
                    elif kind == "EXP":
                        exp_done[e[1:]] = t.at("exps") + 1
                        bank_read[e[3]] = (self.sem("exps"), t.at("exps") + 1)
                    elif kind == "T":
                        _, p, k = e
                        tiles = range(2 * k, min(2 * k + 2, self.tiles))
                        c = max(c for c in range(self.nb) if self.off[c] < (tiles[-1] + 1) * P)
                        bank = t_slot(kind, t)
                        pe.wait_ge(self.sem("exps"), exp_done[p, 1, c])
                        for n, tile in enumerate(tiles):
                            for half in range(2):
                                mm = pe.transpose(bank[:, (2 * n + half) * P:(2 * n + half + 1) * P],
                                                  prob[:, 2 * (p % 2) + half, tile * P:(tile + 1) * P], ident)
                        mm.then_inc(self.sem("t_full"), 1)
                    elif kind == "PV":
                        _, p, k = e
                        pe.wait_ge(self.sem("p_lo"), t.at("PV") + 1)
                        if p == 0:
                            pe.wait_ge(self.sem("v_lo"), v_done[k])
                        if k == 0 and t.local("OUT"):
                            if self.layer == 0:
                                pe.wait_ge(self.sem("heads_out"), t.at("heads_out"))
                            else:
                                pe.wait_ge(self.sem("scaled"), t.local("OUT"))
                        kv = p // (2 * self.kv_groups)
                        dst = banks[:, PV_BANK, (p % 2) * 256:(p % 2) * 256 + 256]
                        buf = t.local("PV") % 3
                        for n, tile in enumerate(range(2 * k, min(2 * k + 2, self.tiles))):
                            v = (v_hi[:, tile, kv * P:(kv + 1) * P], v_lo[:, tile, kv * P:(kv + 1) * P])
                            m = slice(n * 256, (n + 1) * 256)
                            mm = three_passes(pe, dst, [(*v, pt_hi[:, buf, m], pt_lo[:, buf, m])],
                                              start=(tile == 0), stop=(tile == self.tiles - 1))
                        mm.then_inc(self.sem("pv"), 1)
                    elif kind == "NORM":
                        bank = t_slot(kind, t)
                        pe.wait_ge(self.sem("diag"), t.at("diag"))
                        pe.matmul(bank[:, 0:256], ones, diag[:].rearrange("p h n -> p (h n)"),
                                  start=True, stop=True).then_inc(self.sem("t_full"), 1)
                    elif kind == "WO":
                        bank = t_slot(kind, t)
                        pe.wait_ge(self.sem("heads_out"), t.at("heads_out"))
                        for h in range(8):
                            w = ring_item(t, h)
                            pe.matmul(bank, heads[:, h, :], w, start=(h == 0), stop=(h == 7)
                                      ).then_inc(self.sem("wo_part" if h < 7 else "t_full"), 1)

                self.walk(visit)

            def act(self, act):
                def visit(e, t):
                    kind, nxt = e[0], t.at("t_full") + 1
                    bank = banks[:, self.t_bank(t), :]
                    if self.layer == 0 and kind == "CTX":
                        ctx_act_block(act, e[1])
                    elif kind == "WK":
                        weights, landed = self.item(t)
                        act.wait_ge(*landed)
                        if t.local("K"):
                            act.wait_ge(self.sem("k_full"), t.at("k_full"))
                        nc.scalar.activation(wk_hi[:].rearrange("p c n -> p (c n)"), weights,
                                             ACT.Copy).then_inc(self.sem("wk_hi"), 1)
                    elif kind == "WV":
                        if t.local("V"):
                            act.wait_ge(self.sem("t_full"), t.at("t_full"))
                        for h in range(2):
                            weights, landed = self.item(t, h)
                            act.wait_ge(*landed)
                            nc.scalar.activation(wv_hi[:, 2 * h:2 * h + 2, :].rearrange("p c n -> p (c n)"), weights,
                                                 ACT.Copy).then_inc(self.sem("wv_hi"), 1)
                    elif kind == "QMM":
                        act.wait_ge(self.sem("t_full"), nxt)
                        if t.local("QMM"):
                            act.wait_ge(self.sem("q_lo"), t.at("q_lo"))
                        elif self.layer == 1:
                            act.wait_ge(*reach("bo_added", 1))
                        nc.scalar.activation(rows[:], bank, ACT.Copy).then_inc(self.sem("q_row"), 1)
                    elif kind == "QHALF":
                        h = 2 * e[1]
                        act.wait_ge(self.sem("q_col"), t.at("q_col"))
                        if t.local("S"):
                            act.wait_ge(self.sem("s_full"), t.at("s_full"))
                        nc.scalar.activation(q_hi[:, h:h + 2, :].rearrange("p h n -> p (h n)"),
                                             rows[:, h * P:(h + 2) * P], ACT.Copy).then_inc(self.sem("q_hi"), 1)
                    elif kind == "K":
                        c = e[1]
                        o, w = self.off[c], self.cuts[c]
                        act.wait_ge(self.sem("k_full"), t.at("k_full") + 1)
                        if self.layer == 0:
                            nc.scalar.activation(k_hi[:, o:o + w], banks[:, c, 0:w],
                                                 ACT.Copy).then_inc(self.sem("k_hi"), 1)
                        else:
                            kv = t.local("K") // self.nb
                            nc.scalar.activation(k_hi[:, o:o + w], banks[:, c, 0:w], ACT.Identity,
                                                 bias=bias_k[:, kv:kv + 1]).then_inc(self.sem("k_hi"), 1)
                    elif kind == "V":
                        k = e[1]
                        n = min(2, self.tiles - 2 * k)
                        act.wait_ge(self.sem("t_full"), nxt)
                        nc.scalar.activation(v_hi[:, 2 * k:2 * k + n, :].rearrange("p t n -> p (t n)"),
                                             bank[:, 0:256 * n], ACT.Copy).then_inc(self.sem("v_hi"), 1)
                    elif kind == "EXP":
                        _, p, half, c = e
                        slot = 2 * (p % 2) + half
                        o, w = self.off[c], self.cuts[c]
                        if c == 0:
                            act.wait_ge(self.sem("neg_max"), t.at("neg_max"))
                        nc.scalar.activation(prob[:, slot, o:o + w], banks[:, c, 0:w], ACT.Exp,
                                             bias=stat[:, slot, 10:11], accum_out=stat[:, slot, c:c + 1]
                                             ).then_inc(self.sem("exps"), 1)
                    elif kind == "T":
                        n, w = t.local("T"), 256 * min(2, self.tiles - 2 * e[2])
                        act.wait_ge(self.sem("t_full"), nxt)
                        if n >= 3:
                            act.wait_ge(self.sem("pv"), t.at("T", back=2))
                        nc.scalar.activation(pt_hi[:, n % 3, 0:w], bank[:, 0:w],
                                             ACT.Copy).then_inc(self.sem("p_hi"), 1)
                    elif kind == "NORM":
                        act.wait_ge(self.sem("t_full"), nxt)
                        if t.local("NORM"):
                            act.wait_ge(self.sem("heads_out"), t.at("heads_out"))
                        nc.scalar.activation(inv_row[:], bank[:, 0:256], ACT.Copy).then_inc(self.sem("r_row"), 1)

                self.walk(visit)

            def dve(self, dve):
                def minus(out, in0, hi):
                    return nc.vector.tensor_tensor(out, in0, hi.bitcast(F32), ALU.subtract)

                def visit(e, t):
                    kind, nxt = e[0], t.at("t_full") + 1
                    bank = banks[:, self.t_bank(t), :]
                    if self.layer == 0 and kind == "CTX":
                        ctx_dve_block(dve, e[1])
                    elif kind == "WK":
                        dve.wait_ge(self.sem("wk_hi"), t.at("wk_hi") + 1)
                        minus(wk_lo[:].rearrange("p c n -> p (c n)"), self.item(t)[0],
                              wk_hi[:].rearrange("p c n -> p (c n)")).then_inc(self.sem("wk_lo"), 1)
                    elif kind == "WV":
                        for h in range(2):
                            dve.wait_ge(self.sem("wv_hi"), t.at("wv_hi") + h + 1)
                            minus(wv_lo[:, 2 * h:2 * h + 2, :].rearrange("p c n -> p (c n)"), self.item(t, h)[0],
                                  wv_hi[:, 2 * h:2 * h + 2, :].rearrange("p c n -> p (c n)")
                                  ).then_inc(self.sem("wv_lo"), 1)
                    elif kind == "QMM":
                        if self.layer == 1 and not t.local("QMM"):
                            dve.wait_ge(*reach("bo_in", 16))
                            nc.vector.tensor_tensor(x[:], x[:], rows[:], ALU.add).then_inc(sem("bo_added"), 1)
                            dve.wait_ge(*reach("bo_added", 1))
                    elif kind == "QTR":
                        g = t.local("QTR")
                        dve.wait_ge(self.sem("t_full"), nxt)
                        if self.layer == 0:
                            ins = nc.vector.tensor_scalar(rows[:], bank, ATT_SCALE, None, ALU.mult)
                        else:
                            ins = nc.vector.scalar_tensor_tensor(
                                rows[:].rearrange("p (h n) -> p h n", h=4), bank.rearrange("p (h n) -> p h n", h=4),
                                ATT_SCALE, bias_q[:, 4 * g:4 * g + 4].unsqueeze(2).broadcast_to([P, 4, P]),
                                ALU.mult, ALU.add)
                        ins.then_inc(self.sem("q_col"), 1)
                    elif kind == "QHALF":
                        h = 2 * e[1]
                        dve.wait_ge(self.sem("q_hi"), t.at("q_hi") + 1)
                        minus(q_lo[:, h:h + 2, :].rearrange("p h n -> p (h n)"), rows[:, h * P:(h + 2) * P],
                              q_hi[:, h:h + 2, :].rearrange("p h n -> p (h n)")).then_inc(self.sem("q_lo"), 1)
                    elif kind == "K":
                        c = e[1]
                        o, w = self.off[c], self.cuts[c]
                        dve.wait_ge(self.sem("k_hi"), t.at("k_hi") + 1)
                        if self.layer == 0:
                            minus(k_lo[:, o:o + w], banks[:, c, 0:w], k_hi[:, o:o + w]).then_inc(self.sem("k_lo"), 1)
                        else:
                            kv = t.local("K") // self.nb
                            nc.vector.scalar_tensor_tensor(
                                k_lo[:, o:o + w], banks[:, c, 0:w], bias_k[:, kv:kv + 1],
                                k_hi[:, o:o + w].bitcast(F32), ALU.add, ALU.subtract).then_inc(self.sem("k_lo"), 1)
                    elif kind == "V":
                        k = e[1]
                        n = min(2, self.tiles - 2 * k)
                        dve.wait_ge(self.sem("v_hi"), t.at("v_hi") + 1)
                        minus(v_lo[:, 2 * k:2 * k + n, :].rearrange("p t n -> p (t n)"), bank[:, 0:256 * n],
                              v_hi[:, 2 * k:2 * k + n, :].rearrange("p t n -> p (t n)")
                              ).then_inc(self.sem("v_lo"), 1)
                    elif kind == "MAX":
                        _, p, half, c = e
                        slot = 2 * (p % 2) + half
                        dve.wait_ge(self.sem("s_full"), t.at("s_full"))
                        nc.vector.tensor_reduce(stat[:, slot, 5 + c:6 + c], banks[:, c, 0:self.cuts[c]],
                                                AX.X, ALU.max).then_inc(self.sem("max_step"), 1)
                    elif kind == "NEG":
                        _, p, half = e
                        slot = 2 * (p % 2) + half
                        dve.wait_ge(self.sem("max_step"), t.at("max_step"))
                        nc.vector.tensor_reduce(stat[:, slot, 10:11], stat[:, slot, 5:5 + self.nb], AX.X,
                                                ALU.max, negate=True).then_inc(self.sem("neg_max"), 1)
                    elif kind == "T":
                        n, w = t.local("T"), 256 * min(2, self.tiles - 2 * e[2])
                        dve.wait_ge(self.sem("p_hi"), t.at("p_hi") + 1)
                        minus(pt_lo[:, n % 3, 0:w], bank[:, 0:w], pt_hi[:, n % 3, 0:w]).then_inc(self.sem("p_lo"), 1)
                    elif kind == "RD":
                        p = e[1]
                        dve.wait_ge(self.sem("exps"), exp_done[p])
                        nc.vector.tensor_reduce(inv[:, 0:2], stat[:, 2 * (p % 2):2 * (p % 2) + 2, 0:self.nb], AX.X,
                                                ALU.add).then_inc(self.sem("rd_step"), 1)
                        dve.wait_ge(self.sem("rd_step"), t.at("rd_step") + 1)
                        nc.vector.reciprocal(inv[:, 2:4], inv[:, 0:2]).then_inc(self.sem("rd_step"), 1)
                        dve.wait_ge(self.sem("rd_step"), t.at("rd_step") + 2)
                        if t.local("NORM"):
                            dve.wait_ge(self.sem("r_row"), t.at("r_row"))
                        for half in range(2):
                            ins = nc.vector.tensor_scalar(diag[:, half, :], ident, inv[:, 2 + half:3 + half], None,
                                                          ALU.mult)
                        ins.then_inc(self.sem("diag"), 1)
                    elif kind == "EXP":
                        exp_done[e[1]] = t.at("exps") + 1
                    elif kind == "OUT":
                        p, n = e[1], t.local("OUT")
                        dst = heads[:, 2 * (p % 4):2 * (p % 4) + 2, :].rearrange("p h n -> p (h n)")
                        dve.wait_ge(self.sem("r_row"), t.at("r_row"))
                        dve.wait_ge(self.sem("pv"), t.at("pv"))
                        ins = nc.vector.tensor_tensor(dst, banks[:, PV_BANK, (p % 2) * 256:(p % 2) * 256 + 256],
                                                      inv_row[:], ALU.mult)
                        if self.layer == 1:
                            kv = n // (2 * self.kv_groups)
                            ins.then_inc(self.sem("scaled"), 1)
                            dve.wait_ge(self.sem("scaled"), n + 1)
                            ins = nc.vector.tensor_scalar(dst, dst, bias_v[:, kv:kv + 1], None, ALU.add)
                        ins.then_inc(self.sem("heads_out"), 1)
                    elif kind == "WO":
                        dve.wait_ge(self.sem("t_full"), nxt)
                        if t.local("WO"):
                            dve.wait_ge(self.sem("x_sum"), t.at("x_sum"))
                        nc.vector.tensor_tensor(x[:], x[:], bank, ALU.add).then_inc(self.sem("x_sum"), 1)

                exp_done = {}
                self.walk(visit)
                dve.wait_ge(self.sem("x_sum"), self.before.get("x_sum", 0) + NHEAD // 8)

        cross = [Cross(0)]
        cross.append(Cross(1, cross[0]))

        MLA_SCALE = P ** -0.5 * (0.1 * math.log(128.0) + 1.0) ** 2
        QUADS = NHEAD // 4
        m_pT = m_wqb[:].rearrange("p (h n) -> p h n", h=NHEAD)
        m_out = m_wkvb[:, 0:4096].rearrange("p (h n) -> p h n", h=NHEAD)
        m_kv_w = m_wkvb[0:32, :].rearrange("p (h n) -> p h n", h=NHEAD)
        cos = const[:, C_COS:C_COS + 32]
        sin = const[:, C_SIN:C_SIN + 32]

        def per_head(ap, n, w):
            return ap.unsqueeze(1).broadcast_to([P, n, w])

        def per_column(ap, n, w):
            return ap.unsqueeze(2).broadcast_to([P, n, w])

        def quad(t, n):
            return t[:, 4 * n:4 * n + 4, :].rearrange("p h n -> p (h n)")

        def mla_sync(sp):
            sp.wait_ge(cross[0].sem("x_sum"), 4)
            sp.dma_start(m_wa[:], a["m_wa"].rearrange("(c p) n -> p c n", p=P)).then_inc(sem("m_wa_in"), 16)
            sp.dma_start(m_lnw[:, 0:1], a["m_lnq"]).then_inc(sem("m_lnw_in"), 16)
            sp.dma_start(m_lnw[0:32, 1:2], a["m_lnkv"]).then_inc(sem("m_lnw_in"), 16)
            sp.dma_start(m_wqb[:], a["m_wqb"]).then_inc(sem("m_wqb_in"), 16)
            sp.dma_start(m_wkvb[0:32, :], a["m_wkvb"]).then_inc(sem("m_wkvb_in"), 16)
            for n in range(16):
                if n >= 4:
                    sp.wait_ge(*reach("m_wo_used", n - 3))
                sp.dma_start(m_ring[:, n % 4, :], a["m_wo"][2 * n * P:2 * (n + 1) * P, :]
                             .rearrange("(c p) n -> p c n", p=P)).then_inc(sem(f"m_wo_in{n % 4}"), 16)
            sp.wait_ge(*reach("m_s_full", QUADS))
            for e in range(3):
                sp.dma_start(e_w1[:, e], a["e_w1"][e].rearrange("(c p) n -> p c n", p=P)
                             ).then_inc(sem(f"e_w1_in{e}"), 16)

        def mla_pe(pe):
            pe.wait_ge(*reach("m_wa_in", 16))
            for c in range(DC):
                mm = pe.matmul(banks[:, 0, 0:224], xlnT[:, c, :], m_wa[:, c, :], start=(c == 0), stop=(c == 3))
            mm.then_inc(sem("m_latent"), 1)
            pe.wait_ge(*reach("m_a_ready", 1))
            for c in range(3):
                mm = pe.transpose(banks[:, 1, c * P:(c + 1) * P], m_a[:, c * P:(c + 1) * P], ident)
            mm.then_inc(sem("m_aT_full"), 1)
            pe.wait_ge(*reach("m_aT_ready", 1))
            pe.wait_ge(*reach("m_wqb_in", 16))
            pe.wait_ge(*reach("m_wkvb_in", 16))
            for n in range(QUADS):
                if n >= 2:
                    pe.wait_ge(*reach("m_q_ready", n - 1))
                    pe.wait_ge(*reach("m_nope", n - 1))
                    pe.wait_ge(*reach("m_kT_ready", n - 1))
                    pe.wait_ge(*reach("m_v_ready", n - 1))
                pe.matmul(banks[:, 2 + n % 2, :], m_aT[:, 0, :], m_wqb[:, n * 512:(n + 1) * 512],
                          start=True, stop=True).then_inc(sem("m_q_full"), 1)
                for h in range(4):
                    mm = pe.matmul(banks[0:64, 4 + n % 2, h * P:(h + 1) * P], m_kv_w[:, 4 * n + h, 0:64],
                                   m_aT[0:32, 1, :], start=True, stop=True)
                mm.then_inc(sem("m_k_full"), 1)
                pe.matmul(banks[:, 6 + n % 2, :], m_aT[0:32, 1, :], m_kv_w[:, 4 * n:4 * n + 4, 64:192],
                          start=True, stop=True).then_inc(sem("m_v_full"), 1)
            pe.wait_ge(*reach("m_q_ready", QUADS))
            pe.wait_ge(*reach("m_nope", QUADS))
            pe.wait_ge(*reach("m_kT_ready", QUADS))
            pe.wait_ge(*reach("m_v_ready", QUADS))

            def queries(n):
                if n >= 2:
                    pe.wait_ge(*reach("m_qT_ready", n - 1))
                for h in range(4):
                    mm = pe.transpose(banks[:, 2 + n % 2, h * P:(h + 1) * P], m_q[:, 4 * n + h, :], ident)
                mm.then_inc(sem("m_qT_full"), 1)

            def scores(n):
                pe.wait_ge(*reach("m_qT_ready", n + 1))
                if n == 0:
                    pe.wait_ge(*reach("m_kT_rotary", 1))
                elif n >= 2:
                    pe.wait_ge(*reach("m_masked", n - 1))
                for h in range(4):
                    mm = pe.matmul(banks[:, 4 + n % 2, h * P:(h + 1) * P], m_qT[:, 4 * n + h, :],
                                   m_kT[:, 4 * n + h, :], start=True, stop=True)
                mm.then_inc(sem("m_s_full"), 1)

            def turn_probs(n):
                pe.wait_ge(*reach("m_probs", n + 1))
                if n >= 2:
                    pe.wait_ge(*reach("m_pT_ready", n - 1))
                for h in range(4):
                    mm = pe.transpose(banks[:, 6 + n % 2, h * P:(h + 1) * P], m_q[:, 4 * n + h, :], ident)
                mm.then_inc(sem("m_pT_full"), 1)

            def outputs(n):
                pe.wait_ge(*reach("m_pT_ready", n + 1))
                if n:
                    pe.wait_ge(*reach("m_out_ready", n))
                for h in range(4):
                    mm = pe.matmul(banks[:, 0, h * P:(h + 1) * P], m_v[:, 4 * n + h, :],
                                   m_pT[:, 4 * n + h, :], start=True, stop=True)
                mm.then_inc(sem("m_out_full"), 1)

            def project(q):
                pe.wait_ge(*reach("m_out_ready", q + 1))
                for n in (2 * q, 2 * q + 1):
                    pe.wait_ge(sem(f"m_wo_in{n % 4}"), 16 * (n // 4 + 1))
                    for h in range(2):
                        mm = pe.matmul(banks[:, 1, :], m_out[:, 2 * n + h, :],
                                       m_ring[:, n % 4, h * 512:(h + 1) * 512],
                                       start=(n + h == 0), stop=(n == 15 and h == 1))
                    mm.then_inc(sem("m_wo_used"), 1)

            for n in range(QUADS + 5):
                for stage, lag in ((queries, 0), (scores, 1), (turn_probs, 3), (outputs, 4), (project, 5)):
                    if 0 <= n - lag < QUADS:
                        stage(n - lag)

        def mla_act(act):
            act.wait_ge(*reach("m_latent", 1))
            nc.scalar.activation(m_rot[:, 0], banks[:, 0, 0:P], ACT.Square,
                                 accum_out=ln[:, 12:13]).then_inc(sem("m_sq"), 1)
            nc.scalar.activation(m_rot[:, 1, 0, :], banks[:, 0, P:P + 32], ACT.Square,
                                 accum_out=ln[:, 13:14]).then_inc(sem("m_sq"), 1)
            act.wait_ge(*reach("m_aT_full", 1))
            act.wait_ge(*reach("m_lnw_in", 32))
            nc.scalar.activation(m_aT[:, 0, :], banks[:, 1, 0:P], ACT.Copy, scale=m_lnw[:, 0:1])
            nc.scalar.activation(m_aT[0:32, 1, :], banks[0:32, 1, P:2 * P], ACT.Copy, scale=m_lnw[0:32, 1:2])
            nc.scalar.activation(m_aT[64:128, 2, :], banks[64:128, 1, 2 * P:3 * P],
                                 ACT.Copy).then_inc(sem("m_aT_ready"), 1)
            for n in range(QUADS):
                act.wait_ge(*reach("m_q_full", n + 1))
                nc.scalar.activation(m_q[:, 4 * n:4 * n + 4, 0:64],
                                     banks[:, 2 + n % 2, :].rearrange("p (h n) -> p h n", h=4)[:, :, 0:64],
                                     ACT.Copy).then_inc(sem("m_nope"), 1)
                act.wait_ge(*reach("m_k_full", n + 1))
                nc.scalar.activation(quad(m_kT, n)[0:64, :], banks[0:64, 4 + n % 2, :],
                                     ACT.Copy).then_inc(sem("m_kT_ready"), 1)
                act.wait_ge(*reach("m_v_full", n + 1))
                nc.scalar.activation(quad(m_v, n), banks[:, 6 + n % 2, :], ACT.Copy).then_inc(sem("m_v_ready"), 1)
            for n in range(QUADS + 3):
                if n < QUADS:
                    act.wait_ge(*reach("m_qT_full", n + 1))
                    nc.scalar.activation(quad(m_qT, n), banks[:, 2 + n % 2, :],
                                         ACT.Copy).then_inc(sem("m_qT_ready"), 1)
                if 0 <= n - 1 < QUADS:
                    act.wait_ge(*reach("m_neg_max", n))
                    for h in range(4 * n - 4, 4 * n):
                        nc.scalar.activation(m_q[:, h, :], m_q[:, h, :], ACT.Exp, bias=m_st[:, 0, h:h + 1],
                                             accum_out=m_st[:, 1, h:h + 1]).then_inc(sem("m_exps"), 1)
                if 0 <= n - 3 < QUADS:
                    act.wait_ge(*reach("m_pT_full", n - 2))
                    nc.scalar.activation(quad(m_pT, n - 3), banks[:, 6 + (n - 3) % 2, :],
                                         ACT.Copy).then_inc(sem("m_pT_ready"), 1)

        def rotate(dve, even, odd, first, second, heads, count):
            t = [m_rot[:, k, 0:heads, :] for k in range(4)]
            for k, (v, w) in enumerate(((even, cos), (odd, sin), (odd, cos), (even, sin))):
                ins = nc.vector.tensor_tensor(t[k], v, per_head(w, heads, 32), ALU.mult)
            ins.then_inc(sem("m_turned"), 1)
            dve.wait_ge(*reach("m_turned", count + 1))
            nc.vector.tensor_tensor(first, t[0], t[1], ALU.subtract)
            return nc.vector.tensor_tensor(second, t[2], t[3], ALU.add)

        def mla_dve(dve):
            nc.vector.memset(m_a[:], 0.0).then_inc(sem("m_a_clear"), 1)
            dve.wait_ge(*reach("m_sq", 2))
            nc.vector.tensor_scalar(ln[:, 14:15], ln[:, 12:13], 1.0 / 128, RMS_EPS, ALU.mult, ALU.add)
            nc.vector.tensor_scalar(ln[:, 15:16], ln[:, 13:14], 1.0 / 32, RMS_EPS, ALU.mult,
                                    ALU.add).then_inc(sem("m_var"), 1)
            dve.wait_ge(*reach("m_var", 1))
            rsqrt_dve(dve, ln[:, 14:16], ln[:, 16:18], ln[:, 18:20])
            dve.wait_ge(*reach("m_a_clear", 1))
            nc.vector.tensor_scalar(m_a[:, 0:P], banks[:, 0, 0:P], ln[:, 16:17], None, ALU.mult)
            nc.vector.tensor_scalar(m_a[:, P:P + 32], banks[:, 0, P:P + 32], ln[:, 17:18], None, ALU.mult)
            rotate(dve, banks[:, 0, 160:224:2].unsqueeze(1), banks[:, 0, 161:224:2].unsqueeze(1),
                   m_a[:, 320:352].unsqueeze(1), m_a[:, 352:384].unsqueeze(1), 1, 0).then_inc(sem("m_a_ready"), 1)
            dve.wait_ge(*reach("m_a_ready", 1))
            for n in range(QUADS):
                dve.wait_ge(*reach("m_nope", n + 1))
                if n:
                    dve.wait_ge(*reach("m_q_ready", n))
                pe_part = banks[:, 2 + n % 2, :].rearrange("p (h n) -> p h n", h=4)
                rotate(dve, pe_part[:, :, 64:128:2], pe_part[:, :, 65:128:2], m_q[:, 4 * n:4 * n + 4, 64:96],
                       m_q[:, 4 * n:4 * n + 4, 96:128], 4, n + 1).then_inc(sem("m_q_ready"), 1)

            def inverse(n):
                dve.wait_ge(*reach("m_exps", 4 * n + 4))
                nc.vector.reciprocal(m_st[:, 2, 4 * n:4 * n + 4],
                                     m_st[:, 1, 4 * n:4 * n + 4]).then_inc(sem("m_inv"), 1)
                dve.wait_ge(*reach("m_inv", n + 1))
                nc.vector.tensor_tensor(m_q[:, 4 * n:4 * n + 4, :], m_q[:, 4 * n:4 * n + 4, :],
                                        per_column(m_st[:, 2, 4 * n:4 * n + 4], 4, P),
                                        ALU.mult).then_inc(sem("m_probs"), 1)

            def copy_out(n):
                dve.wait_ge(*reach("m_out_full", n + 1))
                nc.vector.tensor_copy(quad(m_out, n), banks[:, 0, :]).then_inc(sem("m_out_ready"), 1)

            for n in range(QUADS):
                dve.wait_ge(*reach("m_s_full", n + 1))
                nc.vector.scalar_tensor_tensor(
                    m_q[:, 4 * n:4 * n + 4, :], banks[:, 4 + n % 2, :].rearrange("p (h n) -> p h n", h=4), MLA_SCALE,
                    per_head(const[:, C_CAUSAL:C_CAUSAL + P], 4, P), ALU.mult, ALU.add).then_inc(sem("m_masked"), 1)
                dve.wait_ge(*reach("m_masked", n + 1))
                nc.vector.tensor_reduce(m_st[:, 0, 4 * n:4 * n + 4], m_q[:, 4 * n:4 * n + 4, :], AX.X, ALU.max,
                                        negate=True).then_inc(sem("m_neg_max"), 1)
                if n:
                    inverse(n - 1)
                if n >= 3:
                    copy_out(n - 3)
            inverse(QUADS - 1)
            for n in range(QUADS - 3, QUADS):
                copy_out(n)
            dve.wait_ge(*reach("m_wo_used", 16))
            nc.vector.tensor_tensor(x[:], x[:], banks[:, 1, :], ALU.add).then_inc(sem("m_x_sum"), 1)
            dve.wait_ge(*reach("m_x_sum", 1))

        def mla_pool(pool):
            pool.wait_ge(*reach("m_aT_ready", 1))
            nc.gpsimd.tensor_copy(m_kT[64:128, :, :],
                                  m_aT[64:128, 2, :].unsqueeze(1).broadcast_to([64, NHEAD, P])
                                  ).then_inc(sem("m_kT_rotary"), 1)

        EXPERT = (ACT.Tanh, ACT.Gelu, ACT.Silu)
        ratio_row = e_row[0:1, 8 + 3 * D:8 + 3 * D + P]

        def moe_sync(sp):
            sp.wait_ge(*reach("m_x_sum", 1))
            sp.dma_start(e_gw[:, :, 0:3], a["e_gw"][0:D, :].rearrange("(c p) n -> p c n", p=P)
                         ).then_inc(sem("e_small_in"), 16)
            sp.dma_start(e_row[0:1, 0:3], a["e_gw"][D:D + 1, :]).then_inc(sem("e_small_in"), 16)
            sp.dma_start(e_row[0:1, 4:7], a["e_gb"]).then_inc(sem("e_small_in"), 16)
            sp.dma_start(e_row[0:1, 8:8 + 3 * D], a["e_b2"]).then_inc(sem("e_small_in"), 16)
            sp.dma_start(e_b1[:], a["e_b1"]).then_inc(sem("e_small_in"), 16)
            for e in range(3):
                sp.dma_start(e_w2[:, e], a["e_w2"][e].rearrange("(c p) n -> p c n", p=P)).then_inc(sem(f"e_w2_in{e}"), 16)

        def moe_pe(pe):
            for e in range(3):
                pe.wait_ge(sem(f"e_w1_in{e}"), 16)
                for f in range(DC):
                    for c in range(DC):
                        mm = pe.matmul(banks[:, 3 + e, f * P:(f + 1) * P], e_w1[:, e, c, f * P:(f + 1) * P],
                                       xlnT[:, c, :], start=(c == 0), stop=(c == 3))
                mm.then_inc(sem("e_pre"), 1)
                if e == 0:
                    pe.wait_ge(*reach("e_weighed", 1))
                    pe.matmul(banks[:, 0, 0:2], ones, e_s[:, 2:4], start=True, stop=True).then_inc(sem("e_means"), 1)
            pe.wait_ge(*reach("e_small_in", 80))
            for c in range(DC):
                pe.matmul(banks[:, 1, 0:3], xlnT[:, c, :], e_gw[:, c, 0:3], start=(c == 0), stop=False)
            pe.matmul(banks[:, 1, 0:3], ones[0:1, :], e_row[0:1, 4:7], start=False, stop=False)
            pe.wait_ge(*reach("e_ratio", 1))
            pe.matmul(banks[:, 1, 0:3], ratio_row, e_row[0:1, 0:3], start=False, stop=True).then_inc(sem("e_logits"), 1)
            for e in range(3):
                pe.wait_ge(*reach("e_hidden", 4 * (e + 1)))
                pe.wait_ge(sem(f"e_w2_in{e}"), 16)
                bank = (6, 7, 3)[e]
                for f in range(DC):
                    pe.matmul(banks[:, bank, :], e_act[:, e, f, :], e_w2[:, e, f, :], start=(f == 0), stop=False)
                pe.matmul(banks[:, bank, :], ones[0:1, :], e_row[0:1, 8 + e * D:8 + (e + 1) * D],
                          start=False, stop=True).then_inc(sem("e_out"), 1)
                if e == 0:
                    pe.wait_ge(*reach("e_choice", 1))
                    pe.matmul(banks[:, 2, 0:6], ones[0:1, :], e_s[0:1, 40:46], start=True,
                              stop=True).then_inc(sem("e_chosen"), 1)

        def moe_act(act):
            act.wait_ge(*reach("xln_ready", 3))
            nc.scalar.activation(e_act[:, 0].rearrange("p c n -> p (c n)"), xln[:], ACT.Abs,
                                 accum_out=e_s[:, 0:1]).then_inc(sem("e_abs"), 1)
            ln_act(act, 2)
            act.wait_ge(*reach("e_small_in", 80))
            act.wait_ge(*reach("e_abs", 1))

            def hidden(e):
                act.wait_ge(*reach("e_pre", e + 1))
                for f in range(DC):
                    nc.scalar.activation(e_act[:, e, f, :], banks[:, 3 + e, f * P:(f + 1) * P], EXPERT[e],
                                         bias=e_b1[:, 4 * e + f:4 * e + f + 1]).then_inc(sem("e_hidden"), 1)

            hidden(0)
            act.wait_ge(*reach("e_neg_max", 1))
            nc.scalar.activation(e_s[:, 8:11], banks[:, 1, 0:3], ACT.Exp, bias=e_s[:, 5:6],
                                 accum_out=e_s[:, 6:7]).then_inc(sem("e_exp"), 1)
            hidden(1)
            hidden(2)

        def moe_dve(dve):
            def then(ins):
                own_steps[0] += 1
                ins.then_inc(sem("dve_own"), 1)
                dve.wait_ge(*reach("dve_own", own_steps[0]))

            def tt(o, i0, i1, op):
                return nc.vector.tensor_tensor(e_s[:, o:o + 1], e_s[:, i0:i0 + 1], e_s[:, i1:i1 + 1], op)

            dve.wait_ge(*reach("e_abs", 1))
            nc.vector.tensor_scalar(e_s[:, 2:4], const[:, C_MEANS:C_MEANS + 2], e_s[:, 0:1], None,
                                    ALU.mult).then_inc(sem("e_weighed"), 1)
            dve.wait_ge(*reach("e_means", 1))
            then(nc.vector.tensor_scalar(e_s[:, 4:5], banks[:, 0, 1:2], 1e-8, None, ALU.add))
            then(nc.vector.reciprocal(e_s[:, 4:5], e_s[:, 4:5]))
            then(nc.vector.tensor_tensor(e_s[:, 4:5], e_s[:, 4:5], banks[:, 0, 0:1], ALU.mult))
            nc.vector.tensor_scalar(ratio_row, ones[0:1, :], e_s[0:1, 4:5], None, ALU.mult).then_inc(sem("e_ratio"), 1)
            dve.wait_ge(*reach("e_logits", 1))
            nc.vector.tensor_reduce(e_s[:, 5:6], banks[:, 1, 0:3], AX.X, ALU.max, negate=True
                                    ).then_inc(sem("e_neg_max"), 1)
            dve.wait_ge(*reach("e_exp", 1))
            then(nc.vector.reciprocal(e_s[:, 7:8], e_s[:, 6:7]))
            then(nc.vector.tensor_scalar(e_s[:, 12:15], e_s[:, 8:11], e_s[:, 7:8], None, ALU.mult))
            tt(20, 13, 12, ALU.is_gt), tt(21, 14, 12, ALU.is_gt)
            tt(22, 12, 13, ALU.is_ge), tt(23, 14, 13, ALU.is_gt)
            tt(24, 12, 14, ALU.is_ge)
            then(tt(25, 13, 14, ALU.is_ge))
            then(nc.vector.tensor_tensor(e_s[:, 28:31], e_s[:, 20:25:2], e_s[:, 21:26:2], ALU.add))
            nc.vector.tensor_scalar(e_s[:, 40:43], e_s[:, 28:31], 0.0, None, ALU.is_equal)
            nc.vector.tensor_scalar(e_s[:, 43:46], e_s[:, 28:31], 1.0, None, ALU.is_equal).then_inc(sem("e_choice"), 1)
            tt(16, 12, 13, ALU.max)
            then(tt(17, 12, 13, ALU.min))
            tt(32, 16, 14, ALU.max)
            then(tt(18, 16, 14, ALU.min))
            then(tt(33, 17, 18, ALU.max))
            then(tt(34, 32, 33, ALU.add))
            then(nc.vector.tensor_scalar(e_s[:, 34:35], e_s[:, 34:35], 1e-8, None, ALU.add))
            then(nc.vector.reciprocal(e_s[:, 35:36], e_s[:, 34:35]))
            then(nc.vector.tensor_scalar(e_s[:, 36:38], e_s[:, 32:34], e_s[:, 35:36], None, ALU.mult))
            dve.wait_ge(*reach("e_chosen", 1))
            then(nc.vector.tensor_scalar(e_s[:, 48:51], banks[:, 2, 0:3], e_s[:, 36:37], None, ALU.mult))
            then(nc.vector.scalar_tensor_tensor(e_s[:, 52:55], banks[:, 2, 3:6], e_s[:, 37:38], e_s[:, 48:51],
                                                ALU.mult, ALU.add))
            for e in range(3):
                dve.wait_ge(*reach("e_out", e + 1))
                ins = nc.vector.scalar_tensor_tensor(x[:], banks[:, (6, 7, 3)[e], :], e_s[:, 52 + e:53 + e], x[:],
                                                     ALU.mult, ALU.add)
                if e < 2:
                    then(ins)
            ins.then_inc(sem("e_x_sum"), 1)
            dve.wait_ge(*reach("e_x_sum", 1))

        N_BLOCK = 16
        BC_COL, DT_COL = 2 * 8192, 2 * 8192 + 2048
        n_in = 1 + 4 + 2 * N_BLOCK
        upto = const[:, C_UPTO:C_UPTO + P]
        after = const[:, C_AFTER:C_AFTER + P]

        SEG_BANKS = (1, 2, 7)

        def ssm_load(sp, slot, src):
            sp.dma_start(s_w[:, slot, :, 0:src.shape[1]], src.rearrange("(c p) n -> p c n", p=P)
                         ).then_inc(sem(f"s_w_in{slot}"), 16)

        def ssm_first_loads(sp):
            ssm_load(sp, 0, a["s_in"][:, DT_COL:DT_COL + P])
            for m in range(3):
                ssm_load(sp, m + 1, a["s_in"][:, BC_COL + m * 512:BC_COL + (m + 1) * 512])

        def ssm_sync(sp):
            sp.wait_ge(cross[1].sem("x_sum"), 8)
            for k, name in enumerate(("s_dtb", "s_alog", "s_D")):
                sp.dma_start(s_row[0:1, k * P:(k + 1) * P], a[name]).then_inc(sem("s_rows_in"), 16)
            sp.dma_start(s_cw[:], a["s_cw"]).then_inc(sem("s_cw_in"), 16)
            sp.dma_start(s_cbias[:], a["s_cb"]).then_inc(sem("s_cw_in"), 16)
            sp.dma_start(s_nw[:], a["s_nw"]).then_inc(sem("s_nw_in"), 16)
            def load(n, slot, src):
                sp.wait_ge(*reach("s_used", n - NSLOT + 1))
                ssm_load(sp, slot, src)

            load(4, 0, a["s_in"][:, BC_COL + 3 * 512:BC_COL + 4 * 512])
            for b in range(N_BLOCK):
                for n, col in ((5 + 2 * b, 8192 + 512 * b), (6 + 2 * b, 512 * b)):
                    load(n, n % NSLOT, a["s_in"][:, col:col + 512])
            for k in range(4):
                load(n_in + k, (n_in + k) % NSLOT, a["s_out"][k * 512:(k + 1) * 512, :])
            sp.wait_ge(*reach("s_mixed", 16))
            ffn_sync(sp)
            for b in range(4, N_BLOCK):
                sp.wait_ge(*reach("o_lo", 2 * (b - 3)))
                sp.wait_ge(*reach("o_lo_pool", b - 3))
                ssm_load(sp, (n_in + b) % NSLOT, a["s_out"][b * 512:(b + 1) * 512, :])

        def ssm_pe(pe):
            def weights(n, rounds=0):
                pe.wait_ge(sem(f"s_w_in{n % NSLOT}"), (rounds + n // NSLOT + 1) * 16)
                return s_w[:, n % NSLOT]

            w = weights(0)
            for c in range(DC):
                mm = pe.matmul(banks[:, 0, 0:P], xlnT[:, c, :], w[:, c, 0:P], start=(c == 0), stop=False)
            mm.then_inc(sem("s_used"), 1)
            pe.wait_ge(*reach("s_rows_in", 48))
            pe.matmul(banks[:, 0, 0:P], ones[0:1, :], s_row[0:1, 0:P], start=False, stop=True)
            pe.matmul(banks[:, 0, P:3 * P], ones[0:1, :], s_row[0:1, P:3 * P], start=True,
                      stop=True).then_inc(sem("s_dt_full"), 1)

            def conv_proj(m, w, tiles=range(4)):
                if tiles[0] == 0 and (not isinstance(m.half, int) or m.half):
                    pe.wait_ge(*reach("s_conv_done", m.value - 1))
                for t in tiles:
                    for c in range(DC):
                        mm = pe.matmul(banks[:, 3 + m.odd, t * P:(t + 1) * P], w[:, c, t * P:(t + 1) * P],
                                       xlnT[:, c, :], start=(c == 0), stop=(c == 3))
                if tiles[-1] == 3:
                    mm.then_inc(sem("s_used"), 1)

            conv_proj(Nth.of(0), weights(1))
            pe.wait_ge(*reach("s_after_r", 1))
            for m in range(4):
                for n in range(8 * m, 8 * m + 8):
                    pe.wait_ge(*reach(("s_seg_even", "s_seg_odd")[n % 2], n // 2 + 1))
                    if n >= 3:
                        pe.wait_ge(*reach("s_decay_ready", n - 2))
                    for half, last in ((seg_hi, False), (seg_lo, True)):
                        mm = pe.matmul(banks[:, SEG_BANKS[n % 3], :], after_r[:],
                                       half[:, n % 4].rearrange("p h n -> p (h n)"), start=not last, stop=last)
                    mm.then_inc(sem("s_seg_full"), 1)
                    if n % 2:
                        conv_proj(Nth.of(m + 1), weights(m + 2), (n % 8 // 2,))
            pe.wait_ge(*reach("s_conv_act", 4))
            for q in range(2):
                for g in range(4 * q, 4 * q + 4):
                    mm = pe.matmul(banks[:, 5 + q, (g % 4) * P:(g % 4 + 1) * P], s_bT[:, g, :], s_cT[:, g, :],
                                   start=True, stop=True)
                mm.then_inc(sem("s_cb_full"), 1)

            def head_block(b):
                pe.wait_ge(*reach("s_conv_act", b.value + 5))
                if isinstance(b.half, int) and b.value == 0:
                    pe.wait_ge(*reach("s_cb_ready", 2))
                else:
                    pe.wait_ge(*reach("s_hs_ready", b.value))
                for t in range(4):
                    mm = pe.transpose(banks[:, 5, t * P:(t + 1) * P], s_chan[:, b.odd, t, :], ident)
                mm.then_inc(sem("s_hs_full"), 1)

            def mix_block(b):
                pe.wait_ge(*reach("s_mixed", b.value + 1))
                pe.wait_ge(*reach("s_hs_ready", b.value + 1))
                if not isinstance(b.half, int) or b.value:
                    pe.wait_ge(*reach("s_y_read", b.value))
                for j in range(8):
                    mm = pe.matmul(banks[:, 7, 64 * j:64 * j + 64], s_mix[:, b.odd, j, :],
                                   s_hs[:, b.odd, 64 * j:64 * j + 64], start=True, stop=True)
                mm.then_inc(sem("s_y_full"), 1)

            def gate_proj(b):
                pe.wait_ge(*reach("gate_hi", b.value * 2 + 2))
                for c in range(DC):
                    pe.matmul(banks[:, 6, :], xT_hi[:, c, :], gate_hi[:, c, :], start=(c == 0), stop=False)
                    pe.matmul(banks[:, 6, :], xT_lo[:, c, :], gate_hi[:, c, :], start=False, stop=False)
                for c in range(DC):
                    if c % 2 == 0:
                        pe.wait_ge(*reach("gate_lo", b.value * 2 + (c // 2 + 1)))
                    mm = pe.matmul(banks[:, 6, :], xT_hi[:, c, :], gate_lo(b)[:, c, :], start=False, stop=(c == 3))
                mm.then_inc(sem("s_used"), 1)

            pe.wait_ge(*reach("s_cb_ready", 2))
            pe.wait_ge(*reach("s_xT_lo", 1))
            gate_proj(Nth.of(0))
            conv_proj(Nth.of(5), weights(7))
            pe.wait_ge(*reach("s_gate_ready", 1))
            gate_proj(Nth.of(1))
            head_block(Nth.of(0))
            with pe.Fori(1, N_BLOCK // 2) as j:
                for odd in range(2):
                    b = Nth(j, odd)
                    conv_proj(b + 4, weights(5 + 2 * odd, j))
                    mix_block(b - 2)
                    pe.wait_ge(*reach("s_gate_ready", b.value))
                    gate_proj(b)
                    head_block(b - 1)
            def turn_out(b):
                pe.wait_ge(*reach("s_scaled", b.value + 1))
                if not isinstance(b.half, int) or b.half:
                    pe.wait_ge(*reach("g_lo", b.value - 1))
                for t in range(4):
                    mm = pe.transpose(banks[:, 1 + b.odd, t * P:(t + 1) * P], s_tanh[:, b.odd, t, :], ident)
                mm.then_inc(sem("s_gT_full"), 1)

            def out_proj(b, first=False, last=False):
                pe.wait_ge(*reach("g_lo", b.value + 1))
                for t in range(4):
                    if t % 2 == 0:
                        pe.wait_ge(*reach("o_lo", b.value * 2 + (t // 2 + 1)))
                    if t == 3:
                        pe.wait_ge(*reach("o_lo_pool", b.value + 1))
                    mm = three_passes(pe, banks[:, 0, :], [(g_hi[:, b.odd, t, :], g_lo[:, b.odd, t, :],
                                                            o_hi[:, b.odd, t, :], o_lo[:, b.odd, t, :])],
                                      start=first and t == 0, stop=last and t == 3)
                    if t % 2:
                        mm.then_inc(sem("o_used"), 1)

            mix_block(Nth.of(14))
            turn_out(Nth.of(0))
            head_block(Nth.of(15))
            mix_block(Nth.of(15))
            turn_out(Nth.of(1))
            out_proj(Nth.of(0), first=True)
            with pe.Fori(1, N_BLOCK // 2) as j:
                for odd in range(2):
                    turn_out(Nth(j, odd))
                    out_proj(Nth(j, odd) - 1)
            out_proj(Nth.of(15), last=True)

        def conv_tile(m):
            return 64 + 4 * m.value if isinstance(m.half, int) and m.value < 4 else m.value * 4 - 16

        def gate_lo(b):
            return s_w_lo[:, (6 + 2 * b.odd) % NSLOT]

        def ssm_act(act):
            nc.scalar.activation(after_r[:], after, ACT.Copy).then_inc(sem("s_after_r"), 1)
            act.wait_ge(*reach("xlnT_ready", 5))
            nc.scalar.activation(xT_hi[:], xlnT[:], ACT.Copy).then_inc(sem("s_xT_hi"), 1)
            act.wait_ge(*reach("s_dt_full", 1))
            nc.scalar.activation(s_dt[:, 4, :], banks[:, 0, 0:P], ACT.Abs).then_inc(sem("s_dt_abs"), 1)
            act.wait_ge(*reach("s_dt_abs", 1))
            nc.scalar.activation(s_dt[:, 4, :], s_dt[:, 4, :], ACT.Exp, scale=-1.0).then_inc(sem("s_dt_exp"), 1)
            nc.scalar.activation(s_dt[:, 1, :], banks[:, 0, P:2 * P], ACT.Exp).then_inc(sem("s_a_exp"), 1)
            act.wait_ge(*reach("s_dt_u", 1))
            nc.scalar.activation(s_dt[:, 6, :], s_dt[:, 5, :], ACT.Ln).then_inc(sem("s_dt_ln"), 1)

            def conv_first(m, used):
                act.wait_ge(*reach("s_used", used))
                if not isinstance(m.half, int) or m.half:
                    act.wait_ge(*reach("s_conv_act", m.value - 1))
                for t in range(4):
                    k = conv_tile(m) + t
                    ins = nc.scalar.activation(s_conv[:, m.odd, t, :], banks[:, 3 + m.odd, t * P:(t + 1) * P],
                                               ACT.Identity, bias=s_cbias[:, part(k, 1)],
                                               scale=s_cw[:, part(k, 1), 3:4].rearrange("p a n -> p (a n)"))
                ins.then_inc(sem("s_conv_first"), 1)

            def conv_tanh(m):
                act.wait_ge(*reach("s_conv_done", m.value + 1))
                if not isinstance(m.half, int) or m.half:
                    act.wait_ge(*reach("s_conv_act", m.value - 1))
                nc.scalar.activation(s_tanh[:, m.odd], s_conv[:, m.odd], ACT.Tanh, scale=0.5
                                     ).then_inc(sem("s_conv_tanh"), 1)

            act.wait_ge(*reach("s_cw_in", 32))
            conv_first(Nth.of(0), 2)
            for m in range(4):
                for n in range(8 * m, 8 * m + 8):
                    act.wait_ge(*reach("s_seg_full", n + 1))
                    nc.scalar.activation(s_decay[:, 4 * n:4 * n + 4, :].rearrange("p h n -> p (h n)"),
                                         banks[:, SEG_BANKS[n % 3], :], ACT.Exp).then_inc(sem("s_decay_ready"), 1)
                    if n % 8 == 0 and m:
                        conv_tanh(Nth.of(m - 1))
                    if n % 8 == 1 and m:
                        conv_first(Nth.of(m), m + 2)

            def split_gate(b):
                item = 6 + 2 * b.odd
                act.wait_ge(sem(f"s_w_in{item % NSLOT}"), (b.half + (item // NSLOT + 1)) * 16)
                for h in range(2):
                    nc.scalar.activation(gate_hi[:, 2 * h:2 * h + 2, :], s_w[:, item % NSLOT, 2 * h:2 * h + 2, :],
                                         ACT.Copy).then_inc(sem("gate_hi"), 1)

            conv_tanh(Nth.of(3))
            split_gate(Nth.of(0))
            conv_first(Nth.of(4), 6)

            def hs_copy(b):
                act.wait_ge(*reach("s_hs_full", b.value + 1))
                if not isinstance(b.half, int) or b.half:
                    act.wait_ge(*reach("s_y_read", b.value - 1))
                nc.scalar.activation(s_hs[:, b.odd, :], banks[:, 5, :], ACT.Copy, scale=0.5
                                     ).then_inc(sem("s_hs_ready"), 1)

            def square(b):
                act.wait_ge(*reach("s_g_ready", b.value + 1))
                if not isinstance(b.half, int) or b.value:
                    act.wait_ge(*reach("s_squares", b.value))
                nc.scalar.activation(s_sq[:], s_g[:, part(b.value * 512, 512)], ACT.Square,
                                     accum_out=s_squares[:, part(b.value, 1)]).then_inc(sem("s_squares"), 1)

            def gate_tanh(b):
                act.wait_ge(*reach("s_used", b.value * 2 + 7))
                if not isinstance(b.half, int) or b.half:
                    act.wait_ge(*reach("s_g_ready", b.value - 1))
                nc.scalar.activation(s_gate[:, b.odd, :], banks[:, 6, :], ACT.Tanh, scale=0.5
                                     ).then_inc(sem("s_gate_tanh"), 1)

            def turn(b, squares=True, more=True):
                hs_copy(b - 2)
                gate_tanh(b - 1)
                if more:
                    split_gate(b)
                if squares:
                    square(b - 3)
                conv_tanh(b + 3)
                if more:
                    conv_first(b + 4, b.value * 2 + 6)

            gate_tanh(Nth.of(0))
            split_gate(Nth.of(1))
            conv_tanh(Nth.of(4))
            conv_first(Nth.of(5), 8)
            turn(Nth.of(2), squares=False)
            turn(Nth.of(3))
            with act.Fori(2, N_BLOCK // 2) as j:
                turn(Nth(j, 0))
                turn(Nth(j, 1))
            turn(Nth.of(16), more=False)

            def weights_hi(b, item, rounds=0):
                slot = item % NSLOT
                act.wait_ge(sem(f"s_w_in{slot}"), (rounds + item // NSLOT + 1) * 16)
                for h in range(2):
                    if not isinstance(b.half, int) or b.half:
                        act.wait_ge(*reach("o_used", b.value * 2 + (h - 3)))
                    nc.scalar.activation(o_hi[:, b.odd, 2 * h:2 * h + 2, :], s_w[:, slot, 2 * h:2 * h + 2, :],
                                         ACT.Copy).then_inc(sem("o_hi"), 1)

            def outputs_hi(b):
                act.wait_ge(*reach("s_gT_full", b.value + 1))
                for t in range(4):
                    ins = nc.scalar.activation(g_hi[:, b.odd, t, :], banks[:, 1 + b.odd, t * P:(t + 1) * P],
                                               ACT.Copy, scale=s_nw[:, part(b.value * 4 + t, 1)])
                ins.then_inc(sem("g_hi"), 1)

            act.wait_ge(*reach("s_mixed", 12))
            weights_hi(Nth.of(0), n_in)
            hs_copy(Nth.of(15))
            square(Nth.of(14))
            act.wait_ge(*reach("s_nw_in", 16))
            outputs_hi(Nth.of(0))
            for k in range(1, 4):
                weights_hi(Nth.of(k), n_in + k)
                if k == 1:
                    square(Nth.of(15))
                outputs_hi(Nth.of(k))
            with act.Fori(1, N_BLOCK // 4) as j:
                for k in range(4):
                    b = Nth(j * 2 + k // 2, k % 2)
                    weights_hi(b, n_in + k, j)
                    outputs_hi(b)
            act.wait_ge(*reach("f_w_in", 16))
            nc.scalar.activation(f_sign[:], f_w[:], ACT.Sign).then_inc(sem("f_sign_ready"), 1)

        def ssm_pool(pool):
            pool.wait_ge(*reach("s_xT_hi", 1))
            nc.gpsimd.tensor_tensor(xT_lo[:], xlnT[:], xT_hi[:].bitcast(F32), ALU.subtract
                                    ).then_inc(sem("s_xT_lo"), 1)
            pool.wait_ge(*reach("s_dA_ready", 3))
            for n in range(0, 32, 2):
                if n >= 4:
                    pool.wait_ge(*reach("s_seg_full", n - 3))
                for half, dA in ((seg_hi, dA_hi), (seg_lo, dA_lo)):
                    ins = nc.gpsimd.tensor_tensor(half[:, n % 4], per_head(upto, 4, P),
                                                  per_column(dA[:, 4 * n:4 * n + 4].bitcast(F32), 4, P), ALU.mult)
                ins.then_inc(sem("s_seg_even"), 1)

            def skip(b):
                pool.wait_ge(*reach("s_hs_ready", b.value + 1))
                if not isinstance(b.half, int) or b.half:
                    pool.wait_ge(*reach("s_g_ready", b.value - 1))
                nc.gpsimd.tensor_tensor(s_y[:, b.odd, :].rearrange("p (h n) -> p h n", h=8),
                                        s_hs[:, b.odd, :].rearrange("p (h n) -> p h n", h=8),
                                        per_column(s_dt[:, 3, part(b.value * 8, 8)], 8, 64), ALU.mult
                                        ).then_inc(sem("s_skip"), 1)

            def split_gate(b):
                slot = (6 + 2 * b.odd) % NSLOT
                for h in range(2):
                    pool.wait_ge(*reach("gate_hi", b.value * 2 + (h + 1)))
                    for c in (2 * h, 2 * h + 1):
                        ins = nc.gpsimd.tensor_tensor(gate_lo(b)[:, c, :], s_w[:, slot, c, :],
                                                      gate_hi[:, c, :].bitcast(F32), ALU.subtract)
                    ins.then_inc(sem("gate_lo"), 1)

            split_gate(Nth.of(0))
            split_gate(Nth.of(1))
            pool.wait_ge(*reach("s_cb_ready", 2))
            skip(Nth.of(0))
            split_gate(Nth.of(2))
            skip(Nth.of(1))
            split_gate(Nth.of(3))
            with pool.Fori(2, N_BLOCK // 2) as j:
                for odd in range(2):
                    skip(Nth(j, odd) - 2)
                    split_gate(Nth(j, odd))
            skip(Nth.of(14))
            return skip

        def out_pool(pool, skip):
            def out_lo(b, item):
                pool.wait_ge(*reach("o_hi", b.value * 2 + 2))
                nc.gpsimd.tensor_tensor(o_lo[:, b.odd, 3, :], s_w[:, item % NSLOT, 3, :],
                                        o_hi[:, b.odd, 3, :].bitcast(F32), ALU.subtract
                                        ).then_inc(sem("o_lo_pool"), 1)

            rsqrt_pool(pool, "s_var_ready", 1, s_var[:, 1, 0:7], s_var[:, 2, 0:7])
            pool.wait_ge(*reach("s_mixed", 16))
            out_lo(Nth.of(0), n_in)
            skip(Nth.of(15))
            out_lo(Nth.of(1), n_in + 1)
            rsqrt_pool(pool, "s_var_ready", 2, s_var[:, 1, 7:8], s_var[:, 2, 7:8])
            out_lo(Nth.of(2), n_in + 2)
            out_lo(Nth.of(3), n_in + 3)
            with pool.Fori(1, N_BLOCK // 4) as j:
                for k in range(4):
                    out_lo(Nth(j * 2 + k // 2, k % 2), n_in + k)

        def ssm_dve(dve):
            def then(ins):
                own_steps[0] += 1
                ins.then_inc(sem("dve_own"), 1)
                dve.wait_ge(*reach("dve_own", own_steps[0]))

            d = s_dt
            dve.wait_ge(*reach("s_dt_exp", 1))
            nc.vector.tensor_scalar(d[:, 5, :], d[:, 4, :], 1.0, None, ALU.add).then_inc(sem("s_dt_u"), 1)
            dve.wait_ge(*reach("s_dt_u", 1))
            then(nc.vector.tensor_scalar(d[:, 7, :], d[:, 5, :], -1.0, None, ALU.add))
            then(nc.vector.tensor_scalar(d[:, 2, :], d[:, 7, :], 0.0, None, ALU.is_equal))
            then(nc.vector.tensor_tensor(d[:, 7, :], d[:, 7, :], d[:, 2, :], ALU.add))
            then(nc.vector.reciprocal(d[:, 7, :], d[:, 7, :]))
            dve.wait_ge(*reach("s_dt_ln", 1))
            then(nc.vector.tensor_tensor(d[:, 7, :], d[:, 7, :], d[:, 6, :], ALU.mult))
            then(nc.vector.tensor_tensor(d[:, 7, :], d[:, 7, :], d[:, 2, :], ALU.add))
            then(nc.vector.tensor_tensor(d[:, 7, :], d[:, 7, :], d[:, 4, :], ALU.mult))
            then(nc.vector.scalar_tensor_tensor(d[:, 0, :], banks[:, 0, 0:P], 0.0, d[:, 7, :], ALU.max, ALU.add))
            then(nc.vector.tensor_scalar(d[:, 0, :], d[:, 0, :], 100.0, 0.0, ALU.min, ALU.max))
            dve.wait_ge(*reach("s_a_exp", 1))
            nc.vector.scalar_tensor_tensor(d[:, 2, :], d[:, 0, :], -1.0, d[:, 1, :], ALU.mult, ALU.mult
                                           ).then_inc(sem("s_dA_ready"), 1)
            dve.wait_ge(*reach("s_dA_ready", 1))
            nc.vector.tensor_copy(dA_hi[:], d[:, 2, :]).then_inc(sem("s_dA_ready"), 1)
            dve.wait_ge(*reach("s_dA_ready", 2))
            nc.vector.tensor_tensor(dA_lo[:], d[:, 2, :], dA_hi[:].bitcast(F32), ALU.subtract
                                    ).then_inc(sem("s_dA_ready"), 1)
            dve.wait_ge(*reach("s_dA_ready", 3))
            then(nc.vector.tensor_copy(d[:, 3, :], banks[:, 0, 2 * P:3 * P]))

            def taps(m, which=range(1, 4)):
                for k in which:
                    if k == 1:
                        dve.wait_ge(*reach("s_conv_first", m.value + 1))
                    else:
                        dve.wait_ge(*reach("s_tap", m.value * 2 + (k - 1)))
                    for t in range(4):
                        ins = nc.vector.scalar_tensor_tensor(
                            s_conv[:, m.odd, t, k:P], banks[:, 3 + m.odd, t * P:(t + 1) * P - k],
                            s_cw[:, part(conv_tile(m) + t, 1), 3 - k:4 - k].rearrange("p a n -> p (a n)"),
                            s_conv[:, m.odd, t, k:P], ALU.mult, ALU.add)
                    ins.then_inc(sem("s_tap" if k < 3 else "s_conv_done"), 1)

            def silu(m, dst=None):
                dve.wait_ge(*reach("s_conv_tanh", m.value + 1))
                if dst is None:
                    dst = s_chan[:, m.odd]
                    if not isinstance(m.half, int) or m.value >= 6:
                        dve.wait_ge(*reach("s_hs_full", m.value - 5))
                nc.vector.scalar_tensor_tensor(dst.rearrange("p t n -> p (t n)"),
                                               s_tanh[:, m.odd].rearrange("p t n -> p (t n)"), 1.0,
                                               s_conv[:, m.odd].rearrange("p t n -> p (t n)"), ALU.add,
                                               ALU.mult).then_inc(sem("s_conv_act"), 1)

            bc = [s_bT[:, 0:4, :], s_bT[:, 4:8, :], s_cT[:, 0:4, :], s_cT[:, 4:8, :]]
            for m in range(4):
                for n in range(8 * m + 1, 8 * m + 8, 2):
                    if n >= 4:
                        dve.wait_ge(*reach("s_seg_full", n - 3))
                    for half, dA in ((seg_hi, dA_hi), (seg_lo, dA_lo)):
                        ins = nc.vector.tensor_tensor(half[:, n % 4], per_head(upto, 4, P),
                                                      per_column(dA[:, 4 * n:4 * n + 4].bitcast(F32), 4, P), ALU.mult)
                    ins.then_inc(sem("s_seg_odd"), 1)
                    if n % 8 == 3 and m:
                        silu(Nth.of(m - 1), bc[m - 1])
                    if n % 8 > 1:
                        taps(Nth.of(m), (n % 8 // 2,))
            silu(Nth.of(3), bc[3])
            for q in range(2):
                dve.wait_ge(*reach("s_cb_full", q + 1))
                nc.vector.scalar_tensor_tensor(
                    s_cb[:, 4 * q:4 * q + 4, :], banks[:, 5 + q, :].rearrange("p (g n) -> p g n", g=4), 0.25,
                    per_head(upto, 4, P), ALU.mult, ALU.mult).then_inc(sem("s_cb_ready"), 1)
            dve.wait_ge(*reach("s_cb_ready", 2))
            dve.wait_ge(*reach("s_decay_ready", 32))

            def mix(b):
                if not isinstance(b.half, int) or b.half:
                    dve.wait_ge(*reach("s_y_full", b.value - 1))
                for k in range(8):
                    h = b.value * 8 + k
                    ins = nc.vector.scalar_tensor_tensor(
                        s_mix[:, b.odd, k, :], s_decay[:, part(h, 1), :].rearrange("p a n -> p (a n)"),
                        d[:, 0, part(h, 1)], s_cb[:, part(b.half, 1), :].rearrange("p a n -> p (a n)"),
                        ALU.mult, ALU.mult)
                ins.then_inc(sem("s_mixed"), 1)

            def finish(b):
                dve.wait_ge(*reach("s_skip", b.value + 1))
                dve.wait_ge(*reach("s_y_full", b.value + 1))
                nc.vector.tensor_tensor(s_y[:, b.odd, :], s_y[:, b.odd, :], banks[:, 7, :], ALU.add
                                        ).then_inc(sem("s_y_read"), 1)
                dve.wait_ge(*reach("s_y_read", b.value + 1))
                nc.vector.scalar_tensor_tensor(s_g[:, part(b.value * 512, 512)], s_y[:, b.odd, :], 0.5,
                                               s_gate[:, b.odd, :], ALU.mult, ALU.mult).then_inc(sem("s_g_ready"), 1)

            def gate(b):
                dve.wait_ge(*reach("s_gate_tanh", b.value + 1))
                nc.vector.scalar_tensor_tensor(s_gate[:, b.odd, :], s_gate[:, b.odd, :], 1.0, banks[:, 6, :],
                                               ALU.add, ALU.mult).then_inc(sem("s_gate_ready"), 1)

            def turn(b, finished=True):
                taps(b + 4)
                gate(b)
                mix(b)
                silu(b + 4)
                if finished:
                    finish(b - 1)

            turn(Nth.of(0), finished=False)
            turn(Nth.of(1))
            with dve.Fori(1, N_BLOCK // 2 - 1) as j:
                turn(Nth(j, 0))
                turn(Nth(j, 1))
            turn(Nth.of(14))

            def mean_squares(g0, g1):
                dve.wait_ge(*reach("s_squares", 2 * g1))
                v = s_var[:, 1, g0:g1]
                then(nc.vector.tensor_tensor(v, s_squares[:, 2 * g0:2 * g1:2], s_squares[:, 2 * g0 + 1:2 * g1:2],
                                             ALU.add))
                nc.vector.tensor_scalar(v, v, 1.0 / 1024, EPS, ALU.mult, ALU.add).then_inc(sem("s_var_ready"), 1)

            def roots_of(g0, g1):
                rsqrt_dve(dve, s_var[:, 1, g0:g1], s_var[:, 2, g0:g1], s_var[:, 3, g0:g1])

            def scale(b):
                if not isinstance(b.half, int) or b.half:
                    dve.wait_ge(*reach("s_gT_full", b.value - 1))
                nc.vector.tensor_scalar(s_tanh[:, b.odd].rearrange("p t n -> p (t n)"),
                                        s_g[:, part(b.value * 512, 512)], s_var[:, 2, part(b.half, 1)], None,
                                        ALU.mult).then_inc(sem("s_scaled"), 1)

            def weights_lo(b, item):
                for h, (t0, t1) in enumerate(((0, 2), (2, 3))):
                    dve.wait_ge(*reach("o_hi", b.value * 2 + (h + 1)))
                    nc.vector.tensor_tensor(o_lo[:, b.odd, t0:t1, :], s_w[:, item % NSLOT, t0:t1, :],
                                            o_hi[:, b.odd, t0:t1, :].bitcast(F32), ALU.subtract
                                            ).then_inc(sem("o_lo"), 1)

            def outputs_lo(b):
                dve.wait_ge(*reach("g_hi", b.value + 1))
                for t in range(4):
                    ins = nc.vector.scalar_tensor_tensor(
                        g_lo[:, b.odd, t, :], banks[:, 1 + b.odd, t * P:(t + 1) * P],
                        s_nw[:, part(b.value * 4 + t, 1)], g_hi[:, b.odd, t, :].bitcast(F32), ALU.mult, ALU.subtract)
                ins.then_inc(sem("g_lo"), 1)

            taps(Nth.of(19))
            gate(Nth.of(15))
            mean_squares(0, 7)
            mix(Nth.of(15))
            roots_of(0, 7)
            scale(Nth.of(0))
            silu(Nth.of(19))
            finish(Nth.of(14))
            weights_lo(Nth.of(0), n_in)
            scale(Nth.of(1))
            finish(Nth.of(15))
            outputs_lo(Nth.of(0))
            scale(Nth.of(2))
            for k in range(1, 4):
                weights_lo(Nth.of(k), n_in + k)
                if k == 1:
                    mean_squares(7, 8)
                outputs_lo(Nth.of(k))
                if k == 1:
                    roots_of(7, 8)
                scale(Nth.of(k + 2))
            with dve.Fori(1, N_BLOCK // 4 - 1) as j:
                for k in range(4):
                    b = Nth(j * 2 + k // 2, k % 2)
                    weights_lo(b, n_in + k)
                    outputs_lo(b)
                    scale(b + 2)
            for b in range(12, 16):
                weights_lo(Nth.of(b), n_in + b)
                outputs_lo(Nth.of(b))
                if b < 14:
                    scale(Nth.of(b + 2))
            dve.wait_ge(*reach("o_used", 2 * N_BLOCK))
            nc.vector.tensor_tensor(x[:], x[:], banks[:, 0, :], ALU.add).then_inc(sem("s_x_sum"), 1)
            dve.wait_ge(*reach("s_x_sum", 1))

        def ffn_sync(sp):
            sp.dma_start(f_gw[:], a["f_gw"].rearrange("(c p) n -> p c n", p=P)).then_inc(sem("f_gw_in"), 16)
            sp.dma_start(f_w[:], a["f_w"].rearrange("(c p) n -> p c n", p=P)).then_inc(sem("f_w_in"), 16)
            sp.dma_start(f_scale[:, 0, :], a["f_in"]).then_inc(sem("f_scale_in"), 16)
            sp.dma_start(f_scale[:, 1, :], a["f_out"]).then_inc(sem("f_scale_in"), 16)
            sp.dma_start(f_bias[:], a["f_b"].broadcast_to([P, D])).then_inc(sem("f_bias_in"), 16)

        def ffn_pe(pe):
            pe.wait_ge(*reach("f_gw_in", 16))
            for c in range(DC):
                mm = pe.matmul(banks[:, 0, 0:8], xlnT[:, c, :], f_gw[:, c, :], start=(c == 0), stop=(c == 3))
            mm.then_inc(sem("f_logits"), 1)
            pe.wait_ge(*reach("f_routing", 1))
            pe.transpose(banks[0:8, 1, 0:P], f_r[:, 8:16], ident).then_inc(sem("f_rT_full"), 1)
            pe.wait_ge(*reach("f_rT_ready", 1))
            pe.wait_ge(*reach("f_scale_in", 32))
            for k in range(2):
                pe.matmul(banks[:, 2 + k, :], f_rT[:], f_scale[:, k, :], start=True, stop=True
                          ).then_inc(sem("f_scales"), 1)
            pe.wait_ge(*reach("f_scaled", 1))
            for c in range(DC):
                mm = pe.transpose(banks[:, 4, c * P:(c + 1) * P], f_xs[:, c * P:(c + 1) * P], ident)
            mm.then_inc(sem("f_xT_full"), 1)
            pe.wait_ge(*reach("f_xT_ready", 1))
            for c in range(DC):
                mm = pe.matmul(banks[:, 5, :], f_xT[:, c, :], f_sign[:, c, :], start=(c == 0), stop=(c == 3))
            mm.then_inc(sem("f_out_full"), 1)

        def ffn_act(act):
            act.wait_ge(*reach("f_neg_max", 1))
            nc.scalar.activation(f_r[:, 0:8], banks[:, 0, 0:8], ACT.Exp, bias=f_r[:, 16:17],
                                 accum_out=f_r[:, 17:18]).then_inc(sem("f_exp"), 1)
            act.wait_ge(*reach("f_rT_full", 1))
            nc.scalar.activation(f_rT[:], banks[0:8, 1, 0:P], ACT.Copy).then_inc(sem("f_rT_ready"), 1)
            act.wait_ge(*reach("f_scales", 2))
            nc.scalar.activation(f_os[:], banks[:, 3, :], ACT.Copy).then_inc(sem("f_os_ready"), 1)
            act.wait_ge(*reach("f_xT_full", 1))
            act.wait_ge(*reach("f_sign_ready", 1))
            nc.scalar.activation(f_xT[:].rearrange("p c n -> p (c n)"), banks[:, 4, :],
                                 ACT.Copy).then_inc(sem("f_xT_ready"), 1)

        def ffn_dve(dve):
            dve.wait_ge(*reach("f_logits", 1))
            nc.vector.tensor_reduce(f_r[:, 16:17], banks[:, 0, 0:8], AX.X, ALU.max, negate=True
                                    ).then_inc(sem("f_neg_max"), 1)
            dve.wait_ge(*reach("f_exp", 1))
            nc.vector.reciprocal(f_r[:, 18:19], f_r[:, 17:18]).then_inc(sem("f_inv"), 1)
            dve.wait_ge(*reach("f_inv", 1))
            nc.vector.tensor_scalar(f_r[:, 8:16], f_r[:, 0:8], f_r[:, 18:19], None, ALU.mult
                                    ).then_inc(sem("f_routing"), 1)
            dve.wait_ge(*reach("f_scales", 1))
            nc.vector.tensor_tensor(f_xs[:], xln[:], banks[:, 2, :], ALU.mult).then_inc(sem("f_scaled"), 1)
            dve.wait_ge(*reach("f_bias_in", 16))
            nc.vector.tensor_tensor(x[:], x[:], f_bias[:], ALU.add).then_inc(sem("f_biased"), 1)
            dve.wait_ge(*reach("f_out_full", 1))
            dve.wait_ge(*reach("f_os_ready", 1))
            dve.wait_ge(*reach("f_biased", 1))
            nc.vector.tensor_tensor(f_os[:], f_os[:], banks[:, 5, :], ALU.mult).then_inc(sem("f_y"), 1)
            dve.wait_ge(*reach("f_y", 1))
            nc.vector.tensor_tensor(x[:], x[:], f_os[:], ALU.add).then_inc(sem("f_x_sum"), 1)

        block = ctx.enter_context(nc.Block())

        @block.sync
        def _(sp):
            sp.dma_start(x[:], a["x"]).then_inc(sem("x_in"), 16)
            sp.dma_start(const[:], a["const"]).then_inc(sem("const_in"), 16)
            cross[0].sync(sp)
            mla_sync(sp)
            moe_sync(sp)
            sp.dma_start(bias_q[:], a["bq1"]).then_inc(sem("biases_in"), 16)
            sp.dma_start(bias_k[:], a["bkv1"][:, 0:8]).then_inc(sem("biases_in"), 16)
            sp.dma_start(bias_v[:], a["bkv1"][:, 8:16]).then_inc(sem("biases_in"), 16)
            cross[1].sync(sp)
            ssm_sync(sp)
            sp.wait_ge(*reach("f_x_sum", 1))
            sp.dma_start(out, x[:]).then_inc(sem("out_written"), 16)
            sp.wait_ge(*reach("out_written", 16))

        @block.gpsimd
        def _(pool):
            nc.gpsimd.memset(minus_half[:], -0.5).then_inc(sem("half_set"), 1)
            pool.wait_ge(*reach("half_set", 1))
            ln_pool(pool, 0)
            ln_pool(pool, 1)
            rsqrt_pool(pool, "m_var", 1, ln[:, 14:16], ln[:, 16:18])
            mla_pool(pool)
            for n in range(2, 5):
                ln_pool(pool, n)
            out_pool(pool, ssm_pool(pool))
            ln_pool(pool, 5)

        @block.tensor
        def _(pe):
            pe.wait_ge(*reach("const_in", 16))
            ln_pe(pe, 0)
            cross[0].pe(pe)
            ln_pe(pe, 1)
            mla_pe(pe)
            ln_pe(pe, 2)
            moe_pe(pe)
            ln_pe(pe, 3)
            cross[1].pe(pe)
            ln_pe(pe, 4)
            ssm_pe(pe)
            ln_pe(pe, 5)
            ffn_pe(pe)

        @block.scalar
        def _(act):
            ln_act(act, 0)
            ctx_act(act)
            cross[0].act(act)
            ln_act(act, 1)
            mla_act(act)
            moe_act(act)
            ln_act(act, 3)
            act.wait_ge(*reach("biases_in", 48))
            cross[1].act(act)
            ln_act(act, 4)
            ssm_act(act)
            ln_act(act, 5)
            ffn_act(act)

        @block.vector
        def _(dve):
            dve.wait_ge(*reach("x_in", 16))
            dve.wait_ge(*reach("const_in", 16))
            ln_dve(dve, 0)
            ctx_dve(dve)
            cross[0].dve(dve)
            ln_dve(dve, 1)
            mla_dve(dve)
            ln_dve(dve, 2)
            moe_dve(dve)
            ln_dve(dve, 3)
            dve.wait_ge(*reach("biases_in", 48))
            nc.vector.tensor_scalar(bias_q[:], bias_q[:], ATT_SCALE, None, ALU.mult).then_inc(sem("bq_scaled"), 1)
            dve.wait_ge(*reach("bq_scaled", 1))
            cross[1].dve(dve)
            ln_dve(dve, 4)
            ssm_dve(dve)
            ln_dve(dve, 5)
            ffn_dve(dve)


_OUT = (1, 128, 512)


def kernel(**inputs):
    import numpy as np
    import concourse.bacc as bacc
    from concourse.bass_utils import run_bass_kernel_spmd

    t, arrays = _layout(np, inputs)
    nc = bacc.Bacc("TRN2", target_bir_lowering=False, num_devices=1)
    aps = {n: nc.dram_tensor(n, v.shape, mybir.dt.from_np(v.dtype), kind="ExternalInput").ap()
           for n, v in arrays.items()}
    out = nc.dram_tensor("y", (128, 512), mybir.dt.float32, kind="ExternalOutput").ap()
    build(nc, aps, out)
    r = run_bass_kernel_spmd(nc, [arrays], core_ids=[0])
    return r.results[0]["y"].reshape(_OUT)


def _layout(np, i):
    c = np.ascontiguousarray
    i = {k: np.asarray(v) for k, v in i.items()}
    ar = {
        "x": c(i["x"][0]),
        "ctxT": c(i["ctx_4096"][0].T),
        "const": _constants(np),
        "Wq0": i["L0_xattn_Wq"], "Wk0": i["L0_xattn_Wk"], "Wv0": i["L0_xattn_Wv"], "Wo0": i["L0_xattn_Wo"],
        "Wq1": i["L1_xattn_Wq"], "Wk1": c(i["L1_xattn_Wkv"][:, :1024]), "Wv1": c(i["L1_xattn_Wkv"][:, 1024:]),
        "Wo1": i["L1_xattn_Wo"], "bq1": c(i["L1_xattn_bq"].reshape(32, 128).T),
        "bkv1": c(i["L1_xattn_bkv"].reshape(16, 128).T), "bo1": c(i["L1_xattn_bo"].reshape(1, 512)),
        "m_wa": c(np.concatenate([i["L0_attn_wq_a"], i["L0_attn_wkv_a"]]).T),
        "m_lnq": c(i["L0_attn_q_a_ln_w"].reshape(128, 1)), "m_lnkv": c(i["L0_attn_kv_a_ln_w"].reshape(32, 1)),
        "m_wqb": c(i["L0_attn_wq_b"].T), "m_wkvb": c(i["L0_attn_wkv_b"].T), "m_wo": c(i["L0_attn_wo"].T),
        "e_gw": i["L0_ffn_gate_w"], "e_gb": c(i["L0_ffn_gate_b"].reshape(1, 3)),
        "e_w1": i["L0_ffn_w1"], "e_b1": c(i["L0_ffn_b1"].reshape(12, 128).T),
        "e_w2": i["L0_ffn_w2"], "e_b2": c(i["L0_ffn_b2"].reshape(1, 1536)),
        "s_in": c(i["L1_attn_in_proj_w"].T),
        "s_cw": c(i["L1_attn_conv_w"].reshape(80, 128, 4).transpose(1, 0, 2)),
        "s_cb": c(i["L1_attn_conv_b"].reshape(80, 128).T),
        "s_dtb": c(i["L1_attn_dt_bias"].reshape(1, 128)), "s_alog": c(i["L1_attn_A_log"].reshape(1, 128)),
        "s_D": c(i["L1_attn_D"].reshape(1, 128)), "s_nw": c(i["L1_attn_norm_w"].reshape(64, 128).T),
        "s_out": c(i["L1_attn_out_proj_w"].T),
        "f_w": c(i["L1_ffn_weight"].T), "f_b": c(i["L1_ffn_bias"].reshape(1, 512)),
        "f_gw": c(i["L1_ffn_gate_w"].T), "f_in": i["L1_ffn_in_channel_scale"],
        "f_out": i["L1_ffn_out_channel_scale"],
    }
    return i, {k: c(v) for k, v in ar.items()}


def _constants(np):
    import math
    n = np.arange(128)
    k, m = n[:, None], n[None, :]
    dim, base, factor, orig = 64, 10000.0, 128.0, 1024
    turn = lambda r: dim * math.log(orig / (r * 2 * math.pi)) / (2 * math.log(base))
    low, high = max(math.floor(turn(32.0)), 0), min(math.ceil(turn(1.0)), dim - 1)
    hi = high + 0.001 if low == high else float(high)
    keep = 1.0 - np.clip((np.arange(dim // 2, dtype=np.float32) - low) / (hi - low), 0.0, 1.0)
    extra = 1.0 / base ** (np.arange(0, dim, 2, dtype=np.float32) / dim)
    freq = extra / factor * (1.0 - keep) + extra * keep
    angle = np.outer(np.arange(128, dtype=np.float32), freq)
    vision = int(128 * 0.3)
    return np.concatenate([
        (k == m), np.ones((128, 128)), (k <= m), (k > m), np.where(m <= k, 0.0, MASKED),
        np.cos(angle), np.sin(angle),
        (k >= vision) / ((128 - vision) * 512.0), (k < vision) / (vision * 512.0),
    ], axis=1).astype(np.float32)
```
